# Optimizing a Trainium2 kernel written in Bass

```python
import numpy as np
import jax
import jax.numpy as jnp

def _softmax(x, axis=-1):
    return jax.nn.softmax(x, axis=axis)

def _gelu(x):
    return jax.nn.gelu(x, approximate=True)

def _silu(x):
    return jax.nn.silu(x)

def _sigmoid(x):
    return jax.nn.sigmoid(x)

def _layernorm(x, axis=-1, eps=1e-05):
    m = jnp.mean(x, axis=axis, keepdims=True)
    v = jnp.var(x, axis=axis, keepdims=True)
    return (x - m) / jnp.sqrt(v + eps)

def _scatter_add(tgt, idx, src, axis=0):
    return tgt.at[idx].add(src)

def _segment_sum(src, seg, n):
    return jax.ops.segment_sum(src, seg, n)
kernel_name = 'mk_recurrent_d2_jaxref_r4_da5a5f'

def setup_inputs(seed: int=0):
    np.random.seed(seed)
    _w = jnp.asarray

    def _L0_attn_setup():
        import jax, jax.numpy as jnp
        import numpy as np
        HEADS = 16
        DIM_HEAD = 64
        B, T, C = (4, 512, 256)

        def apply_rope(x):
            d = x.shape[-1]
            seq_len = x.shape[1]
            inv_freq = 1.0 / 10000.0 ** (jnp.arange(0, d, 2, dtype=jnp.float32) / d)
            pos = jnp.arange(seq_len, dtype=jnp.float32)
            ang = pos[:, None] * inv_freq[None, :]
            sin = jnp.sin(ang)[None]
            cos = jnp.cos(ang)[None]
            x1, x2 = (x[..., 0::2], x[..., 1::2])
            rot = jnp.stack([x1 * cos - x2 * sin, x1 * sin + x2 * cos], axis=-1)
            return rot.reshape(x.shape)
        key = jax.random.key(seed)
        ks = jax.random.split(key, 6)
        inner = HEADS * DIM_HEAD
        w = 0.02
        return {'x': jax.random.normal(ks[0], (B, T, C), dtype=jnp.float32), 'Wq': jax.random.normal(ks[1], (C, inner), dtype=jnp.float32) * w, 'Wk': jax.random.normal(ks[2], (C, inner), dtype=jnp.float32) * w, 'Wv': jax.random.normal(ks[3], (C, inner), dtype=jnp.float32) * w, 'Wo': jax.random.normal(ks[4], (inner, C), dtype=jnp.float32) * w, 'bo': jnp.zeros((C,), dtype=jnp.float32)}
    _L0_attn_in = _L0_attn_setup()

    def _L0_ffn_setup():
        import jax, jax.numpy as jnp
        import numpy as np
        DIM = 256
        HIDDEN = 768
        SCALE = 1.0 / 127.0

        def _dequant(w_int, dtype):
            return w_int.astype(dtype) * jnp.asarray(SCALE, dtype)
        key = jax.random.key(seed)
        k_x, k_g, k_u, k_d = jax.random.split(key, 4)
        x = jax.random.normal(k_x, (4, 512, DIM), dtype=jnp.float32)
        w_gate = jax.random.randint(k_g, (HIDDEN, DIM), -127, 128, dtype=jnp.int32)
        w_up = jax.random.randint(k_u, (HIDDEN, DIM), -127, 128, dtype=jnp.int32)
        w_down = jax.random.randint(k_d, (DIM, HIDDEN), -127, 128, dtype=jnp.int32)
        return {'x': x, 'w_gate': w_gate, 'w_up': w_up, 'w_down': w_down}
    _L0_ffn_in = _L0_ffn_setup()

    def _L1_attn_setup():
        import jax, jax.numpy as jnp
        import numpy as np
        EMBED_DIM = 256
        NUM_HEADS = 16
        HEAD_DIM = EMBED_DIM // NUM_HEADS
        key = jax.random.key(seed)
        ks = jax.random.split(key, 9)
        s = 1.0 / np.sqrt(EMBED_DIM)
        mk = lambda k: jax.random.uniform(k, (EMBED_DIM, EMBED_DIM), jnp.float32, -s, s)
        bk = lambda k: jax.random.uniform(k, (EMBED_DIM,), jnp.float32, -s, s)
        return {'input_tensor': jax.random.normal(ks[0], (4, 512, EMBED_DIM), jnp.float32), 'wq': mk(ks[1]), 'bq': bk(ks[2]), 'wk': mk(ks[3]), 'bk_': bk(ks[4]), 'wv': mk(ks[5]), 'bv': bk(ks[6]), 'wo': mk(ks[7]), 'bo': bk(ks[8])}
    _L1_attn_in = _L1_attn_setup()

    def _L1_ffn_setup():
        import jax, jax.numpy as jnp
        import numpy as np
        D_MODEL = 256
        D_FF = 704
        N_EXPERTS = 8
        key = jax.random.key(seed)
        k_in, k1, k2, k3 = jax.random.split(key, 4)
        scale = 0.02
        inputs = jax.random.normal(k_in, (4, N_EXPERTS * 512, D_MODEL), dtype=jnp.float32)
        w1 = jax.random.normal(k1, (N_EXPERTS, D_MODEL, D_FF), dtype=jnp.float32) * scale
        w3 = jax.random.normal(k3, (N_EXPERTS, D_MODEL, D_FF), dtype=jnp.float32) * scale
        w2 = jax.random.normal(k2, (N_EXPERTS, D_FF, D_MODEL), dtype=jnp.float32) * scale
        return {'inputs': inputs, 'w1': w1, 'w3': w3, 'w2': w2}
    _L1_ffn_in = _L1_ffn_setup()
    _d = {'L0_attn_x': _L0_attn_in['x'], 'L0_attn_Wq': _L0_attn_in['Wq'], 'L0_attn_Wk': _L0_attn_in['Wk'], 'L0_attn_Wv': _L0_attn_in['Wv'], 'L0_attn_Wo': _L0_attn_in['Wo'], 'L0_attn_bo': _L0_attn_in['bo'], 'L0_ffn_w_gate': _L0_ffn_in['w_gate'], 'L0_ffn_w_up': _L0_ffn_in['w_up'], 'L0_ffn_w_down': _L0_ffn_in['w_down'], 'L1_attn_wq': _L1_attn_in['wq'], 'L1_attn_bq': _L1_attn_in['bq'], 'L1_attn_wk': _L1_attn_in['wk'], 'L1_attn_bk_': _L1_attn_in['bk_'], 'L1_attn_wv': _L1_attn_in['wv'], 'L1_attn_bv': _L1_attn_in['bv'], 'L1_attn_wo': _L1_attn_in['wo'], 'L1_attn_bo': _L1_attn_in['bo'], 'L1_ffn_w1': _L1_ffn_in['w1'], 'L1_ffn_w3': _L1_ffn_in['w3'], 'L1_ffn_w2': _L1_ffn_in['w2']}
    _x0 = _d['L0_attn_x']
    _d['L0_attn_x'] = jax.random.normal(jax.random.fold_in(jax.random.key(seed), 1), (8, 512, 256), dtype=_x0.dtype)
    del _x0
    return _d

def reference(L0_attn_x, L0_attn_Wq, L0_attn_Wk, L0_attn_Wv, L0_attn_Wo, L0_attn_bo, L0_ffn_w_gate, L0_ffn_w_up, L0_ffn_w_down, L1_attn_wq, L1_attn_bq, L1_attn_wk, L1_attn_bk_, L1_attn_wv, L1_attn_bv, L1_attn_wo, L1_attn_bo, L1_ffn_w1, L1_ffn_w3, L1_ffn_w2):

    def _L0_attn_ref(x, Wq, Wk, Wv, Wo, bo):
        import jax, jax.numpy as jnp
        import numpy as np
        HEADS = 16
        DIM_HEAD = 64
        B, T, C = (4, 512, 256)

        def apply_rope(x):
            d = x.shape[-1]
            seq_len = x.shape[1]
            inv_freq = 1.0 / 10000.0 ** (jnp.arange(0, d, 2, dtype=jnp.float32) / d)
            pos = jnp.arange(seq_len, dtype=jnp.float32)
            ang = pos[:, None] * inv_freq[None, :]
            sin = jnp.sin(ang)[None]
            cos = jnp.cos(ang)[None]
            x1, x2 = (x[..., 0::2], x[..., 1::2])
            rot = jnp.stack([x1 * cos - x2 * sin, x1 * sin + x2 * cos], axis=-1)
            return rot.reshape(x.shape)
        b, t, c = x.shape
        h, d = (HEADS, DIM_HEAD)
        scale = d ** (-0.5)

        def split_heads(z):
            return z.reshape(b, t, h, d).transpose(0, 2, 1, 3).reshape(b * h, t, d)
        q = split_heads(x @ Wq)
        k = split_heads(x @ Wk)
        v = split_heads(x @ Wv)
        q = apply_rope(q)
        k = apply_rope(k)
        sim = jnp.einsum('bid,bjd->bij', q, k) * scale
        causal = jnp.tril(jnp.ones((t, t), dtype=bool))
        sim = jnp.where(causal[None], sim, -jnp.inf)
        attn = jax.nn.softmax(sim, axis=-1)
        out = jnp.einsum('bij,bjd->bid', attn, v)
        out = out.reshape(b, h, t, d).transpose(0, 2, 1, 3).reshape(b, t, h * d)
        return out @ Wo + bo

    def _L0_ffn_ref(x, w_gate, w_up, w_down):
        import jax, jax.numpy as jnp
        import numpy as np
        DIM = 256
        HIDDEN = 768
        SCALE = 1.0 / 127.0

        def _dequant(w_int, dtype):
            return w_int.astype(dtype) * jnp.asarray(SCALE, dtype)
        wg = _dequant(w_gate, x.dtype)
        wu = _dequant(w_up, x.dtype)
        wd = _dequant(w_down, x.dtype)
        gate = jnp.einsum('bsd,hd->bsh', x, wg)
        up = jnp.einsum('bsd,hd->bsh', x, wu)
        h = jax.nn.silu(gate) * up
        return jnp.einsum('bsh,dh->bsd', h, wd)

    def _L1_attn_ref(input_tensor, wq, bq, wk, bk_, wv, bv, wo, bo):
        import jax, jax.numpy as jnp
        import numpy as np
        EMBED_DIM = 256
        NUM_HEADS = 16
        HEAD_DIM = EMBED_DIM // NUM_HEADS
        B, S, E = input_tensor.shape
        H, D = (NUM_HEADS, HEAD_DIM)
        q = input_tensor @ wq.T + bq
        k = input_tensor @ wk.T + bk_
        v = input_tensor @ wv.T + bv
        q = q.reshape(B, S, H, D).transpose(0, 2, 1, 3)
        k = k.reshape(B, S, H, D).transpose(0, 2, 1, 3)
        v = v.reshape(B, S, H, D).transpose(0, 2, 1, 3)
        scores = jnp.einsum('bhsd,bhtd->bhst', q, k) / jnp.sqrt(jnp.float32(D))
        attn = jax.nn.softmax(scores, axis=-1)
        out = jnp.einsum('bhst,bhtd->bhsd', attn, v)
        out = out.transpose(0, 2, 1, 3).reshape(B, S, E)
        return out @ wo.T + bo

    def _L1_ffn_ref(inputs, w1, w3, w2):
        import jax, jax.numpy as jnp
        import numpy as np
        D_MODEL = 256
        D_FF = 704
        N_EXPERTS = 8
        B, T, D = inputs.shape
        E = w1.shape[0]
        C = T // E
        x = inputs.reshape(B, E, C, D)
        gate = jnp.einsum('becd,edf->becf', x, w1)
        up = jnp.einsum('becd,edf->becf', x, w3)
        h = jax.nn.silu(gate) * up
        out = jnp.einsum('becf,efd->becd', h, w2)
        return out.reshape(B, T, D)
    x = L0_attn_x
    xn = _layernorm(x, axis=-1)
    s = _L0_attn_ref(xn, L0_attn_Wq, L0_attn_Wk, L0_attn_Wv, L0_attn_Wo, L0_attn_bo)
    g = _silu(_L0_ffn_ref(xn, L0_ffn_w_gate, L0_ffn_w_up, L0_ffn_w_down))
    x = x + s * g
    xn = _layernorm(x, axis=-1)
    s = _L1_attn_ref(xn, L1_attn_wq, L1_attn_bq, L1_attn_wk, L1_attn_bk_, L1_attn_wv, L1_attn_bv, L1_attn_wo, L1_attn_bo)
    g = _silu(_L1_ffn_ref(xn, L1_ffn_w1, L1_ffn_w3, L1_ffn_w2))
    x = x + s * g
    return x

_drawn_inputs = setup_inputs


def setup_inputs(seed=0):
    import zlib

    import numpy as np

    out = dict(_drawn_inputs(seed))
    spreads = {'L0_attn_bo': (0.0, 0.1)}
    factors = {'L1_attn_wq': 8.0,
     'L1_attn_bq': 8.0,
     'L1_attn_wk': 8.0,
     'L1_attn_wv': 8.0,
     'L1_attn_bv': 8.0,
     'L1_attn_wo': 8.0,
     'L1_attn_bo': 32.319,
     'L1_ffn_w1': 8.0,
     'L1_ffn_w3': 8.0,
     'L1_ffn_w2': 8.0,
     'L1_attn_bk_': 8.0}
    for name, (base, spread) in spreads.items():
        noise = np.random.default_rng([zlib.crc32(name.encode()), seed]).standard_normal(out[name].shape)
        drawn = base * np.exp(spread * noise) if base else spread * noise
        out[name] = jnp.asarray(drawn.astype(out[name].dtype))
    for name, factor in factors.items():
        out[name] = (out[name] * factor).astype(out[name].dtype)
    return out
```

```python
from contextlib import ExitStack

import numpy as np

import concourse.bass as bass
from concourse import mybir
from concourse.alu_op_type import AluOpType as ALU

ACT = mybir.ActivationFunctionType
AXX = mybir.AxisListType.X
F32 = mybir.dt.float32
F32R = mybir.dt.float32r
BF16 = mybir.dt.bfloat16
I32 = mybir.dt.int32

P = 128
B, T, C = 8, 512, 256
NT = T // P
NC = C // P
EPS = 1e-5

H0, D0 = 16, 64
NP0 = H0 // 2
PC0 = 6 * D0
F0 = 768
NF0 = F0 // P
DEQ = 1.0 / 127.0

H1, D1 = 16, 16
NG1 = 4
E1, F1 = 8, 704
NF1 = (F1 + P - 1) // P
FP1 = NF1 * P
FR1 = F1 - (NF1 - 1) * P
CE = T // E1

SOFF = [0, 128, 384, 768]
PTOFF = [0, 512, 1024, 896]
NEG = -1.0e30


def rope_tables():
    inv = (np.float32(1.0) / np.float32(10000.0) ** (np.arange(0, D0, 2, dtype=np.float32) / np.float32(D0))).astype(np.float32)
    ang = (np.arange(T, dtype=np.float32)[:, None] * inv[None, :]).astype(np.float32).astype(np.float64)
    t = np.stack([np.cos(ang), np.sin(ang), -np.sin(ang)], 1).astype(np.float32)
    return np.ascontiguousarray(t.reshape(NT, P, 3, D0 // 2).transpose(1, 0, 2, 3))


class Names:
    pass


class Mem:

    def __init__(self, nc, ctx):
        self.nc, self.ctx = nc, ctx

    def sb(self, name, shape, dt=F32):
        return self.ctx.enter_context(self.nc.sbuf_tensor(name, shape, dt))

    def ps(self, name, shape, dt=F32):
        return self.ctx.enter_context(self.nc.psum_tensor(name, shape, dt))

    def sem(self, name):
        return self.ctx.enter_context(self.nc.semaphore(name))


def setup_constants(nc, m, c):
    c.ident = m.sb("ident", [P, P])
    c.identb = m.sb("identb", [P, P], BF16)
    c.maskb = m.sb("maskb", [P, P], BF16)
    set_done = m.sem("set_done")
    with nc.Block() as block:
        @block.gpsimd
        def _(pool):
            pool.memset(c.ident[:], 0.0).then_inc(set_done, 1)
            pool.memset(c.identb[:], 0.0).then_inc(set_done, 1)
            pool.memset(c.maskb[:], 0.0).then_inc(set_done, 1)
            pool.wait_ge(set_done, 3)
            for eye in (c.ident, c.identb):
                pool.affine_select(out=eye[:], in_=eye[:], compare_op=ALU.not_equal, fill=1.0, base=0,
                                   pattern=[[-1, P]], channel_multiplier=1).then_inc(set_done, 1)
            pool.affine_select(out=c.maskb[:], in_=c.maskb[:], compare_op=ALU.is_ge, fill=NEG, base=0,
                               pattern=[[-1, P]], channel_multiplier=1).then_inc(set_done, 1)
            pool.wait_ge(set_done, 6)


def load_layer0(nc, m, c, io):
    c.wq_hi = m.sb("wq_hi", [P, NC, NP0 * PC0], F32R)
    c.wq_lo = m.sb("wq_lo", [P, NC, NP0 * PC0], F32R)
    c.wo_hi = m.sb("wo_hi", [P, NP0, C], F32R)
    c.wo_lo = m.sb("wo_lo", [P, NP0, C], F32R)
    c.wg = m.sb("wg", [P, NC, F0], F32R)
    c.wu = m.sb("wu", [P, NC, F0], F32R)
    c.wd = m.sb("wd", [P, NF0, C], F32R)
    c.mean = m.sb("mean", [P, B * NT])
    c.rstd = m.sb("rstd", [P, B * NT])
    c.rope = m.sb("rope", [P, NT, 3, D0 // 2])
    c.bo = m.sb("bo", [P, C])
    with ExitStack() as ctx:
        t = Mem(nc, ctx)
        xa = t.sb("xa", [P, B * NT, C])
        wq_raw = t.sb("wq_raw", [P, NC, NP0 * PC0])
        wo_raw = t.sb("wo_raw", [P, NP0, C])
        int_raw = t.sb("int_raw", [P, NC, F0], I32)
        stats = t.sb("stats", [P, B * NT, 6])
        aggr = t.sb("aggr", [P, B * NT, 2])
        dev = t.sb("dev", [P, B * NT])
        eps = t.sb("eps", [P, 1])
        x_in = [t.sem(f"x_in{i}") for i in range(2)]
        wq_in = t.sem("wq_in")
        wo_in = t.sem("wo_in")
        small_in = t.sem("small_in")
        int_in = t.sem("int_in")
        int_cast = t.sem("int_cast")
        stats_done = t.sem("stats_done")
        aggr_done = t.sem("aggr_done")
        eps_set = t.sem("eps_set")
        dev_done = t.sem("dev_done")
        rstd_done = t.sem("rstd_done")
        hi_done = t.sem("hi_done")
        lo_done = t.sem("lo_done")
        with nc.Block() as block:
            @block.sync
            def _(sp):
                xt = io.x.rearrange("b (t p) c -> p (b t) c", p=P)
                half = B * NT // 2
                for i in range(2):
                    sp.dma_start(xa[:, i * half:(i + 1) * half, :], xt[:, i * half:(i + 1) * half, :]).then_inc(x_in[i], 16)
                sp.dma_start(c.rope[:], io.rope).then_inc(small_in, 16)
                sp.dma_start(c.bo[:], io.bo0.partition_broadcast(P)).then_inc(small_in, 16)
                sp.wait_ge(small_in, 32)

            @block.scalar
            def _(act):
                act.dma_start(wq_raw[:], io.wqkv0.rearrange("(c p) n -> p c n", p=P)).then_inc(wq_in, 16)
                act.dma_start(wo_raw[:], io.wo0.rearrange("(c p) n -> p c n", p=P)).then_inc(wo_in, 16)
                act.wait_ge(wq_in, 16)
                for i in range(NC):
                    v = wq_raw[:, i, :].rearrange("p (h n) -> p h n", n=PC0)
                    o = c.wq_hi[:, i, :].rearrange("p (h n) -> p h n", n=PC0)
                    act.mul(o[:, :, 0:2 * D0], v[:, :, 0:2 * D0], 1.0 / 8.0).then_inc(hi_done, 1)
                    act.copy(o[:, :, 2 * D0:], v[:, :, 2 * D0:]).then_inc(hi_done, 1)
                act.wait_ge(wo_in, 16)
                act.copy(c.wo_hi[:], wo_raw[:]).then_inc(hi_done, 1)
                act.wait_ge(aggr_done, B * NT)
                act.wait_ge(eps_set, 1)
                act.activation(dev[:], aggr[:, :, 1], ACT.Sqrt, bias=eps[:]).then_inc(dev_done, 1)

            @block.gpsimd
            def _(pool):
                for i, (src, dst) in enumerate(((io.wg0, c.wg), (io.wu0, c.wu), (io.wd0, c.wd))):
                    if i:
                        pool.wait_ge(int_cast, i)
                    stage = int_raw[:].rearrange("p c n -> p (c n)")
                    n = dst.shape[1] * dst.shape[2]
                    pool.dma_start(stage[:, 0:n].rearrange("p (c n) -> p c n", c=dst.shape[1]),
                                   src.rearrange("(c p) n -> p c n", p=P)).then_inc(int_in, 16)
                    pool.wait_ge(int_in, 16 * (i + 1))
                    pool.tensor_copy(dst[:].rearrange("p c n -> p (c n)"), stage[:, 0:n]).then_inc(int_cast, 1)
                pool.wait_ge(int_cast, 3)

            @block.vector
            def _(dve):
                dve.memset(eps[:], EPS).then_inc(eps_set, 1)
                for i in range(B * NT):
                    if i % (B * NT // 2) == 0:
                        dve.wait_ge(x_in[i // (B * NT // 2)], 16)
                    dve.bn_stats(stats[:, i, :], xa[:, i, :]).then_inc(stats_done, 1)
                for i in range(B * NT):
                    dve.wait_ge(stats_done, i + 1)
                    dve.bn_aggr(aggr[:, i, :], stats[:, i, :]).then_inc(aggr_done, 1)
                dve.wait_ge(aggr_done, B * NT)
                dve.tensor_copy(c.mean[:], aggr[:, :, 0]).then_inc(rstd_done, 1)
                for i in range(NC):
                    dve.wait_ge(hi_done, 2 * i + 2)
                    v = wq_raw[:, i, :].rearrange("p (h n) -> p h n", n=PC0)
                    h = c.wq_hi[:, i, :].bitcast(F32).rearrange("p (h n) -> p h n", n=PC0)
                    o = c.wq_lo[:, i, :].rearrange("p (h n) -> p h n", n=PC0)
                    dve.scalar_tensor_tensor(out=o[:, :, 0:2 * D0], in0=v[:, :, 0:2 * D0], scalar=1.0 / 8.0,
                                             in1=h[:, :, 0:2 * D0], op0=ALU.mult, op1=ALU.subtract).then_inc(lo_done, 1)
                    dve.tensor_tensor(o[:, :, 2 * D0:], v[:, :, 2 * D0:], h[:, :, 2 * D0:], ALU.subtract).then_inc(lo_done, 1)
                dve.wait_ge(hi_done, 2 * NC + 1)
                dve.tensor_tensor(c.wo_lo[:], wo_raw[:], c.wo_hi[:].bitcast(F32), ALU.subtract).then_inc(lo_done, 1)
                dve.wait_ge(dev_done, 1)
                dve.reciprocal(c.rstd[:], dev[:]).then_inc(rstd_done, 1)
                dve.wait_ge(rstd_done, 2)
                dve.wait_ge(lo_done, 2 * NC + 1)


def layer0(nc, m, c, io):
    with ExitStack() as ctx:
        t = Mem(nc, ctx)
        x = t.sb("x", [P, 2 * NT, C])
        xn = t.sb("xn", [P, NT, C])
        xt_hi = t.sb("xt_hi", [P, NC, T], F32R)
        xt_lo = t.sb("xt_lo", [P, NC, T], F32R)
        ho_hi = t.sb("ho_hi", [P, NP0, T], F32R)
        ho_lo = t.sb("ho_lo", [P, NP0, T], F32R)
        gate = t.sb("gate", [P, NT, C])
        sg = t.sb("sg", [P, 2, T])
        hid = t.sb("hid", [P, 2, T])
        ra = t.sb("ra", [P, 2, 4 * D0])
        rb = t.sb("rb", [P, 2, 4 * D0])
        qk = t.sb("qk", [P, NT, 4 * D0])
        zq = t.sb("zq", [P, NT, 2, 2 * D0], F32R)
        zk = t.sb("zk", [P, NT, 2, 3 * D0], F32R)
        qs = t.sb("qs", [P, 2, T], F32R)
        k1 = t.sb("k1", [P, 2, T], F32R)
        k2 = t.sb("k2", [P, 2, T], F32R)
        pr = t.sb("pr", [P, 2, 1280])
        pt = t.sb("pt", [P, 2, 1280])
        v_next = t.sb("v_next", [P, NT, 2 * D0])
        v_cur = t.sb("v_cur", [P, NT, 2 * D0])
        nmax = t.sb("nmax", [P, 2, NT])
        rsum = t.sb("rsum", [P, 2, NT])
        rinv = t.sb("rinv", [P, 2, NT])
        so = t.sb("so", [P, 2, C])
        sc = t.ps("sc", [P, 3, 512])
        po = t.ps("po", [P, 512])
        w = t.ps("w", [P, 4, 512])
        x_loaded = t.sem("x_loaded")
        x1_stored = t.sem("x1_stored")
        x1_ready = t.sem("x1_ready")
        xn_ready = t.sem("xn_ready")
        xn_turned = t.sem("xn_turned")
        xt_hi_done = t.sem("xt_hi_done")
        xt_lo_done = t.sem("xt_lo_done")
        gate_up_done = t.sem("gate_up_done")
        silu_done = t.sem("silu_done")
        hid_done = t.sem("hid_done")
        hid_hi_done = t.sem("hid_hi_done")
        hid_lo_done = t.sem("hid_lo_done")
        down_done = t.sem("down_done")
        g_done = t.sem("g_done")
        proj_done = t.sem("proj_done")
        v_next_done = t.sem("v_next_done")
        v_cur_done = t.sem("v_cur_done")
        rope_mult = t.sem("rope_mult")
        rope_done = t.sem("rope_done")
        z_hi_done = t.sem("z_hi_done")
        z_lo_done = t.sem("z_lo_done")
        z_turned = t.sem("z_turned")
        stack_act = t.sem("stack_act")
        stack_dve = t.sem("stack_dve")
        s_done = t.sem("s_done")
        max_done = t.sem("max_done")
        exp_done = t.sem("exp_done")
        rinv_done = t.sem("rinv_done")
        inverse_seen = t.sem("inverse_seen")
        scaled = t.sem("scaled")
        p_turned = t.sem("p_turned")
        pt_copied = t.sem("pt_copied")
        av_done = t.sem("av_done")
        o_hi_done = t.sem("o_hi_done")
        o_lo_done = t.sem("o_lo_done")
        wo_done = t.sem("wo_done")
        so_done = t.sem("so_done")
        mul_done = t.sem("mul_done")

        def score(i):
            return (0, 256 * i) if i < 2 else (i - 1, 0)

        x_dram = io.x.rearrange("b (t p) c -> p b t c", p=P)
        x1_dram = io.x1.rearrange("b (t p) c -> p b t c", p=P)

        with nc.Block() as block:
            @block.sync
            def _(sp):
                sp.dma_start(x[:, 0:NT, :], x_dram[:, 0]).then_inc(x_loaded, 16)
                with sp.Fori(0, B - 1) as b:
                    sp.wait_ge(x_loaded, 16 * b + 16)
                    sp.wait_ge(x1_stored, 16 * b)
                    sp.dma_start(x[:, bass.ds((b + 1) % 2 * NT, NT), :], x_dram[:, bass.ds(b + 1, 1)].rearrange("p o t c -> p (o t) c")).then_inc(x_loaded, 16)
                    sp.wait_ge(x1_ready, NT * b + NT)
                    sp.dma_start(x1_dram[:, bass.ds(b, 1)].rearrange("p o t c -> p (o t) c"), x[:, bass.ds(b % 2 * NT, NT), :]).then_inc(x1_stored, 16)
                sp.wait_ge(x1_stored, 16 * (B - 1))
                sp.wait_ge(x1_ready, NT * B)
                sp.dma_start(x1_dram[:, B - 1], x[:, (B - 1) % 2 * NT:(B - 1) % 2 * NT + NT, :]).then_inc(x1_stored, 16)
                sp.wait_ge(x1_stored, 16 * B)

            @block.tensor
            def _(pe):
                def turn_x(b):
                    for k in range(NC):
                        pe.wait_ge(so_done, NT * b)
                        for i in range(NT):
                            pe.wait_ge(xn_ready, NT * b + i + 1)
                            mm = pe.transpose(w[:, k, i * P:(i + 1) * P], xn[:, i, k * P:(k + 1) * P], c.ident[:])
                        mm.then_inc(xn_turned, 1)

                def ffn(b):
                    for f in range(NF0):
                        for j, wt in enumerate((c.wg, c.wu)):
                            bank = (2 * f + j) % 4
                            if f < 2:
                                pe.wait_ge(xt_hi_done, NC * b + NC)
                                pe.wait_ge(xt_lo_done, NC * b + NC)
                            elif j == 0:
                                pe.wait_ge(silu_done, NF0 * b + f - 1)
                            else:
                                pe.wait_ge(hid_done, NF0 * b + f - 1)
                            for k in range(NC):
                                for q, xt in enumerate((xt_hi, xt_lo)):
                                    mm = pe.matmul(w[:, bank, :], wt[:, k, f * P:(f + 1) * P], xt[:, k, :],
                                                   start=(k == 0 and q == 0), stop=(k == NC - 1 and q == 1))
                            mm.then_inc(gate_up_done, 1)
                    pe.wait_ge(silu_done, NF0 * b + NF0)
                    pe.wait_ge(hid_done, NF0 * b + NF0)
                    for i in range(NT):
                        for f in range(NF0):
                            pe.wait_ge(hid_hi_done, NF0 * b + f + 1)
                            pe.wait_ge(hid_lo_done, NF0 * b + f + 1)
                            for q, hh in enumerate((ho_hi, ho_lo)):
                                mm = pe.matmul(w[:, i, 0:C], hh[:, f, i * P:(i + 1) * P], c.wd[:, f, :],
                                               start=(f == 0 and q == 0), stop=(f == NF0 - 1 and q == 1))
                        mm.then_inc(down_done, 1)

                def project(b, hp, first):
                    n = b * NP0 + hp
                    cols = bass.ds(hp * PC0, PC0)
                    for i in range(NT):
                        if first:
                            pe.wait_ge(g_done, NT * b + NT)
                        elif i == 0:
                            pe.wait_ge(pt_copied, 6 * n - 9)
                        else:
                            pe.wait_ge(pt_copied, 6 * n - 9 + i)
                        bank = (3 + i) % 4
                        for k in range(NC):
                            xh, xl = (a[:, k, i * P:(i + 1) * P] for a in (xt_hi, xt_lo))
                            pe.matmul(w[:, bank, 0:PC0], xh, c.wq_hi[:, k, cols], start=(k == 0), stop=False)
                            pe.matmul(w[:, bank, 0:PC0], xh, c.wq_lo[:, k, cols], start=False, stop=False)
                            mm = pe.matmul(w[:, bank, 0:PC0], xl, c.wq_hi[:, k, cols], start=False, stop=(k == NC - 1))
                        mm.then_inc(proj_done, 1)

                def turn_z(n):
                    pe.wait_ge(z_hi_done, 4 * n + 4)
                    pe.wait_ge(z_lo_done, 4 * n + 4)
                    pe.wait_ge(v_next_done, NT * n + NT)
                    for j in range(6):
                        if j == 4:
                            pe.wait_ge(stack_act, 3 * n + 1)
                        if j == 5:
                            pe.wait_ge(stack_act, 3 * n + 2)
                        h, at = ((0, None), (1, None), (0, 0), (0, D0), (1, 0), (1, D0))[j]
                        for i in range(NT):
                            src = zq[:, i, h, :] if at is None else zk[:, i, h, at:at + 2 * D0]
                            mm = pe.transpose(w[:, (3 + j) % 4, i * P:(i + 1) * P], src.bitcast(F32), c.ident[:])
                        mm.then_inc(z_turned, 1)

                def scores(n, h):
                    if h == 0:
                        pe.wait_ge(stack_act, 3 * n + 3)
                        pe.wait_ge(stack_dve, 3 * n + 3)
                    for i in range(NT):
                        bank, at = score(i)
                        pe.wait_ge(exp_done, 8 * n + 4 * h + (2, 2, 3, 4)[i])
                        width = max(256, (i + 1) * P)
                        q = qs[:, h, i * P:(i + 1) * P]
                        out = sc[:, bank, at:at + width]
                        pe.matmul(out, q, k1[:, h, 0:width], start=True, stop=False)
                        pe.matmul(out, q, k2[:, h, 0:width], start=False, stop=False)
                        pe.matmul(sc[:, bank, at + i * P:at + (i + 1) * P], c.identb[:], c.maskb[:],
                                  start=False, stop=True).then_inc(s_done, 1)

                def turn_p(n, h):
                    pe.wait_ge(scaled, 8 * n + 4 * h + 4)
                    first = 1 - h
                    tiles = [[(0, i, i * P) for i in range(4)],
                             [(1, i, (i - 1) * P) for i in range(1, 4)] + [(3, 3, 3 * P)],
                             [(2, i, (i - 2) * P) for i in range(2, 4)]]
                    for j, tile in enumerate(tiles):
                        for kt, i, at in tile:
                            mm = pe.transpose(w[:, first + j, at:at + P],
                                              pr[:, h, SOFF[i] + kt * P:SOFF[i] + (kt + 1) * P], c.ident[:])
                        mm.then_inc(p_turned, 1)

                def weigh(n):
                    pe.wait_ge(pt_copied, 6 * n + 6)
                    pe.wait_ge(v_cur_done, n + 1)
                    pe.wait_ge(o_hi_done, n)
                    pe.wait_ge(o_lo_done, n)
                    for kt in range(NT):
                        for h in range(2):
                            mm = pe.matmul(po[h * D0:(h + 1) * D0, kt * P:T], v_cur[:, kt, h * D0:(h + 1) * D0],
                                           pt[:, h, PTOFF[kt]:PTOFF[kt] + T - kt * P], start=(kt == 0), stop=(kt == NT - 1))
                    mm.then_inc(av_done, 1)

                def pair(b, hp, first=False, last=False):
                    n = b * NP0 + hp
                    scores(n, 0)
                    if not first:
                        pe.wait_ge(pt_copied, 6 * n - 4)
                        turn_p(n - 1, 1)
                        weigh(n - 1)
                    if not last:
                        if first:
                            project_next(b, hp + 1)
                        else:
                            project(b, hp + 1, False)
                    scores(n, 1)
                    if not last:
                        turn_z(n + 1)
                        pe.wait_ge(stack_act, 3 * n + 6)
                        pe.wait_ge(stack_dve, 3 * n + 5)
                    else:
                        pe.wait_ge(pt_copied, 6 * n)
                    turn_p(n, 0)

                def project_next(b, hp):
                    cols = bass.ds(hp * PC0, PC0)
                    for i in range(NT):
                        bank = (3 + i) % 4
                        for k in range(NC):
                            xh, xl = (a[:, k, i * P:(i + 1) * P] for a in (xt_hi, xt_lo))
                            pe.matmul(w[:, bank, 0:PC0], xh, c.wq_hi[:, k, cols], start=(k == 0), stop=False)
                            pe.matmul(w[:, bank, 0:PC0], xh, c.wq_lo[:, k, cols], start=False, stop=False)
                            mm = pe.matmul(w[:, bank, 0:PC0], xl, c.wq_hi[:, k, cols], start=False, stop=(k == NC - 1))
                        mm.then_inc(proj_done, 1)

                def out_project(b):
                    n = b * NP0 + NP0
                    pe.wait_ge(pt_copied, 6 * n)
                    pe.wait_ge(o_hi_done, n)
                    pe.wait_ge(o_lo_done, n)
                    for i in range(NT):
                        for k in range(NP0):
                            oh, ol = (a[:, k, i * P:(i + 1) * P] for a in (ho_hi, ho_lo))
                            pe.matmul(w[:, i, 0:C], oh, c.wo_hi[:, k, :], start=(k == 0), stop=False)
                            pe.matmul(w[:, i, 0:C], oh, c.wo_lo[:, k, :], start=False, stop=False)
                            mm = pe.matmul(w[:, i, 0:C], ol, c.wo_hi[:, k, :], start=False, stop=(k == NP0 - 1))
                        mm.then_inc(wo_done, 1)

                with pe.Fori(0, B) as b:
                    turn_x(b)
                    ffn(b)
                    project(b, 0, True)
                    turn_z(b * NP0)
                    pair(b, 0, first=True)
                    with pe.Fori(1, NP0 - 1) as hp:
                        pair(b, hp)
                    pair(b, NP0 - 1, last=True)
                    n = b * NP0 + NP0 - 1
                    pe.wait_ge(pt_copied, 6 * n + 2)
                    turn_p(n, 1)
                    weigh(n)
                    out_project(b)

            @block.scalar
            def _(act):
                def exps(n, h):
                    for i in range(NT):
                        act.wait_ge(max_done, 8 * n + 4 * h + (2, 2, 3, 4)[i])
                        bank, at = score(i)
                        act.activation(pr[:, h, SOFF[i]:SOFF[i] + (i + 1) * P], sc[:, bank, at:at + (i + 1) * P], ACT.Exp,
                                       bias=nmax[:, h, i:i + 1], accum_out=rsum[:, h, i:i + 1]).then_inc(exp_done, 1)

                def take_z(n):
                    for i in range(NT):
                        act.wait_ge(rope_mult, NT * n + i + 1)
                        if i == 0:
                            act.wait_ge(v_cur_done, n)
                        act.copy(v_next[:, i, :], w[:, (3 + i) % 4, 4 * D0:PC0]).then_inc(v_next_done, 1)
                        if i % 2:
                            act.wait_ge(rope_done, NT * n + i + 1)
                            if i == 1:
                                act.wait_ge(z_turned, 6 * n)
                            two = slice(i - 1, i + 1)
                            act.copy(zq[:, two, :, 0:D0], qk[:, two, 0:2 * D0].rearrange("p t (h d) -> p t h d", h=2)).then_inc(z_hi_done, 1)
                            kk = qk[:, two, 2 * D0:].rearrange("p t (h d) -> p t h d", h=2)
                            for j in (0, 2):
                                last = act.copy(zk[:, two, :, j * D0:(j + 1) * D0], kk)
                            last.then_inc(z_hi_done, 1)

                def take_stacks(n):
                    act.wait_ge(s_done, 8 * n)
                    for j, dst in enumerate((qs[:, 0, :], qs[:, 1, :], k1[:, 0, :])):
                        act.wait_ge(z_turned, 6 * n + j + 1)
                        act.copy(dst, w[:, (3 + j) % 4, :]).then_inc(stack_act, 1)

                def take_o(n, hp):
                    act.wait_ge(av_done, n + 1)
                    act.copy(ho_hi[:, bass.ds(hp, 1), :].rearrange("p o t -> p (o t)"), po[:, :]).then_inc(o_hi_done, 1)

                def pass_v(n):
                    act.wait_ge(av_done, n)
                    act.wait_ge(v_next_done, NT * n + NT)
                    act.copy(v_cur[:], v_next[:]).then_inc(v_cur_done, 1)

                def pair(b, hp, first=False, last=False):
                    n = b * NP0 + hp
                    exps(n, 0)
                    if not first:
                        take_o(n - 1, hp - 1)
                    pass_v(n)
                    if not last:
                        take_z(n + 1)
                        take_stacks(n + 1)
                    exps(n, 1)

                act.copy(nmax[:, 0, 0:1], c.ident[:, 0:1]).then_inc(exp_done, 4)
                with act.Fori(0, B) as b:
                    for k in range(NC):
                        act.wait_ge(xn_turned, NC * b + k + 1)
                        act.wait_ge(proj_done, NT * NP0 * b)
                        act.copy(xt_hi[:, k, :], w[:, k, :]).then_inc(xt_hi_done, 1)
                    for f in range(NF0 + 1):
                        if f < NF0:
                            act.wait_ge(gate_up_done, 2 * NF0 * b + 2 * f + 1)
                            if f > 1:
                                act.wait_ge(hid_done, NF0 * b + f - 1)
                            act.activation(sg[:, f % 2, :], w[:, 2 * f % 4, :], ACT.Silu, scale=DEQ).then_inc(silu_done, 1)
                        if f > 0:
                            act.wait_ge(hid_done, NF0 * b + f)
                            if f == 1:
                                act.wait_ge(wo_done, NT * b)
                            act.copy(ho_hi[:, f - 1, :], hid[:, (f - 1) % 2, :]).then_inc(hid_hi_done, 1)
                    for i in range(NT):
                        act.wait_ge(down_done, NT * b + i + 1)
                        if i == 0:
                            act.wait_ge(x1_ready, NT * b)
                        act.activation(gate[:, i, :], w[:, i, 0:C], ACT.Silu, scale=DEQ).then_inc(g_done, 1)
                    take_z(b * NP0)
                    take_stacks(b * NP0)
                    pair(b, 0, first=True)
                    with act.Fori(1, NP0 - 1) as hp:
                        pair(b, hp)
                    pair(b, NP0 - 1, last=True)
                    take_o(b * NP0 + NP0 - 1, NP0 - 1)

            @block.vector
            def _(dve):
                def maxima(n, h):
                    for i in range(NT):
                        bank, at = score(i)
                        dve.wait_ge(s_done, 8 * n + 4 * h + (2, 2, 3, 4)[i])
                        dve.tensor_reduce(nmax[:, h, i:i + 1], sc[:, bank, at:at + (i + 1) * P], AXX, ALU.max,
                                          negate=True).then_inc(max_done, 1)

                def take_p(n, h):
                    first = 1 - h
                    for j, (at, width) in enumerate(((0, 512), (512, 512), (1024, 256))):
                        dve.wait_ge(p_turned, 6 * n + 3 * h + j + 1)
                        if j == 0:
                            dve.wait_ge(av_done, n)
                        dve.tensor_copy(pt[:, h, at:at + width], w[:, first + j, 0:width]).then_inc(pt_copied, 1)

                def invert(n, h):
                    dve.wait_ge(exp_done, 8 * n + 4 * h + 8)
                    dve.reciprocal(rinv[:, h, :], rsum[:, h, :]).then_inc(rinv_done, 1)

                def rope(n):
                    for i in range(NT):
                        dve.wait_ge(proj_done, NT * n + i + 1)
                        if i > 1:
                            dve.wait_ge(rope_done, NT * n + i - 1)
                        elif i == 0:
                            dve.wait_ge(rope_done, NT * n)
                        src = w[:, (3 + i) % 4, 0:4 * D0].rearrange("p (s e d) -> p s e d", s=4, e=2)
                        a = ra[:, i % 2, :].rearrange("p (s d) -> p s d", d=D0 // 2)
                        r = rb[:, i % 2, :].rearrange("p (s e d) -> p s e d", s=4, e=2)
                        dve.tensor_tensor(a, w[:, (3 + i) % 4, 0:4 * D0].rearrange("p (s d) -> p s d", d=D0 // 2),
                                          c.rope[:, i, 0, :].unsqueeze(1).to_broadcast([P, 8, D0 // 2]), ALU.mult)
                        dve.tensor_tensor(r[:, :, 0, :], src[:, :, 1, :],
                                          c.rope[:, i, 2, :].unsqueeze(1).to_broadcast([P, 4, D0 // 2]), ALU.mult)
                        dve.tensor_tensor(r[:, :, 1, :], src[:, :, 0, :],
                                          c.rope[:, i, 1, :].unsqueeze(1).to_broadcast([P, 4, D0 // 2]), ALU.mult).then_inc(rope_mult, 1)

                def take_stacks(n):
                    dve.wait_ge(s_done, 8 * n)
                    for j, dst in enumerate((k2[:, 0, :], k1[:, 1, :], k2[:, 1, :])):
                        dve.wait_ge(z_turned, 6 * n + j + 4)
                        dve.tensor_copy(dst, w[:, (6 + j) % 4, :]).then_inc(stack_dve, 1)

                def take_o(n, hp):
                    dve.wait_ge(o_hi_done, n + 1)
                    at = bass.ds(hp, 1)
                    dve.tensor_tensor(ho_lo[:, at, :].rearrange("p o t -> p (o t)"), po[:, :],
                                      ho_hi[:, at, :].bitcast(F32).rearrange("p o t -> p (o t)"), ALU.subtract).then_inc(o_lo_done, 1)

                def pair(b, hp, first=False, last=False):
                    n = b * NP0 + hp
                    maxima(n, 0)
                    if not first:
                        take_p(n - 1, 1)
                    invert(n, 0)
                    if not first:
                        take_o(n - 1, hp - 1)
                    if not last:
                        rope(n + 1)
                    maxima(n, 1)
                    if not last:
                        take_stacks(n + 1)
                    take_p(n, 0)
                    invert(n, 1)

                with dve.Fori(0, B) as b:
                    dve.wait_ge(x_loaded, 16 * b + 16)
                    dve.wait_ge(xn_turned, NC * b)
                    for i in range(NT):
                        dve.tensor_scalar(xn[:, i, :], x[:, bass.ds(b % 2 * NT + i, 1), :].rearrange("p o c -> p (o c)"),
                                          c.mean[:, bass.ds(b * NT + i, 1)], c.rstd[:, bass.ds(b * NT + i, 1)],
                                          ALU.subtract, ALU.mult).then_inc(xn_ready, 1)
                    for k in range(NC):
                        dve.wait_ge(xt_hi_done, NC * b + k + 1)
                        dve.tensor_tensor(xt_lo[:, k, :], w[:, k, :], xt_hi[:, k, :].bitcast(F32), ALU.subtract).then_inc(xt_lo_done, 1)
                    for f in range(NF0):
                        dve.wait_ge(silu_done, NF0 * b + f + 1)
                        dve.wait_ge(gate_up_done, 2 * NF0 * b + 2 * f + 2)
                        if f > 1:
                            dve.wait_ge(hid_lo_done, NF0 * b + f - 1)
                        dve.scalar_tensor_tensor(out=hid[:, f % 2, :], in0=w[:, (2 * f + 1) % 4, :], scalar=DEQ,
                                                 in1=sg[:, f % 2, :], op0=ALU.mult, op1=ALU.mult).then_inc(hid_done, 1)
                    rope(b * NP0)
                    take_stacks(b * NP0)
                    pair(b, 0, first=True)
                    with dve.Fori(1, NP0 - 1) as hp:
                        pair(b, hp)
                    pair(b, NP0 - 1, last=True)
                    n = b * NP0 + NP0 - 1
                    take_p(n, 1)
                    take_o(n, NP0 - 1)
                    for i in range(NT):
                        dve.wait_ge(wo_done, NT * b + i + 1)
                        if i > 1:
                            dve.wait_ge(x1_ready, NT * b + i - 1)
                        dve.tensor_tensor(so[:, i % 2, :], w[:, i, 0:C], c.bo[:], ALU.add).then_inc(so_done, 1)

            @block.gpsimd
            def _(pool):
                def scale(n, h):
                    pool.wait_ge(rinv_done, 2 * n + h + 1)
                    pool.sem_inc(inverse_seen, 1)
                    for i in range(NT):
                        p = pr[:, h, SOFF[i]:SOFF[i] + (i + 1) * P]
                        pool.tensor_scalar(p, p, rinv[:, h, i:i + 1], 1.0, ALU.mult, ALU.mult).then_inc(scaled, 1)

                def split_z(n):
                    for i in range(NT):
                        pool.wait_ge(rope_mult, NT * n + i + 1)
                        if i == 0:
                            pool.wait_ge(z_lo_done, 4 * n)
                            pool.wait_ge(z_hi_done, 4 * n)
                        pool.tensor_tensor(qk[:, i, :], ra[:, i % 2, :], rb[:, i % 2, :], ALU.add).then_inc(rope_done, 1)
                        if i % 2:
                            two = slice(i - 1, i + 1)
                            pool.wait_ge(rope_done, NT * n + i + 1)
                            pool.wait_ge(z_hi_done, 4 * n + i)
                            pool.tensor_tensor(zq[:, two, :, D0:2 * D0], qk[:, two, 0:2 * D0].rearrange("p t (h d) -> p t h d", h=2),
                                               zq[:, two, :, 0:D0].bitcast(F32), ALU.subtract).then_inc(z_lo_done, 1)
                            pool.wait_ge(z_hi_done, 4 * n + i + 1)
                            pool.tensor_tensor(zk[:, two, :, D0:2 * D0], qk[:, two, 2 * D0:].rearrange("p t (h d) -> p t h d", h=2),
                                               zk[:, two, :, 0:D0].bitcast(F32), ALU.subtract).then_inc(z_lo_done, 1)

                def pair(n, last=False):
                    scale(n, 0)
                    if not last:
                        split_z(n + 1)
                    scale(n, 1)

                with pool.Fori(0, B) as b:
                    for f in range(NF0):
                        pool.wait_ge(hid_hi_done, NF0 * b + f + 1)
                        pool.tensor_tensor(ho_lo[:, f, :], hid[:, f % 2, :], ho_hi[:, f, :].bitcast(F32), ALU.subtract).then_inc(hid_lo_done, 1)
                    split_z(b * NP0)
                    pair(b * NP0)
                    with pool.Fori(1, NP0 - 1) as hp:
                        pair(b * NP0 + hp)
                    pair(b * NP0 + NP0 - 1, last=True)
                    for i in range(NT):
                        pool.wait_ge(so_done, NT * b + i + 1)
                        pool.wait_ge(g_done, NT * b + i + 1)
                        pool.tensor_tensor(so[:, i % 2, :], so[:, i % 2, :], gate[:, i, :], ALU.mult).then_inc(mul_done, 1)
                        pool.wait_ge(mul_done, NT * b + i + 1)
                        xi = x[:, bass.ds(b % 2 * NT + i, 1), :].rearrange("p o c -> p (o c)")
                        pool.tensor_tensor(xi, xi, so[:, i % 2, :], ALU.add).then_inc(x1_ready, 1)


def norm_transpose1(nc, c, io):
    with ExitStack() as ctx:
        t = Mem(nc, ctx)
        xa = t.sb("xa1", [P, B * NT, C])
        xn = t.sb("xn1", [P, 2, NT, C])
        stats = t.sb("stats1", [P, B * NT, 6])
        aggr = t.sb("aggr1", [P, B * NT, 2])
        dev = t.sb("dev1", [P, B * NT])
        rstd = t.sb("rstd1", [P, B * NT])
        eps = t.sb("eps1", [P, 1])
        w = t.ps("w1p", [P, 4, 512])
        x_in = [t.sem(f"x1_in{i}") for i in range(2)]
        eps_set = t.sem("eps_set1")
        stats_done = t.sem("stats_done1")
        aggr_done = t.sem("aggr_done1")
        dev_done = t.sem("dev_done1")
        rstd_done = t.sem("rstd_done1")
        xn_ready = t.sem("xn_ready1")
        xn_turned = t.sem("xn_turned1")
        hi_done = t.sem("hi_done1")
        lo_done = t.sem("lo_done1")
        stored = t.sem("xt1_stored")
        with nc.Block() as block:
            @block.sync
            def _(sp):
                xt = io.x1.rearrange("b (t p) c -> p (b t) c", p=P)
                half = B * NT // 2
                for i in range(2):
                    sp.dma_start(xa[:, i * half:(i + 1) * half, :], xt[:, i * half:(i + 1) * half, :]).then_inc(x_in[i], 16)
                sp.wait_ge(hi_done, NC * B)
                sp.dma_start(io.xt1_hi, c.xt1_hi[:].bitcast(F32)).then_inc(stored, 16)
                sp.wait_ge(lo_done, NC * B)
                sp.dma_start(io.xt1_lo, c.xt1_lo[:].bitcast(F32)).then_inc(stored, 16)
                sp.wait_ge(stored, 32)

            @block.vector
            def _(dve):
                dve.memset(eps[:], EPS).then_inc(eps_set, 1)
                for i in range(B * NT):
                    if i % (B * NT // 2) == 0:
                        dve.wait_ge(x_in[i // (B * NT // 2)], 16)
                    dve.bn_stats(stats[:, i, :], xa[:, i, :]).then_inc(stats_done, 1)
                for i in range(B * NT):
                    dve.wait_ge(stats_done, i + 1)
                    dve.bn_aggr(aggr[:, i, :], stats[:, i, :]).then_inc(aggr_done, 1)
                dve.wait_ge(dev_done, 1)
                dve.wait_ge(aggr_done, B * NT)
                dve.reciprocal(rstd[:], dev[:]).then_inc(rstd_done, 1)
                dve.wait_ge(rstd_done, 1)

                def normalise(b, u):
                    dve.wait_ge(xn_turned, NC * b - NC * u)
                    for i in range(NT):
                        at = bass.ds(b * NT + i, 1)
                        dve.tensor_scalar(xn[:, u, i, :], xa[:, at, :].rearrange("p o c -> p (o c)"), aggr[:, at, 0],
                                          rstd[:, at], ALU.subtract, ALU.mult).then_inc(xn_ready, 1)

                with dve.Fori(0, B // 2) as bb:
                    for u in range(2):
                        normalise(bb * 2 + u, u)
                    for u in range(2):
                        b = bb * 2 + u
                        for k in range(NC):
                            dve.wait_ge(hi_done, NC * b + k + 1)
                            at = bass.ds(b * T, T)
                            dve.tensor_tensor(c.xt1_lo[:, k, at], w[:, 2 * u + k, :], c.xt1_hi[:, k, at].bitcast(F32),
                                              ALU.subtract).then_inc(lo_done, 1)

            @block.tensor
            def _(pe):
                with pe.Fori(0, B // 2) as bb:
                    for u in range(2):
                        b = bb * 2 + u
                        pe.wait_ge(xn_ready, NT * b + NT)
                        pe.wait_ge(lo_done, NC * 2 * bb)
                        for k in range(NC):
                            for i in range(NT):
                                mm = pe.transpose(w[:, 2 * u + k, i * P:(i + 1) * P], xn[:, u, i, k * P:(k + 1) * P], c.ident[:])
                            mm.then_inc(xn_turned, 1)

            @block.scalar
            def _(act):
                act.wait_ge(aggr_done, B * NT)
                act.wait_ge(eps_set, 1)
                act.activation(dev[:], aggr[:, :, 1], ACT.Sqrt, bias=eps[:]).then_inc(dev_done, 1)
                with act.Fori(0, B // 2) as bb:
                    for u in range(2):
                        b = bb * 2 + u
                        for k in range(NC):
                            act.wait_ge(xn_turned, NC * b + k + 1)
                            act.copy(c.xt1_hi[:, k, bass.ds(b * T, T)], w[:, 2 * u + k, :]).then_inc(hi_done, 1)


def load_layer1(nc, m, c, io):
    c.wq1_hi, c.wq1_lo = (m.sb(n, [P, NC, 3 * C], F32R) for n in ("wq1_hi", "wq1_lo"))
    c.wo1_hi, c.wo1_lo = (m.sb(n, [P, NC, C], F32R) for n in ("wo1_hi", "wo1_lo"))
    c.bqkv1 = m.sb("bqkv1", [P, 3 * C])
    c.bo1 = m.sb("bo1_sb", [P, C])
    with ExitStack() as ctx:
        t = Mem(nc, ctx)
        wq = t.sb("wq1_raw", [P, NC, 3 * C])
        wo = t.sb("wo1_raw", [P, NC, C])
        loaded = t.sem("l1_loaded")
        hi = t.sem("l1_hi")
        lo = t.sem("l1_lo")
        with nc.Block() as block:
            @block.sync
            def _(sp):
                sp.dma_start(wq[:], io.wqkv1.rearrange("(c p) n -> p c n", p=P)).then_inc(loaded, 16)
                sp.dma_start(wo[:], io.wo1.rearrange("(c p) n -> p c n", p=P)).then_inc(loaded, 16)
                sp.dma_start(c.bqkv1[:], io.bqkv1.partition_broadcast(P)).then_inc(loaded, 16)
                sp.dma_start(c.bo1[:], io.bo1.partition_broadcast(P)).then_inc(loaded, 16)

            @block.scalar
            def _(act):
                act.wait_ge(loaded, 64)
                act.mul(c.wq1_hi[:, :, 0:C], wq[:, :, 0:C], 0.25).then_inc(hi, 1)
                act.copy(c.wq1_hi[:, :, C:], wq[:, :, C:]).then_inc(hi, 1)
                act.copy(c.wo1_hi[:], wo[:]).then_inc(hi, 1)

            @block.vector
            def _(dve):
                dve.wait_ge(loaded, 64)
                dve.tensor_scalar(c.bqkv1[:, 0:C], c.bqkv1[:, 0:C], 0.25, None, ALU.mult).then_inc(lo, 1)
                dve.wait_ge(hi, 3)
                dve.scalar_tensor_tensor(out=c.wq1_lo[:, :, 0:C], in0=wq[:, :, 0:C], scalar=0.25,
                                         in1=c.wq1_hi[:, :, 0:C].bitcast(F32), op0=ALU.mult, op1=ALU.subtract).then_inc(lo, 1)
                dve.tensor_tensor(c.wq1_lo[:, :, C:], wq[:, :, C:], c.wq1_hi[:, :, C:].bitcast(F32), ALU.subtract).then_inc(lo, 1)
                dve.tensor_tensor(c.wo1_lo[:], wo[:], c.wo1_hi[:].bitcast(F32), ALU.subtract).then_inc(lo, 1)
                dve.wait_ge(lo, 4)


def experts(nc, c, io):
    with ExitStack() as ctx:
        t = Mem(nc, ctx)
        r1, r3 = (t.sb(f"raw{n}", [P, NC, FP1]) for n in (1, 3))
        r2 = t.sb("raw2", [P, NF1, C])
        w1h, w1l, w3h, w3l = (t.sb(n, [P, 2, NC, FP1], F32R) for n in ("w1h", "w1l", "w3h", "w3l"))
        w2h, w2l = (t.sb(n, [P, 2, NF1, C], F32R) for n in ("w2h", "w2l"))
        hh, hl = (t.sb(n, [P, NF1, T], F32R) for n in ("hh", "hl"))
        sg = t.sb("sg1", [P, 2, T])
        hid = t.sb("hid1", [P, 2, T])
        go = t.sb("go", [P, NT, C])
        w = t.ps("wx", [P, 4, 512])
        dn = t.ps("dn", [P, 4, 512])
        w13_in = t.sem("w13_in")
        w2_in = t.sem("w2_in")
        pad_set = t.sem("pad_set")
        hi13 = t.sem("hi13")
        lo13 = t.sem("lo13")
        hi2 = t.sem("hi2")
        lo2 = t.sem("lo2")
        gate_up_done = t.sem("gate_up_done1")
        silu_done = t.sem("silu_done1")
        hid_done = t.sem("hid_done1")
        hid_hi_done = t.sem("hid_hi_done1")
        hid_lo_done = t.sem("hid_lo_done1")
        down_done = t.sem("down_done1")
        g_done = t.sem("g_done1")
        g_stored = t.sem("g_stored")

        with nc.Block() as block:
            @block.sync
            def _(sp):
                def load(e):
                    one = bass.ds(e, 1)
                    full = (NF1 - 1) * P
                    sp.wait_ge(hi13, 2 * e)
                    sp.wait_ge(lo13, 2 * e)
                    sp.dma_start(r1[:, :, 0:F1], io.w1[one].rearrange("o (c p) f -> p (o c) f", p=P)).then_inc(w13_in, 16)
                    sp.dma_start(r3[:, :, 0:F1], io.w3[one].rearrange("o (c p) f -> p (o c) f", p=P)).then_inc(w13_in, 16)
                    sp.wait_ge(hi2, e)
                    sp.wait_ge(lo2, e)
                    sp.dma_start(r2[:, 0:NF1 - 1, :], io.w2[one, 0:full].rearrange("o (f p) n -> p (o f) n", p=P)).then_inc(w2_in, 16)
                    sp.dma_start(r2[0:FR1, NF1 - 1:NF1, :], io.w2[one, full:F1].rearrange("o p n -> p o n")).then_inc(w2_in, 16)

                def store(e):
                    for i in range(NT):
                        sp.wait_ge(g_done, NT * e + i + 1)
                        dst = io.gate1.rearrange("b (e k) c -> e b k c", e=E1)[bass.ds(e, 1), 2 * i:2 * i + 2]
                        sp.dma_start(dst.rearrange("o b k c -> (o b) k c"), go[:, i, :]).then_inc(g_stored, 16)

                sp.wait_ge(pad_set, 3)
                load(0)
                load(1)
                with sp.Fori(0, E1 - 2) as e:
                    store(e)
                    load(e + 2)
                store(E1 - 2)
                store(E1 - 1)
                sp.wait_ge(g_stored, 16 * NT * E1)

            @block.gpsimd
            def _(pool):
                pool.memset(r2[FR1:P, NF1 - 1, :], 0.0).then_inc(pad_set, 1)
                pool.wait_ge(pad_set, 1)
                pool.memset(r1[:, :, F1:FP1], 0.0).then_inc(pad_set, 1)
                pool.memset(r3[:, :, F1:FP1], 0.0).then_inc(pad_set, 1)
                with pool.Fori(0, E1) as e:
                    for f in range(NF1):
                        pool.wait_ge(hid_hi_done, NF1 * e + f + 1)
                        pool.tensor_tensor(hl[:, f, :], hid[:, f % 2, :], hh[:, f, :].bitcast(F32),
                                           ALU.subtract).then_inc(hid_lo_done, 1)

            @block.scalar
            def _(act):
                def split(e, u, part):
                    if part == 0:
                        act.wait_ge(down_done, NT * (e - 1))
                    if part < 2:
                        act.wait_ge(w13_in, 32 * e + 32)
                        act.copy((w1h, w3h)[part][:, u], (r1, r3)[part][:]).then_inc(hi13, 1)
                    else:
                        act.wait_ge(w2_in, 32 * e + 32)
                        act.copy(w2h[:, u], r2[:]).then_inc(hi2, 1)

                def ffn(e, u, last=False):
                    for f in range(NF1 + 1):
                        if f < NF1:
                            act.wait_ge(gate_up_done, 2 * NF1 * e + 2 * f + 1)
                            if f > 1:
                                act.wait_ge(hid_done, NF1 * e + f - 1)
                            act.activation(sg[:, f % 2, :], w[:, 2 * f % 4, :], ACT.Silu).then_inc(silu_done, 1)
                        if f > 0:
                            act.wait_ge(hid_done, NF1 * e + f)
                            act.copy(hh[:, f - 1, :], hid[:, (f - 1) % 2, :]).then_inc(hid_hi_done, 1)
                        if f in (1, 3, 5) and not last:
                            split(e + 1, 1 - u, f // 2)
                    for i in range(NT):
                        act.wait_ge(down_done, NT * e + i + 1)
                        if i == 0:
                            act.wait_ge(g_stored, 16 * NT * e)
                        act.activation(go[:, i, :], dn[:, i, 0:C], ACT.Silu).then_inc(g_done, 1)

                act.wait_ge(pad_set, 3)
                act.wait_ge(w13_in, 32)
                act.copy(w1h[:, 0], r1[:]).then_inc(hi13, 1)
                act.copy(w3h[:, 0], r3[:]).then_inc(hi13, 1)
                act.wait_ge(w2_in, 32)
                act.copy(w2h[:, 0], r2[:]).then_inc(hi2, 1)
                with act.Fori(0, E1 // 2 - 1) as p:
                    ffn(2 * p, 0)
                    ffn(2 * p + 1, 1)
                ffn(E1 - 2, 0)
                ffn(E1 - 1, 1, last=True)

            @block.vector
            def _(dve):
                def split(e, u, part):
                    if part < 2:
                        dve.wait_ge(hi13, 2 * e + part + 1)
                        hi, lo, raw = ((w1h, w1l, r1), (w3h, w3l, r3))[part]
                        dve.tensor_tensor(lo[:, u], raw[:], hi[:, u].bitcast(F32), ALU.subtract).then_inc(lo13, 1)
                    else:
                        dve.wait_ge(hi2, e + 1)
                        dve.tensor_tensor(w2l[:, u], r2[:], w2h[:, u].bitcast(F32), ALU.subtract).then_inc(lo2, 1)

                def ffn(e, u, last=False):
                    for f in range(NF1):
                        dve.wait_ge(silu_done, NF1 * e + f + 1)
                        dve.wait_ge(gate_up_done, 2 * NF1 * e + 2 * f + 2)
                        if f > 1:
                            dve.wait_ge(hid_lo_done, NF1 * e + f - 1)
                        dve.tensor_tensor(hid[:, f % 2, :], w[:, (2 * f + 1) % 4, :], sg[:, f % 2, :],
                                          ALU.mult).then_inc(hid_done, 1)
                        if f in (2, 4, 5) and not last:
                            split(e + 1, 1 - u, {2: 0, 4: 1, 5: 2}[f])

                for part in range(3):
                    split(0, 0, part)
                with dve.Fori(0, E1 // 2 - 1) as p:
                    ffn(2 * p, 0)
                    ffn(2 * p + 1, 1)
                ffn(E1 - 2, 0)
                ffn(E1 - 1, 1, last=True)

            @block.tensor
            def _(pe):
                def tokens(xt, k, e):
                    return xt[:, k, :].rearrange("p (b e k) -> p b e k", b=B, e=E1)[:, :, bass.ds(e, 1), :].rearrange("p b o k -> p b (o k)")

                def ffn(e, u):
                    pe.wait_ge(hi13, 2 * e + 2)
                    pe.wait_ge(lo13, 2 * e + 2)
                    for f in range(NF1):
                        cols = slice(f * P, (f + 1) * P)
                        for j, (wh, wl) in enumerate(((w1h, w1l), (w3h, w3l))):
                            if f < 2:
                                pe.wait_ge(silu_done, NF1 * e)
                                pe.wait_ge(hid_done, NF1 * e)
                            elif j == 0:
                                pe.wait_ge(silu_done, NF1 * e + f - 1)
                            else:
                                pe.wait_ge(hid_done, NF1 * e + f - 1)
                            out = w[:, (2 * f + j) % 4, :].rearrange("p (b k) -> p b k", b=B)
                            for k in range(NC):
                                pe.matmul(out, wh[:, u, k, cols], tokens(c.xt1_hi, k, e), start=(k == 0), stop=False)
                                pe.matmul(out, wh[:, u, k, cols], tokens(c.xt1_lo, k, e), start=False, stop=False)
                                mm = pe.matmul(out, wl[:, u, k, cols], tokens(c.xt1_hi, k, e), start=False, stop=(k == NC - 1))
                            mm.then_inc(gate_up_done, 1)
                    pe.wait_ge(hi2, e + 1)
                    pe.wait_ge(lo2, e + 1)
                    pe.wait_ge(g_done, NT * e)
                    for f in range(NF1):
                        pe.wait_ge(hid_hi_done, NF1 * e + f + 1)
                        pe.wait_ge(hid_lo_done, NF1 * e + f + 1)
                        for i in range(NT):
                            a, b = hh[:, f, i * P:(i + 1) * P], hl[:, f, i * P:(i + 1) * P]
                            pe.matmul(dn[:, i, 0:C], a, w2h[:, u, f, :], start=(f == 0), stop=False)
                            pe.matmul(dn[:, i, 0:C], a, w2l[:, u, f, :], start=False, stop=False)
                            mm = pe.matmul(dn[:, i, 0:C], b, w2h[:, u, f, :], start=False, stop=(f == NF1 - 1))
                            if f == NF1 - 1:
                                mm.then_inc(down_done, 1)

                with pe.Fori(0, E1 // 2) as p:
                    ffn(2 * p, 0)
                    ffn(2 * p + 1, 1)


def attention1(nc, c, io):
    HG = H1 // NG1
    S3 = 3 * D1
    wq_hi, wq_lo = c.wq1_hi, c.wq1_lo
    with ExitStack() as ctx:
        t = Mem(nc, ctx)
        xs_hi, xs_lo = (t.sb(n, [P, NC, T], F32R) for n in ("xs_hi", "xs_lo"))
        x1 = t.sb("x1_sb", [P, NT, C])
        g1 = t.sb("g1_sb", [P, NT, C])
        qn = t.sb("qn", [P, NT, 3 * C])
        zq = t.sb("zq1", [P, NT, HG, 3, D1], F32R)
        zk = t.sb("zk1", [P, NT, HG, P], F32R)
        qb = t.sb("qb", [P, NG1, 2, T], F32R)
        kb = t.sb("kb", [P, NG1, HG, T], F32R)
        vs = t.sb("vs", [P, NT, H1, 2 * D1])
        pt = t.sb("pt1", [P, HG, NT, T])
        nm = t.sb("nm", [P, NT, HG])
        sn = t.sb("sn", [P, NT, 4, 2 * D1], F32R)
        ou = t.sb("ou", [P, T])
        inv = t.sb("inv", [P, NT, HG, 1])
        on = t.sb("on", [P, NT, C])
        ot_hi, ot_lo = (t.sb(n, [P, NC, T], F32R) for n in ("ot_hi", "ot_lo"))
        so = t.sb("so1", [P, 2, C])
        ps = t.ps("ps", [P, 2, 512])
        pst = t.ps("pst", [P, 2, 512])
        po = t.ps("po1", [P, 512])
        pn = t.ps("pn", [P, 512])
        w = t.ps("w1a", [P, 2, 512])
        sn_hi_done = t.sem("a_sn_hi_done")
        xs_in = t.sem("a_xs_in")
        xg_in = t.sem("a_xg_in")
        x_stored = t.sem("a_x_stored")
        x_done = t.sem("a_x_done")
        zs_set = t.sem("a_zs_set")
        vs_set = t.sem("a_vs_set")
        proj_done = t.sem("a_proj_done")
        qn_done = t.sem("a_qn_done")
        z_hi_done = t.sem("a_z_hi_done")
        z_lo_done = t.sem("a_z_lo_done")
        z_turned = t.sem("a_z_turned")
        stack_done = t.sem("a_stack_done")
        s_done = t.sem("a_s_done")
        max_done = t.sem("a_max_done")
        sn_done = t.sem("a_sn_done")
        n_turned = t.sem("a_n_turned")
        n_done = t.sem("a_n_done")
        st_done = t.sem("a_st_done")
        exp_done = t.sem("a_exp_done")
        vs_done = t.sem("a_vs_done")
        av_done = t.sem("a_av_done")
        ou_done = t.sem("a_ou_done")
        o_turned = t.sem("a_o_turned")
        inv_done = t.sem("a_inv_done")
        on_done = t.sem("a_on_done")
        on_turned = t.sem("a_on_turned")
        ot_hi_done = t.sem("a_ot_hi_done")
        ot_lo_done = t.sem("a_ot_lo_done")
        out_done = t.sem("a_out_done")
        so_done = t.sem("a_so_done")
        mul_done = t.sem("a_mul_done")

        with nc.Block() as block:
            @block.sync
            def _(sp):
                def load_xs(b):
                    sp.dma_start(xs_hi[:].bitcast(F32), io.xt1_hi[:, :, bass.ds(b * T, T)]).then_inc(xs_in, 16)
                    sp.dma_start(xs_lo[:].bitcast(F32), io.xt1_lo[:, :, bass.ds(b * T, T)]).then_inc(xs_in, 16)

                def load_xg(b):
                    for dst, src in ((x1, io.x1), (g1, io.gate1)):
                        sp.dma_start(dst[:], src[bass.ds(b, 1)].rearrange("o (t p) c -> p (o t) c", p=P)).then_inc(xg_in, 16)

                def store(b):
                    sp.wait_ge(x_done, NT * b + NT)
                    sp.dma_start(io.out[bass.ds(b, 1)].rearrange("o (t p) c -> p (o t) c", p=P), x1[:]).then_inc(x_stored, 16)
                    sp.wait_ge(x_stored, 16 * b + 16)

                load_xs(0)
                load_xg(0)
                with sp.Fori(0, B - 1) as b:
                    sp.wait_ge(proj_done, 2 * NT * b + 2 * NT)
                    load_xs(b + 1)
                    store(b)
                    load_xg(b + 1)
                store(B - 1)

            @block.gpsimd
            def _(pool):
                pool.memset(zk[:].bitcast(F32), 0.0).then_inc(zs_set, 1)
                pool.memset(sn[:].bitcast(F32), 0.0).then_inc(zs_set, 1)
                pool.memset(vs[:], 0.0).then_inc(vs_set, 1)
                pool.wait_ge(vs_set, 1)
                pool.memset(vs[:, :, :, D1:D1 + 1], 1.0).then_inc(vs_set, 1)
                pool.wait_ge(zs_set, 2)
                for h in range(HG):
                    at = 2 * S3 + h % 2
                    pool.memset(zk[:, :, h, at:at + 3:2].bitcast(F32), 1.0).then_inc(zs_set, 1)

                def split_z(b, g):
                    q = NG1 * b + g
                    src = qn[:, :, g * HG * D1:(g + 1) * HG * D1]
                    pool.wait_ge(z_hi_done, 4 * q + 2)
                    pool.tensor_tensor(zq[:, :, :, 1, :], src.rearrange("p t (h d) -> p t h d", d=D1),
                                       zq[:, :, :, 0, :].bitcast(F32), ALU.subtract).then_inc(z_lo_done, 1)
                    pool.wait_ge(z_hi_done, 4 * q + 4)
                    ks = qn[:, :, C + g * HG * D1:C + (g + 1) * HG * D1]
                    for e in range(2):
                        base = e * S3
                        pool.tensor_tensor(zk[:, :, e::2, base + 2 * D1:base + 3 * D1],
                                           ks.rearrange("p t (h e d) -> p t h e d", e=2, d=D1)[:, :, :, e, :],
                                           zk[:, :, e::2, base:base + D1].bitcast(F32), ALU.subtract).then_inc(z_lo_done, 1)

                def finish(b):
                    for i in range(NT):
                        pool.wait_ge(so_done, NT * b + i + 1)
                        if i == 0:
                            pool.wait_ge(xg_in, 32 * b + 32)
                        pool.tensor_tensor(so[:, i % 2, :], so[:, i % 2, :], g1[:, i, :], ALU.mult).then_inc(mul_done, 1)
                        pool.wait_ge(mul_done, NT * b + i + 1)
                        pool.tensor_tensor(x1[:, i, :], x1[:, i, :], so[:, i % 2, :], ALU.add).then_inc(x_done, 1)

                def row(b, first=False, last=False):
                    for g in range(NG1):
                        if g == 1 and not first:
                            finish(b - 1)
                        if g < NG1 - 2:
                            split_z(b, g + 2)
                        elif not last:
                            split_z(b + 1, g + 2 - NG1)

                split_z(0, 0)
                split_z(0, 1)
                row(0, first=True)
                with pool.Fori(1, B - 1) as b:
                    row(b)
                row(B - 1, last=True)
                finish(B - 1)

            @block.tensor
            def _(pe):
                def project(b, i):
                    for j, (at, width) in enumerate(((0, 2 * C), (2 * C, C))):
                        if i > 0:
                            pe.wait_ge(qn_done, 2 * NT * b + 2 * i - 1 + j)
                        for k in range(NC):
                            xh, xl = (a[:, k, i * P:(i + 1) * P] for a in (xs_hi, xs_lo))
                            cols = slice(at, at + width)
                            pe.matmul(w[:, j, 0:width], xh, wq_hi[:, k, cols], start=(k == 0), stop=False)
                            pe.matmul(w[:, j, 0:width], xh, wq_lo[:, k, cols], start=False, stop=False)
                            mm = pe.matmul(w[:, j, 0:width], xl, wq_hi[:, k, cols], start=False, stop=(k == NC - 1))
                        mm.then_inc(proj_done, 1)

                def turn_z(q, j):
                    if j == 0:
                        pe.wait_ge(z_hi_done, 4 * q + 4)
                        pe.wait_ge(z_lo_done, 3 * q + 3)
                    if j > 1:
                        pe.wait_ge(stack_done, 6 * q + j - 1)
                    for i in range(NT):
                        if j < 2:
                            src = zq[:, i, 2 * j:2 * j + 2].rearrange("p h s d -> p (h s d)")
                            mm = pe.transpose(w[0:2 * S3, j % 2, i * P:(i + 1) * P], src.bitcast(F32), c.ident[:])
                        else:
                            mm = pe.transpose(w[:, j % 2, i * P:(i + 1) * P], zk[:, i, j - 2, :].bitcast(F32), c.ident[:])
                    mm.then_inc(z_turned, 1)

                def score(q, g, h, i):
                    if h == 0 and i == 0:
                        pe.wait_ge(stack_done, 6 * q + 6)
                    n = 16 * q + 4 * h + i
                    pe.wait_ge(max_done, n)
                    pe.matmul(ps[:, i % 2, :], qb[0:2 * S3, g, h // 2, i * P:(i + 1) * P], kb[0:2 * S3, g, h, :],
                              start=True, stop=True).then_inc(s_done, 1)

                def score_t(q, g, h, i):
                    if h == 0 and i == 0:
                        pe.wait_ge(n_done, 2 * q + 2)
                    n = 16 * q + 4 * h + i
                    pe.wait_ge(exp_done, n)
                    pe.matmul(pst[:, i % 2, :], kb[:, g, h, i * P:(i + 1) * P], qb[:, g, h // 2, :],
                              start=True, stop=True).then_inc(st_done, 1)

                def weigh(q, g, kt, rows_done):
                    if kt == 0:
                        pe.wait_ge(exp_done, 16 * q + 17)
                        pe.wait_ge(ou_done, q)
                        pe.wait_ge(vs_done, rows_done)
                    for h in range(HG):
                        mm = pe.matmul(po[2 * D1 * h:2 * D1 * (h + 1), :], vs[:, kt, g * HG + h, :], pt[:, h, kt, :],
                                       start=(kt == 0), stop=(kt == NT - 1))
                    if kt == NT - 1:
                        mm.then_inc(av_done, 1)

                def turn_n(q):
                    pe.wait_ge(sn_done, q + 1)
                    pe.wait_ge(on_done, q - 1) if not isinstance(q, int) or q > 0 else None
                    for i in range(NT):
                        mm = pe.transpose(pn[:, i * P:(i + 1) * P], sn[:, i].rearrange("p a b -> p (a b)").bitcast(F32), c.ident[:])
                    mm.then_inc(n_turned, 1)

                def turn_o(q, n_turns):
                    pe.wait_ge(ou_done, q + 1)
                    pe.wait_ge(n_done, 2 * n_turns)
                    for i in range(NT):
                        mm = pe.transpose(pn[:, i * P:(i + 1) * P], ou[:, i * P:(i + 1) * P], c.ident[:])
                    mm.then_inc(o_turned, 1)

                def out_project(b):
                    pe.wait_ge(on_done, NG1 * b + NG1)
                    for k in range(NC):
                        for i in range(NT):
                            mm = pe.transpose(w[:, k, i * P:(i + 1) * P], on[:, i, k * P:(k + 1) * P], c.ident[:])
                        mm.then_inc(on_turned, 1)
                    for i in range(NT):
                        if i < 2:
                            pe.wait_ge(ot_lo_done, NC * b + NC)
                        else:
                            pe.wait_ge(so_done, NT * b + i - 1)
                        for k in range(NC):
                            oh, ol = (a[:, k, i * P:(i + 1) * P] for a in (ot_hi, ot_lo))
                            pe.matmul(w[:, i % 2, 0:C], oh, c.wo1_hi[:, k, :], start=(k == 0), stop=False)
                            pe.matmul(w[:, i % 2, 0:C], oh, c.wo1_lo[:, k, :], start=False, stop=False)
                            mm = pe.matmul(w[:, i % 2, 0:C], ol, c.wo1_hi[:, k, :], start=False, stop=(k == NC - 1))
                        mm.then_inc(out_done, 1)

                def row(b, first=False, last=False):
                    for g in range(NG1):
                        q = NG1 * b + g
                        g1_, g2_ = (g + 1) % NG1, (g + 2) % NG1
                        more1 = not (last and g + 1 == NG1)
                        more2 = not (last and g + 2 >= NG1)
                        before = not (first and g == 0)
                        for i in range(NT):
                            if more1:
                                score(q + 1, g1_, 0, i)
                            if before:
                                weigh(q - 1, (g + 3) % NG1, i, b + 1 if g else b)
                        turn_n(q)
                        if g == 1 and not first:
                            out_project(b - 1)
                        for h in range(1, HG):
                            for i in range(NT):
                                if more1:
                                    score(q + 1, g1_, h, i)
                                score_t(q, g, h - 1, i)
                            if h == 1 and before:
                                turn_o(q - 1, q + 1)
                            if g == 2 and not last:
                                if h == 1:
                                    pe.wait_ge(xs_in, 32 * b + 64)
                                    pe.wait_ge(stack_done, 6 * q + 12)
                                    pe.wait_ge(z_lo_done, 3 * q + 6)
                                    project(b + 1, 0)
                                    project(b + 1, 1)
                                elif h == 2:
                                    project(b + 1, 2)
                                    project(b + 1, 3)
                        if more2:
                            if g == 1 and not first:
                                pe.wait_ge(so_done, NT * b)
                            elif g == 2:
                                pe.wait_ge(qn_done, 2 * NT * b + 4 * NT)
                            else:
                                pe.wait_ge(stack_done, 6 * q + 12)
                        turns = [[0, 1], [2, 3], [4], [5]]
                        for i in range(NT):
                            score_t(q, g, HG - 1, i)
                            if more2:
                                for j in turns[i]:
                                    turn_z(q + 2, j)

                pe.wait_ge(xs_in, 32)
                for i in range(NT):
                    project(0, i)
                pe.wait_ge(qn_done, 2 * NT)
                for j in range(6):
                    turn_z(0, j)
                pe.wait_ge(stack_done, 6)
                for j in range(6):
                    turn_z(1, j)
                for h in range(HG):
                    for i in range(NT):
                        score(0, 0, h, i)
                row(0, first=True)
                with pe.Fori(1, B - 1) as b:
                    row(b)
                row(B - 1, last=True)
                q = NG1 * B - 1
                for i in range(NT):
                    weigh(q, NG1 - 1, i, B)
                pe.wait_ge(on_done, q)
                turn_o(q, q + 1)
                out_project(B - 1)

            @block.vector
            def _(dve):
                def maxima(q, h):
                    if h == 0:
                        dve.wait_ge(sn_done, q)
                    for i in range(NT):
                        dve.wait_ge(s_done, 16 * q + 4 * h + i + 1)
                        dve.tensor_reduce(nm[:, i, h:h + 1], ps[:, i % 2, :], AXX, ALU.max, negate=True).then_inc(max_done, 1)

                def split_n(q):
                    dve.wait_ge(max_done, 16 * q + 17)
                    dve.wait_ge(n_turned, q)
                    v = nm[:].rearrange("p t (a b) -> p t a b", a=2)
                    dve.tensor_copy(sn[:, :, 0:2, 0:2], v).then_inc(sn_hi_done, 1)
                    dve.wait_ge(sn_hi_done, q + 1)
                    dve.tensor_tensor(sn[:, :, 0:2, 2:4], v, sn[:, :, 0:2, 0:2].bitcast(F32), ALU.subtract).then_inc(sn_done, 1)

                def take_n(q, g):
                    dve.wait_ge(n_turned, q + 1)
                    for a in range(2):
                        dve.tensor_copy(qb[2 * S3:P, g, a, :], pn[2 * D1 * a:2 * D1 * (a + 1), :]).then_inc(n_done, 1)

                def take_o(q, g):
                    dve.wait_ge(o_turned, q + 1)
                    v = pn[:].rearrange("p (t h d) -> p t h d", t=NT, h=HG)
                    dve.reciprocal(inv[:], v[:, :, :, D1:D1 + 1]).then_inc(inv_done, 1)
                    dve.wait_ge(inv_done, q + 1)
                    dve.tensor_tensor(on[:, :, g * HG * D1:(g + 1) * HG * D1].rearrange("p t (h d) -> p t h d", h=HG),
                                      v[:, :, :, 0:D1], inv[:].to_broadcast([P, NT, HG, D1]), ALU.mult).then_inc(on_done, 1)

                def take_proj(b, i):
                    for j, (at, width) in enumerate(((0, 2 * C), (2 * C, C))):
                        dve.wait_ge(proj_done, 2 * NT * b + 2 * i + j + 1)
                        dve.tensor_tensor(qn[:, i, at:at + width], w[:, j, 0:width], c.bqkv1[:, at:at + width],
                                          ALU.add).then_inc(qn_done, 1)

                def finish(b):
                    for k in range(NC):
                        dve.wait_ge(ot_hi_done, NC * b + k + 1)
                        dve.tensor_tensor(ot_lo[:, k, :], w[:, k, :], ot_hi[:, k, :].bitcast(F32), ALU.subtract).then_inc(ot_lo_done, 1)
                    for i in range(NT):
                        dve.wait_ge(out_done, NT * b + i + 1)
                        if i > 1:
                            dve.wait_ge(x_done, NT * b + i - 1)
                        dve.tensor_tensor(so[:, i % 2, :], w[:, i % 2, 0:C], c.bo1[:], ALU.add).then_inc(so_done, 1)

                def row(b, first=False, last=False):
                    for g in range(NG1):
                        q = NG1 * b + g
                        more1 = not (last and g + 1 == NG1)
                        before = not (first and g == 0)
                        if more1:
                            maxima(q + 1, 0)
                        take_n(q, g)
                        if g == 1 and not first:
                            finish(b - 1)
                        for h in range(1, HG):
                            if more1:
                                maxima(q + 1, h)
                            if h == 1 and before:
                                take_o(q - 1, (g + 3) % NG1)
                            if g == 2 and not last:
                                if h == 1:
                                    dve.wait_ge(vs_done, b + 1)
                                    take_proj(b + 1, 0)
                                    take_proj(b + 1, 1)
                                elif h == 2:
                                    take_proj(b + 1, 2)
                                    take_proj(b + 1, 3)
                        if more1:
                            split_n(q + 1)

                dve.memset(inv[:], 0.0).then_inc(max_done, 1)
                for i in range(NT):
                    take_proj(0, i)
                dve.wait_ge(zs_set, 2)
                for h in range(HG):
                    maxima(0, h)
                split_n(0)
                row(0, first=True)
                with dve.Fori(1, B - 1) as b:
                    row(b)
                row(B - 1, last=True)
                take_o(NG1 * B - 1, NG1 - 1)
                finish(B - 1)

            @block.scalar
            def _(act):
                def exps(q, h, i):
                    act.wait_ge(st_done, 16 * q + 4 * h + i + 1)
                    act.activation(pt[:, h, i, :], pst[:, i % 2, :], ACT.Exp).then_inc(exp_done, 1)

                def split_z(b, g):
                    q = NG1 * b + g
                    if g == 0:
                        act.wait_ge(qn_done, 2 * NT * b + 2 * NT)
                    act.wait_ge(z_turned, 6 * q)
                    qs = qn[:, :, g * HG * D1:(g + 1) * HG * D1].rearrange("p t (h d) -> p t h d", d=D1)
                    for j in (0, 2):
                        act.copy(zq[:, :, :, j, :], qs).then_inc(z_hi_done, 1)
                    ks = qn[:, :, C + g * HG * D1:C + (g + 1) * HG * D1].rearrange("p t (h e d) -> p t h e d", e=2, d=D1)
                    for e in range(2):
                        dst = zk[:, :, e::2, e * S3:e * S3 + 2 * D1]
                        for j in range(2):
                            last = act.copy(dst[:, :, :, j * D1:(j + 1) * D1], ks[:, :, :, e, :])
                        last.then_inc(z_hi_done, 1)

                def take_stack(q, g, j):
                    act.wait_ge(z_turned, 6 * q + j + 1)
                    if j < 2:
                        act.copy(qb[0:2 * S3, g, j, :], w[0:2 * S3, j % 2, :]).then_inc(stack_done, 1)
                    else:
                        act.copy(kb[:, g, j - 2, :], w[:, j % 2, :]).then_inc(stack_done, 1)

                def take_o(q):
                    act.wait_ge(av_done, q + 1)
                    act.wait_ge(o_turned, q)
                    act.copy(ou[:], po[:]).then_inc(ou_done, 1)

                def pass_v(b):
                    act.wait_ge(qn_done, 2 * NT * b + 2 * NT)
                    act.copy(vs[:, :, :, 0:D1], qn[:, :, 2 * C:].rearrange("p t (h d) -> p t h d", d=D1)).then_inc(vs_done, 1)

                def row(b, first=False, last=False):
                    turns = [[0, 1], [2, 3], [4], [5]]
                    for g in range(NG1):
                        q = NG1 * b + g
                        more2 = not (last and g + 2 >= NG1)
                        if not (first and g == 0):
                            take_o(q - 1)
                            if g == 0:
                                pass_v(b)
                        if g == 1 and not first:
                            for k in range(NC):
                                act.wait_ge(on_turned, NC * (b - 1) + k + 1)
                                act.copy(ot_hi[:, k, :], w[:, k, :]).then_inc(ot_hi_done, 1)
                        for h in range(HG - 1):
                            for i in range(NT):
                                exps(q, h, i)
                        if more2:
                            split_z(b + (g + 2) // NG1, (g + 2) % NG1)
                        for i in range(NT):
                            exps(q, HG - 1, i)
                            if more2:
                                for j in turns[i]:
                                    take_stack(q + 2, (g + 2) % NG1, j)

                act.wait_ge(zs_set, 2 + HG)
                act.wait_ge(vs_set, 2)
                act.copy(ou[:, 0:1], c.ident[:, 0:1]).then_inc(exp_done, 1)
                for g in range(2):
                    split_z(0, g)
                    for j in range(6):
                        take_stack(g, g, j)
                pass_v(0)
                row(0, first=True)
                with act.Fori(1, B - 1) as b:
                    row(b)
                row(B - 1, last=True)
                take_o(NG1 * B - 1)
                for k in range(NC):
                    act.wait_ge(on_turned, NC * (B - 1) + k + 1)
                    act.copy(ot_hi[:, k, :], w[:, k, :]).then_inc(ot_hi_done, 1)


def program(nc, io):
    with ExitStack() as ctx:
        m, c = Mem(nc, ctx), Names()
        setup_constants(nc, m, c)
        with ExitStack() as inner:
            m0 = Mem(nc, inner)
            load_layer0(nc, m0, c, io)
            layer0(nc, m0, c, io)
        with ExitStack() as inner:
            m1 = Mem(nc, inner)
            c.xt1_hi, c.xt1_lo = (m1.sb(n, [P, NC, B * T], F32R) for n in ("xt1_hi", "xt1_lo"))
            norm_transpose1(nc, c, io)
            experts(nc, c, io)
        with ExitStack() as inner:
            load_layer1(nc, Mem(nc, inner), c, io)
            attention1(nc, c, io)


def kernel(**inputs):
    import concourse.bacc as bacc
    from concourse.bass_utils import run_bass_kernel_spmd

    a = {k: np.asarray(v) for k, v in inputs.items()}
    wq, wk = (a[n].reshape(C, NP0, 2, D0 // 2, 2).transpose(0, 1, 2, 4, 3).reshape(C, NP0, 2 * D0)
              for n in ("L0_attn_Wq", "L0_attn_Wk"))
    wv = a["L0_attn_Wv"].reshape(C, NP0, 2 * D0)
    arrays = {
        "x": a["L0_attn_x"],
        "wqkv0": np.concatenate([wq, wk, wv], 2).reshape(C, NP0 * PC0),
        "wo0": a["L0_attn_Wo"],
        "bo0": a["L0_attn_bo"],
        "wg0": a["L0_ffn_w_gate"].T,
        "wu0": a["L0_ffn_w_up"].T,
        "wd0": a["L0_ffn_w_down"].T,
        "rope": rope_tables(),
        "wqkv1": np.concatenate([a["L1_attn_wq"].T, a["L1_attn_wk"].T, a["L1_attn_wv"].T], 1),
        "bqkv1": np.concatenate([a["L1_attn_bq"], a["L1_attn_bk_"], a["L1_attn_bv"]]),
        "wo1": a["L1_attn_wo"].T,
        "bo1": a["L1_attn_bo"],
        "w1": a["L1_ffn_w1"],
        "w3": a["L1_ffn_w3"],
        "w2": a["L1_ffn_w2"],
    }
    nc = bacc.Bacc("TRN2", target_bir_lowering=False, num_devices=1)
    io = Names()
    arrays = {"in_" + k: np.ascontiguousarray(v) for k, v in arrays.items()}
    aps = {k: nc.dram_tensor(k, v.shape, mybir.dt.from_np(v.dtype), kind="ExternalInput").ap() for k, v in arrays.items()}
    (io.x, io.wqkv0, io.wo0, io.bo0, io.wg0, io.wu0, io.wd0, io.rope, io.wqkv1, io.bqkv1, io.wo1, io.bo1,
     io.w1, io.w3, io.w2) = aps.values()
    io.x1 = nc.dram_tensor("x1_scratch", (B, T, C), F32, kind="Internal").ap()
    io.gate1 = nc.dram_tensor("gate1_scratch", (B, T, C), F32, kind="Internal").ap()
    io.xt1_hi = nc.dram_tensor("xt1_hi_scratch", (P, NC, B * T), F32, kind="Internal").ap()
    io.xt1_lo = nc.dram_tensor("xt1_lo_scratch", (P, NC, B * T), F32, kind="Internal").ap()
    io.out = nc.dram_tensor("out_dram", (B, T, C), F32, kind="ExternalOutput").ap()
    program(nc, io)
    r = run_bass_kernel_spmd(nc, [arrays], core_ids=[0])
    return r.results[0]["out_dram"]
```

```python
from contextlib import ExitStack

import numpy as np

import concourse.bass as bass
from concourse import mybir
from concourse.alu_op_type import AluOpType as ALU

ACT = mybir.ActivationFunctionType
AXX = mybir.AxisListType.X
F32 = mybir.dt.float32
F32R = mybir.dt.float32r
BF16 = mybir.dt.bfloat16
I32 = mybir.dt.int32

P = 128
B, T, C = 8, 512, 256
NT = T // P
NC = C // P
EPS = 1e-5

H0, D0 = 16, 64
NP0 = H0 // 2
PC0 = 6 * D0
F0 = 768
NF0 = F0 // P
DEQ = 1.0 / 127.0

H1, D1 = 16, 16
NG1 = 4
E1, F1 = 8, 704
NF1 = (F1 + P - 1) // P
FP1 = NF1 * P
FR1 = F1 - (NF1 - 1) * P
CE = T // E1

SOFF = [0, 128, 384, 768]
PTOFF = [0, 512, 1024, 896]
NEG = -1.0e30


def rope_tables():
    inv = (np.float32(1.0) / np.float32(10000.0) ** (np.arange(0, D0, 2, dtype=np.float32) / np.float32(D0))).astype(np.float32)
    ang = (np.arange(T, dtype=np.float32)[:, None] * inv[None, :]).astype(np.float32).astype(np.float64)
    t = np.stack([np.cos(ang), np.sin(ang), -np.sin(ang)], 1).astype(np.float32)
    return np.ascontiguousarray(t.reshape(NT, P, 3, D0 // 2).transpose(1, 0, 2, 3))


class Names:
    pass


class Mem:

    def __init__(self, nc, ctx):
        self.nc, self.ctx = nc, ctx

    def sb(self, name, shape, dt=F32):
        return self.ctx.enter_context(self.nc.sbuf_tensor(name, shape, dt))

    def ps(self, name, shape, dt=F32):
        return self.ctx.enter_context(self.nc.psum_tensor(name, shape, dt))

    def sem(self, name):
        return self.ctx.enter_context(self.nc.semaphore(name))


def setup_constants(nc, m, c):
    c.ident = m.sb("ident", [P, P])
    c.identb = m.sb("identb", [P, P], BF16)
    c.maskb = m.sb("maskb", [P, P], BF16)
    set_done = m.sem("set_done")
    with nc.Block() as block:
        @block.gpsimd
        def _(pool):
            pool.memset(c.ident[:], 0.0).then_inc(set_done, 1)
            pool.memset(c.identb[:], 0.0).then_inc(set_done, 1)
            pool.memset(c.maskb[:], 0.0).then_inc(set_done, 1)
            pool.wait_ge(set_done, 3)
            for eye in (c.ident, c.identb):
                pool.affine_select(out=eye[:], in_=eye[:], compare_op=ALU.not_equal, fill=1.0, base=0,
                                   pattern=[[-1, P]], channel_multiplier=1).then_inc(set_done, 1)
            pool.affine_select(out=c.maskb[:], in_=c.maskb[:], compare_op=ALU.is_ge, fill=NEG, base=0,
                               pattern=[[-1, P]], channel_multiplier=1).then_inc(set_done, 1)
            pool.wait_ge(set_done, 6)


def load_layer0(nc, m, c, io):
    c.wq_hi = m.sb("wq_hi", [P, NC, NP0 * PC0], F32R)
    c.wq_lo = m.sb("wq_lo", [P, NC, NP0 * PC0], F32R)
    c.wo_hi = m.sb("wo_hi", [P, NP0, C], F32R)
    c.wo_lo = m.sb("wo_lo", [P, NP0, C], F32R)
    c.wg = m.sb("wg", [P, NC, F0], F32R)
    c.wu = m.sb("wu", [P, NC, F0], F32R)
    c.wd = m.sb("wd", [P, NF0, C], F32R)
    c.mean = m.sb("mean", [P, B * NT])
    c.rstd = m.sb("rstd", [P, B * NT])
    c.rope = m.sb("rope", [P, NT, 3, D0 // 2])
    c.bo = m.sb("bo", [P, C])
    with ExitStack() as ctx:
        t = Mem(nc, ctx)
        xa = t.sb("xa", [P, B * NT, C])
        wq_raw = t.sb("wq_raw", [P, NC, NP0 * PC0])
        wo_raw = t.sb("wo_raw", [P, NP0, C])
        wg_int, wu_int, wd_int = (t.sb(n, [P, NC * F0], I32) for n in ("wg_int", "wu_int", "wd_int"))
        stats = t.sb("stats", [P, B * NT, 6])
        aggr = t.sb("aggr", [P, B * NT, 2])
        dev = t.sb("dev", [P, B * NT])
        eps = t.sb("eps", [P, 1])
        x_in = [t.sem(f"x_in{i}") for i in range(2)]
        wq_in = [t.sem(f"wq_in{i}") for i in range(NC)]
        wg_in = t.sem("wg_in")
        wu_in = t.sem("wu_in")
        wd_in = t.sem("wd_in")
        wo_in = t.sem("wo_in")
        small_in = t.sem("small_in")
        int_cast = t.sem("int_cast")
        stats_done = t.sem("stats_done")
        aggr_done = t.sem("aggr_done")
        eps_set = t.sem("eps_set")
        dev_done = t.sem("dev_done")
        rstd_done = t.sem("rstd_done")
        hi_done = t.sem("hi_done")
        lo_done = t.sem("lo_done")

        def flat(w):
            return w[:].rearrange("p c n -> p (c n)")

        with nc.Block() as block:
            @block.sync
            def _(sp):
                xt = io.x.rearrange("b (t p) c -> p (b t) c", p=P)
                wq = io.wqkv0.rearrange("(c p) n -> p c n", p=P)
                half = B * NT // 2
                for i in range(2):
                    sp.dma_start(wq_raw[:, i, :], wq[:, i, :]).then_inc(wq_in[i], 16)
                    sp.dma_start(xa[:, i * half:(i + 1) * half, :], xt[:, i * half:(i + 1) * half, :]).then_inc(x_in[i], 16)
                sp.dma_start(wo_raw[:], io.wo0.rearrange("(c p) n -> p c n", p=P)).then_inc(wo_in, 16)
                for dst, src, n, done in ((wg_int, io.wg0, NC, wg_in), (wu_int, io.wu0, NC, wu_in), (wd_int, io.wd0, NF0, wd_in)):
                    sp.dma_start(dst[:].rearrange("p (c n) -> p c n", c=n), src.rearrange("(c p) n -> p c n", p=P)).then_inc(done, 16)
                sp.dma_start(c.rope[:], io.rope).then_inc(small_in, 16)
                sp.dma_start(c.bo[:], io.bo0.partition_broadcast(P)).then_inc(small_in, 16)
                sp.wait_ge(small_in, 32)

            @block.scalar
            def _(act):
                for i in range(NC):
                    act.wait_ge(wq_in[i], 16)
                    v = wq_raw[:, i, :].rearrange("p (h n) -> p h n", n=PC0)
                    o = c.wq_hi[:, i, :].rearrange("p (h n) -> p h n", n=PC0)
                    act.mul(o[:, :, 0:2 * D0], v[:, :, 0:2 * D0], 1.0 / 8.0).then_inc(hi_done, 1)
                    act.copy(o[:, :, 2 * D0:], v[:, :, 2 * D0:]).then_inc(hi_done, 1)
                act.wait_ge(wo_in, 16)
                act.copy(c.wo_hi[:], wo_raw[:]).then_inc(hi_done, 1)
                act.wait_ge(wg_in, 16)
                act.copy(flat(c.wg), wg_int[:]).then_inc(int_cast, 1)
                act.wait_ge(wu_in, 16)
                act.copy(flat(c.wu), wu_int[:]).then_inc(int_cast, 1)
                act.wait_ge(aggr_done, B * NT)
                act.wait_ge(eps_set, 1)
                act.activation(dev[:], aggr[:, :, 1], ACT.Sqrt, bias=eps[:]).then_inc(dev_done, 1)
                act.wait_ge(wd_in, 16)
                act.copy(flat(c.wd), wd_int[:]).then_inc(int_cast, 1)
                act.wait_ge(int_cast, 3)

            @block.vector
            def _(dve):
                dve.memset(eps[:], EPS).then_inc(eps_set, 1)
                for half in range(2):
                    i = half
                    dve.wait_ge(hi_done, 2 * i + 2)
                    v = wq_raw[:, i, :].rearrange("p (h n) -> p h n", n=PC0)
                    h = c.wq_hi[:, i, :].bitcast(F32).rearrange("p (h n) -> p h n", n=PC0)
                    o = c.wq_lo[:, i, :].rearrange("p (h n) -> p h n", n=PC0)
                    dve.scalar_tensor_tensor(out=o[:, :, 0:2 * D0], in0=v[:, :, 0:2 * D0], scalar=1.0 / 8.0,
                                             in1=h[:, :, 0:2 * D0], op0=ALU.mult, op1=ALU.subtract).then_inc(lo_done, 1)
                    dve.tensor_tensor(o[:, :, 2 * D0:], v[:, :, 2 * D0:], h[:, :, 2 * D0:], ALU.subtract).then_inc(lo_done, 1)
                    dve.wait_ge(x_in[half], 16)
                    for i in range(B * NT // 2 * half, B * NT // 2 * (half + 1)):
                        dve.bn_stats(stats[:, i, :], xa[:, i, :]).then_inc(stats_done, 1)
                for i in range(B * NT):
                    dve.wait_ge(stats_done, i + 1)
                    dve.bn_aggr(aggr[:, i, :], stats[:, i, :]).then_inc(aggr_done, 1)
                dve.wait_ge(aggr_done, B * NT)
                dve.tensor_copy(c.mean[:], aggr[:, :, 0]).then_inc(rstd_done, 1)
                dve.wait_ge(hi_done, 2 * NC + 1)
                dve.tensor_tensor(c.wo_lo[:], wo_raw[:], c.wo_hi[:].bitcast(F32), ALU.subtract).then_inc(lo_done, 1)
                dve.wait_ge(dev_done, 1)
                dve.reciprocal(c.rstd[:], dev[:]).then_inc(rstd_done, 1)
                dve.wait_ge(rstd_done, 2)
                dve.wait_ge(lo_done, 2 * NC + 1)


def layer0(nc, m, c, io):
    with ExitStack() as ctx:
        t = Mem(nc, ctx)
        x = t.sb("x", [P, 2 * NT, C])
        xn = t.sb("xn", [P, NT, C])
        xt_hi = t.sb("xt_hi", [P, NC, T], F32R)
        xt_lo = t.sb("xt_lo", [P, NC, T], F32R)
        ho_hi = t.sb("ho_hi", [P, NP0, T], F32R)
        ho_lo = t.sb("ho_lo", [P, NP0, T], F32R)
        gate = t.sb("gate", [P, NT, C])
        ra = t.sb("ra", [P, 2, 4 * D0])
        rb = t.sb("rb", [P, 2, 4 * D0])
        qk = t.sb("qk", [P, NT, 4 * D0])
        zq = t.sb("zq", [P, NT, 2, 2 * D0], F32R)
        zk = t.sb("zk", [P, NT, 2, 3 * D0], F32R)
        qs = t.sb("qs", [P, 2, T], F32R)
        k1 = t.sb("k1", [P, 2, T], F32R)
        k2 = t.sb("k2", [P, 2, T], F32R)
        pr = t.sb("pr", [P, 2, 1280])
        sg, hid = (pr[:, h, 0:2 * T].rearrange("p (s t) -> p s t", s=2) for h in range(2))
        pt = t.sb("pt", [P, 2, 1280])
        v_ring = t.sb("v_ring", [P, 4 * NT, 2 * D0])
        v_cur = t.sb("v_cur", [P, NT, 2 * D0])
        nmax = t.sb("nmax", [P, 2, NT])
        rsum = t.sb("rsum", [P, 2, NT])
        rinv = t.sb("rinv", [P, 2, NT])
        so = t.sb("so", [P, 2, C])
        sc = t.ps("sc", [P, 3, 512])
        po = t.ps("po", [P, 512])
        w = t.ps("w", [P, 4, 512])
        x_loaded = t.sem("x_loaded")
        x1_stored = t.sem("x1_stored")
        x1_ready = t.sem("x1_ready")
        xn_ready = t.sem("xn_ready")
        xn_turned = t.sem("xn_turned")
        xt_hi_done = t.sem("xt_hi_done")
        xt_lo_done = t.sem("xt_lo_done")
        gate_up_done = t.sem("gate_up_done")
        silu_done = t.sem("silu_done")
        hid_done = t.sem("hid_done")
        hid_hi_done = t.sem("hid_hi_done")
        hid_lo_done = t.sem("hid_lo_done")
        down_done = t.sem("down_done")
        g_done = t.sem("g_done")
        proj_done = t.sem("proj_done")
        v_done = t.sem("v_done")
        v_cur_done = t.sem("v_cur_done")
        rope_mult = t.sem("rope_mult")
        rope_done = t.sem("rope_done")
        z_hi_done = t.sem("z_hi_done")
        z_lo_done = t.sem("z_lo_done")
        z_turned = t.sem("z_turned")
        stack_act = t.sem("stack_act")
        stack_dve = t.sem("stack_dve")
        s_done = t.sem("s_done")
        max_done = t.sem("max_done")
        exp_done = t.sem("exp_done")
        rinv_done = t.sem("rinv_done")
        inverse_seen = t.sem("inverse_seen")
        scaled = t.sem("scaled")
        p_turned = t.sem("p_turned")
        pt_a_copied = t.sem("pt_a_copied")
        pt_b_copied = t.sem("pt_b_copied")
        av_done = t.sem("av_done")
        o_hi_done = t.sem("o_hi_done")
        o_lo_done = t.sem("o_lo_done")
        wo_done = t.sem("wo_done")
        so_done = t.sem("so_done")
        mul_done = t.sem("mul_done")
        stats1_done = t.sem("stats1_done")

        SLOT = (3, 0, 3, 0)
        FOUR = (3, 0, 1, 2)

        def score(i):
            return (0, 256 * i) if i < 2 else (i - 1, 0)

        x_dram = io.x.rearrange("b (t p) c -> p b t c", p=P)
        x1_dram = io.x1.rearrange("b (t p) c -> p b t c", p=P)

        with nc.Block() as block:
            @block.sync
            def _(sp):
                sp.dma_start(x[:, 0:NT, :], x_dram[:, 0]).then_inc(x_loaded, 16)
                with sp.Fori(0, B - 1) as b:
                    sp.wait_ge(x_loaded, 16 * b + 16)
                    sp.wait_ge(x1_stored, 16 * b + 16)
                    sp.wait_ge(stats1_done, NT * b + NT)
                    sp.dma_start(x[:, bass.ds((b + 1) % 2 * NT, NT), :], x_dram[:, bass.ds(b + 1, 1)].rearrange("p o t c -> p (o t) c")).then_inc(x_loaded, 16)
                    sp.wait_ge(x1_ready, NT * b + NT)
                    sp.dma_start(x1_dram[:, bass.ds(b, 1)].rearrange("p o t c -> p (o t) c"), x[:, bass.ds(b % 2 * NT, NT), :]).then_inc(x1_stored, 16)
                sp.wait_ge(x1_ready, NT * B)
                sp.wait_ge(x1_stored, 16 * B)
                sp.dma_start(x1_dram[:, B - 1], x[:, (B - 1) % 2 * NT:(B - 1) % 2 * NT + NT, :]).then_inc(x1_stored, 16)
                sp.wait_ge(x1_stored, 16 * B + 16)

            @block.tensor
            def _(pe):
                def turn_x(b, k):
                    for i in range(NT):
                        pe.wait_ge(xn_ready, NT * b + i + 1)
                        mm = pe.transpose(w[:, SLOT[k], i * P:(i + 1) * P], xn[:, i, k * P:(k + 1) * P], c.ident[:])
                    mm.then_inc(xn_turned, 1)

                def gate_up(b):
                    for f in range(NF0):
                        for j, wt in enumerate((c.wg, c.wu)):
                            bank = (3 + 2 * f + j) % 4
                            if f < 2:
                                pe.wait_ge(so_done, NT * b + 2 * f + j + 1)
                                if f == 0:
                                    pe.wait_ge(rope_mult, NT * NP0 * b + 3 + j)
                            elif j == 0:
                                pe.wait_ge(silu_done, NF0 * b + f - 1)
                            else:
                                pe.wait_ge(hid_done, NF0 * b + f - 1)
                            for k in range(NC):
                                for q, xt in enumerate((xt_hi, xt_lo)):
                                    mm = pe.matmul(w[:, bank, :], wt[:, k, f * P:(f + 1) * P], xt[:, k, :],
                                                   start=(k == 0 and q == 0), stop=(k == NC - 1 and q == 1))
                            mm.then_inc(gate_up_done, 1)

                def down(b):
                    for i in range(NT):
                        pe.wait_ge(rope_mult, NT * (NP0 * b + 1) + i + 1)
                        for f in range(NF0):
                            if i == 0:
                                pe.wait_ge(hid_hi_done, NF0 * b + f + 1)
                                pe.wait_ge(hid_lo_done, NF0 * b + f + 1)
                            for q, hh in enumerate((ho_hi, ho_lo)):
                                mm = pe.matmul(w[:, FOUR[i], 0:C], hh[:, f, i * P:(i + 1) * P], c.wd[:, f, :],
                                               start=(f == 0 and q == 0), stop=(f == NF0 - 1 and q == 1))
                        mm.then_inc(down_done, 1)

                def project(hp, i, bank):
                    cols = bass.ds(hp * PC0, PC0)
                    for k in range(NC):
                        xh, xl = (a[:, k, i * P:(i + 1) * P] for a in (xt_hi, xt_lo))
                        pe.matmul(w[:, bank, 0:PC0], xh, c.wq_hi[:, k, cols], start=(k == 0), stop=False)
                        pe.matmul(w[:, bank, 0:PC0], xh, c.wq_lo[:, k, cols], start=False, stop=False)
                        mm = pe.matmul(w[:, bank, 0:PC0], xl, c.wq_hi[:, k, cols], start=False, stop=(k == NC - 1))
                    mm.then_inc(proj_done, 1)

                def turn_z(n, j):
                    if j == 0:
                        pe.wait_ge(z_hi_done, 4 * n + 4)
                        pe.wait_ge(z_lo_done, 4 * n + 4)
                    if j > 3:
                        pe.wait_ge(stack_act, 4 * n + j - 3)
                    h, kind = j // 3, j % 3
                    for i in range(NT):
                        src = zk[:, i, h, (kind - 1) * D0:(kind + 1) * D0] if kind else zq[:, i, h, :]
                        mm = pe.transpose(w[:, (1 + j) % 4, i * P:(i + 1) * P], src.bitcast(F32), c.ident[:])
                    mm.then_inc(z_turned, 1)

                def scores(n, h):
                    pe.wait_ge(stack_act, 4 * n + (3 if h == 0 else 4))
                    if h == 1:
                        pe.wait_ge(stack_dve, 2 * n + 2)
                    for i in range(NT):
                        bank, at = score(i)
                        pe.wait_ge(exp_done, 8 * n + 4 * h + (2, 2, 3, 4)[i])
                        width = max(256, (i + 1) * P)
                        q = qs[:, h, i * P:(i + 1) * P]
                        out = sc[:, bank, at:at + width]
                        pe.matmul(out, q, k1[:, h, 0:width], start=True, stop=False)
                        pe.matmul(out, q, k2[:, h, 0:width], start=False, stop=False)
                        pe.matmul(sc[:, bank, at + i * P:at + (i + 1) * P], c.identb[:], c.maskb[:],
                                  start=False, stop=True).then_inc(s_done, 1)

                def turn_p(n, h, j):
                    if j == 0:
                        pe.wait_ge(scaled, 8 * n + 4 * h + 4)
                    tile = ([(0, i, i * P) for i in range(4)],
                            [(1, i, (i - 1) * P) for i in range(1, 4)] + [(3, 3, 3 * P)],
                            [(2, i, (i - 2) * P) for i in range(2, 4)])[j]
                    for kt, i, at in tile:
                        mm = pe.transpose(w[:, 1 - h + j, at:at + P],
                                          pr[:, h, SOFF[i] + kt * P:SOFF[i] + (kt + 1) * P], c.ident[:])
                    mm.then_inc(p_turned, 1)

                def weigh(n):
                    pe.wait_ge(pt_a_copied, 3 * n + 3)
                    pe.wait_ge(pt_b_copied, 3 * n + 3)
                    pe.wait_ge(v_cur_done, n + 1)
                    pe.wait_ge(o_lo_done, n + 1)
                    for kt in range(NT):
                        for h in range(2):
                            mm = pe.matmul(po[h * D0:(h + 1) * D0, kt * P:T], v_cur[:, kt, h * D0:(h + 1) * D0],
                                           pt[:, h, PTOFF[kt]:PTOFF[kt] + T - kt * P], start=(kt == 0), stop=(kt == NT - 1))
                    mm.then_inc(av_done, 1)

                def pair(b, hp, slot="project", turn=True, first=False):
                    n = b * NP0 + hp
                    scores(n, 0)
                    if not first:
                        if slot == "project" or slot == "turn_x" or (slot is None and turn):
                            pe.wait_ge(rope_mult, NT * (n + 1) + 4)
                        elif slot == "next_row":
                            pe.wait_ge(xt_lo_done, NC * (b + 1) + 2)
                        else:
                            pe.wait_ge(stack_act, 4 * n + 4)
                        turn_p(n - 1, 1, 0)
                        for j in (1, 2):
                            pe.wait_ge(pt_a_copied, 3 * n - 3 + j)
                            turn_p(n - 1, 1, j)
                    for i in range(2):
                        if slot is None:
                            continue
                        if first:
                            pe.wait_ge(g_done, NT * b + i + 1)
                        elif i == 0:
                            pe.wait_ge(pt_a_copied, 3 * n)
                        else:
                            pe.wait_ge(pt_b_copied, 3 * n - 2)
                        if slot == "project":
                            project(hp + 2, i, SLOT[i])
                        elif slot == "turn_x":
                            turn_x(b + 1, i)
                        else:
                            project(0, i, SLOT[i])
                    scores(n, 1)
                    if turn:
                        for j in range(6):
                            if j < 2:
                                if first:
                                    pe.wait_ge(g_done, NT * b + j + 3)
                                else:
                                    pe.wait_ge(pt_b_copied, 3 * n - 1 + j)
                            elif j < 4:
                                if slot == "project":
                                    pe.wait_ge(rope_mult, NT * (n + 2) + j - 1)
                                elif slot == "turn_x":
                                    pe.wait_ge(xt_lo_done, NC * (b + 1) + j - 1)
                                elif j == 2:
                                    pe.wait_ge(pt_a_copied, 3 * n)
                                else:
                                    pe.wait_ge(pt_b_copied, 3 * n - 2)
                            turn_z(n + 1, j)
                    if not first:
                        weigh(n - 1)
                    for i in range(2, NT):
                        if slot == "project":
                            pe.wait_ge(stack_act, 4 * (n + 1) + i + 1)
                            project(hp + 2, i, SLOT[i])
                        elif slot == "next_row":
                            pe.wait_ge(rope_mult, NT * (n + 1) + i - 1)
                            project(0, i, SLOT[i])
                    for j in range(3):
                        if j < 2:
                            if turn:
                                pe.wait_ge(stack_dve, 2 * (n + 1) + j + 1)
                            else:
                                pe.wait_ge(pt_b_copied, 3 * n - 1 + j)
                        elif slot == "project":
                            pe.wait_ge(rope_mult, NT * (n + 2) + 3)
                        elif slot == "next_row":
                            pe.wait_ge(rope_mult, NT * (n + 1) + 3)
                        elif turn:
                            pe.wait_ge(stack_act, 4 * (n + 1) + 3)
                        else:
                            pe.wait_ge(pt_a_copied, 3 * n)
                        turn_p(n, 0, j)

                def out_project(b):
                    n = b * NP0 + NP0
                    pe.wait_ge(pt_a_copied, 3 * n)
                    pe.wait_ge(o_lo_done, n + 1)
                    for i in range(NT):
                        for k in range(NP0):
                            oh, ol = (a[:, k, i * P:(i + 1) * P] for a in (ho_hi, ho_lo))
                            pe.matmul(w[:, FOUR[i], 0:C], oh, c.wo_hi[:, k, :], start=(k == 0), stop=False)
                            pe.matmul(w[:, FOUR[i], 0:C], oh, c.wo_lo[:, k, :], start=False, stop=False)
                            mm = pe.matmul(w[:, FOUR[i], 0:C], ol, c.wo_hi[:, k, :], start=False, stop=(k == NP0 - 1))
                        mm.then_inc(wo_done, 1)

                def row(b, last=False):
                    gate_up(b)
                    n = b * NP0
                    for j in range(6):
                        if j in (0, 2):
                            pe.wait_ge(silu_done, NF0 * b + (6 if j == 0 else 5))
                        elif j in (1, 3):
                            pe.wait_ge(hid_done, NF0 * b + (6 if j == 1 else 5))
                        turn_z(n, j)
                    for i in range(NT):
                        if i < 2:
                            pe.wait_ge(stack_act, 4 * n + 3 + i)
                        else:
                            pe.wait_ge(stack_dve, 2 * n - 1 + i)
                        project(1, i, FOUR[i])
                    down(b)
                    pair(b, 0, first=True)
                    with pe.Fori(1, NP0 - 2) as hp:
                        pair(b, hp)
                    pair(b, NP0 - 2, slot=None if last else "turn_x")
                    if not last:
                        pe.wait_ge(xt_hi_done, NC * (b + 2))
                        pe.wait_ge(xt_lo_done, NC * (b + 2))
                    pair(b, NP0 - 1, slot=None if last else "next_row", turn=False)
                    n = b * NP0 + NP0 - 1
                    if last:
                        pe.wait_ge(pt_b_copied, 3 * n - 2)
                    else:
                        pe.wait_ge(rope_mult, NT * (n + 1) + 4)
                    turn_p(n, 1, 0)
                    for j in (1, 2):
                        pe.wait_ge(pt_a_copied, 3 * n + j)
                        turn_p(n, 1, j)
                    weigh(n)
                    out_project(b)

                for k in range(NC):
                    turn_x(0, k)
                pe.wait_ge(xt_hi_done, NC)
                pe.wait_ge(xt_lo_done, NC)
                for i in range(NT):
                    if i > 1:
                        pe.wait_ge(rope_mult, i - 1)
                    project(0, i, SLOT[i])
                with pe.Fori(0, B - 1) as b:
                    row(b)
                row(B - 1, last=True)

            @block.scalar
            def _(act):
                def exps(n, h):
                    for i in range(NT):
                        act.wait_ge(max_done, 8 * n + 4 * h + (2, 2, 3, 4)[i])
                        bank, at = score(i)
                        act.activation(pr[:, h, SOFF[i]:SOFF[i] + (i + 1) * P], sc[:, bank, at:at + (i + 1) * P], ACT.Exp,
                                       bias=nmax[:, h, i:i + 1], accum_out=rsum[:, h, i:i + 1]).then_inc(exp_done, 1)

                def turn_x(b):
                    for k in range(NC):
                        act.wait_ge(xn_turned, NC * b + k + 1)
                        act.copy(xt_hi[:, k, :], w[:, SLOT[k], :]).then_inc(xt_hi_done, 1)

                def take_v(n, hp, i, bank):
                    act.wait_ge(proj_done, NT * n + i + 1)
                    act.copy(v_ring[:, bass.ds(hp % 4 * NT + i, 1), :].rearrange("p o d -> p (o d)"), w[:, bank, 4 * D0:PC0]).then_inc(v_done, 1)

                def split_z(n, half):
                    two = slice(2 * half, 2 * half + 2)
                    act.wait_ge(rope_done, NT * n + 2 * half + 3)
                    act.wait_ge(z_turned, 6 * n + 1)
                    act.copy(zq[:, two, :, 0:D0], qk[:, two, 0:2 * D0].rearrange("p t (h d) -> p t h d", h=2)).then_inc(z_hi_done, 1)
                    kk = qk[:, two, 2 * D0:].rearrange("p t (h d) -> p t h d", h=2)
                    for j in (0, 2):
                        last = act.copy(zk[:, two, :, j * D0:(j + 1) * D0], kk)
                    last.then_inc(z_hi_done, 1)

                def take_stacks(n):
                    for j, dst in enumerate((qs[:, 0, :], k1[:, 0, :], k2[:, 0, :], qs[:, 1, :])):
                        act.wait_ge(z_turned, 6 * n + j + 2)
                        act.copy(dst, w[:, (1 + j) % 4, :]).then_inc(stack_act, 1)

                def take_o(n, hp):
                    act.wait_ge(av_done, n + 2)
                    act.copy(ho_hi[:, bass.ds(hp, 1), :].rearrange("p o t -> p (o t)"), po[:, :]).then_inc(o_hi_done, 1)

                def pass_v(n, hp):
                    act.wait_ge(av_done, n + 1)
                    act.wait_ge(v_done, NT * n + NT)
                    act.copy(v_cur[:], v_ring[:, bass.ds(hp % 4 * NT, NT), :]).then_inc(v_cur_done, 1)

                def take_p(n):
                    for j, (at, width) in enumerate(((0, 512), (512, 512), (1024, 256))):
                        act.wait_ge(p_turned, 6 * n + j + 1)
                        act.copy(pt[:, 0, at:at + width], w[:, 1 + j, 0:width]).then_inc(pt_a_copied, 1)

                def pair(b, hp, slot="project", turn=True, first=False):
                    n = b * NP0 + hp
                    ahead = (n + 2, hp + 2) if slot == "project" else (n + 1, 0)
                    exps(n, 0)
                    if turn:
                        split_z(n + 1, 1)
                    if slot == "turn_x":
                        turn_x(b + 1)
                    elif slot:
                        for i in range(2):
                            take_v(*ahead, i, SLOT[i])
                    if turn:
                        take_stacks(n + 1)
                    exps(n, 1)
                    if slot == "project" or slot == "next_row":
                        split_z(ahead[0], 0)
                    if not first:
                        take_o(n - 1, hp - 1)
                    pass_v(n, hp)
                    if slot == "project" or slot == "next_row":
                        for i in range(2, NT):
                            take_v(*ahead, i, SLOT[i])
                    take_p(n)

                def row(b, last=False):
                    n = b * NP0
                    for f in range(NF0 + 1):
                        if f < NF0:
                            act.wait_ge(gate_up_done, 2 * NF0 * b + 2 * f + 1)
                            if f > 1:
                                act.wait_ge(hid_done, NF0 * b + f - 1)
                            act.activation(sg[:, f % 2, :], w[:, (3 + 2 * f) % 4, :], ACT.Silu, scale=DEQ).then_inc(silu_done, 1)
                        if f == 1:
                            split_z(n, 1)
                        if f > 0:
                            act.wait_ge(hid_done, NF0 * b + f)
                            act.copy(ho_hi[:, f - 1, :], hid[:, (f - 1) % 2, :]).then_inc(hid_hi_done, 1)
                    take_stacks(n)
                    for i in range(NT):
                        take_v(n + 1, 1, i, FOUR[i])
                    split_z(n + 1, 0)
                    for i in range(NT):
                        act.wait_ge(down_done, NT * b + i + 1)
                        act.activation(gate[:, i, :], w[:, FOUR[i], 0:C], ACT.Silu, scale=DEQ).then_inc(g_done, 1)
                    pair(b, 0, first=True)
                    with act.Fori(1, NP0 - 2) as hp:
                        pair(b, hp)
                    pair(b, NP0 - 2, slot=None if last else "turn_x")
                    pair(b, NP0 - 1, slot=None if last else "next_row", turn=False)
                    take_o(b * NP0 + NP0 - 1, NP0 - 1)

                act.copy(nmax[:, 0, 0:1], c.ident[:, 0:1]).then_inc(exp_done, 4)
                turn_x(0)
                for i in range(NT):
                    take_v(0, 0, i, SLOT[i])
                split_z(0, 0)
                with act.Fori(0, B - 1) as b:
                    row(b)
                row(B - 1, last=True)

            @block.vector
            def _(dve):
                def norm(b):
                    dve.wait_ge(x_loaded, 16 * b + 16)
                    for i in range(NT):
                        dve.tensor_scalar(xn[:, i, :], x[:, bass.ds(b % 2 * NT + i, 1), :].rearrange("p o c -> p (o c)"),
                                          c.mean[:, bass.ds(b * NT + i, 1)], c.rstd[:, bass.ds(b * NT + i, 1)],
                                          ALU.subtract, ALU.mult).then_inc(xn_ready, 1)

                def turn_x(b):
                    for k in range(NC):
                        dve.wait_ge(xt_hi_done, NC * b + k + 1)
                        dve.tensor_tensor(xt_lo[:, k, :], w[:, SLOT[k], :], xt_hi[:, k, :].bitcast(F32), ALU.subtract).then_inc(xt_lo_done, 1)

                def maxima(n, h):
                    for i in range(NT):
                        bank, at = score(i)
                        dve.wait_ge(s_done, 8 * n + 4 * h + (2, 2, 3, 4)[i])
                        dve.tensor_reduce(nmax[:, h, i:i + 1], sc[:, bank, at:at + (i + 1) * P], AXX, ALU.max,
                                          negate=True).then_inc(max_done, 1)

                def take_p(n):
                    for j, (at, width) in enumerate(((0, 512), (512, 512), (1024, 256))):
                        dve.wait_ge(p_turned, 6 * n + 3 + j + 1)
                        dve.tensor_copy(pt[:, 1, at:at + width], w[:, j, 0:width]).then_inc(pt_b_copied, 1)

                def invert(n, h):
                    dve.wait_ge(exp_done, 8 * n + 4 * h + 8)
                    dve.reciprocal(rinv[:, h, :], rsum[:, h, :]).then_inc(rinv_done, 1)

                def rope(n, i, bank):
                    dve.wait_ge(v_done, NT * n + i + 1)
                    dve.wait_ge(rope_done, NT * n + i)
                    src = w[:, bank, 0:4 * D0].rearrange("p (s e d) -> p s e d", s=4, e=2)
                    a = ra[:, i % 2, :].rearrange("p (s d) -> p s d", d=D0 // 2)
                    r = rb[:, i % 2, :].rearrange("p (s e d) -> p s e d", s=4, e=2)
                    dve.tensor_tensor(a, w[:, bank, 0:4 * D0].rearrange("p (s d) -> p s d", d=D0 // 2),
                                      c.rope[:, i, 0, :].unsqueeze(1).to_broadcast([P, 8, D0 // 2]), ALU.mult)
                    dve.tensor_tensor(r[:, :, 0, :], src[:, :, 1, :],
                                      c.rope[:, i, 2, :].unsqueeze(1).to_broadcast([P, 4, D0 // 2]), ALU.mult)
                    dve.tensor_tensor(r[:, :, 1, :], src[:, :, 0, :],
                                      c.rope[:, i, 1, :].unsqueeze(1).to_broadcast([P, 4, D0 // 2]), ALU.mult).then_inc(rope_mult, 1)

                def take_stacks(n):
                    for j, dst in ((4, k1[:, 1, :]), (5, k2[:, 1, :])):
                        dve.wait_ge(z_turned, 6 * n + j + 2)
                        dve.tensor_copy(dst, w[:, (1 + j) % 4, :]).then_inc(stack_dve, 1)

                def take_o(n, hp):
                    dve.wait_ge(o_hi_done, n + 1)
                    at = bass.ds(hp, 1)
                    dve.tensor_tensor(ho_lo[:, at, :].rearrange("p o t -> p (o t)"), po[:, :],
                                      ho_hi[:, at, :].bitcast(F32).rearrange("p o t -> p (o t)"), ALU.subtract).then_inc(o_lo_done, 1)

                def pair(b, hp, slot="project", turn=True, first=False):
                    n = b * NP0 + hp
                    ahead = n + 2 if slot == "project" else n + 1
                    if slot == "turn_x":
                        norm(b + 1)
                    maxima(n, 0)
                    if not first:
                        take_p(n - 1)
                    invert(n, 0)
                    if slot == "turn_x":
                        turn_x(b + 1)
                    elif slot:
                        for i in range(2):
                            rope(ahead, i, SLOT[i])
                    maxima(n, 1)
                    if turn:
                        take_stacks(n + 1)
                    invert(n, 1)
                    if not first:
                        take_o(n - 1, hp - 1)
                    if slot == "project" or slot == "next_row":
                        for i in range(2, NT):
                            rope(ahead, i, SLOT[i])

                def stats(b, i):
                    dve.wait_ge(x1_ready, NT * b + NT)
                    dve.bn_stats(c.stats1[:, bass.ds(b * NT + i, 1), :].rearrange("p o s -> p (o s)"), x[:, bass.ds(b % 2 * NT + i, 1), :].rearrange("p o c -> p (o c)")).then_inc(stats1_done, 1)

                def row(b, first=False, last=False):
                    n = b * NP0
                    for f in range(NF0 + 1):
                        if f < NF0:
                            dve.wait_ge(silu_done, NF0 * b + f + 1)
                            dve.wait_ge(gate_up_done, 2 * NF0 * b + 2 * f + 2)
                            dve.scalar_tensor_tensor(out=hid[:, f % 2, :], in0=w[:, (4 + 2 * f) % 4, :], scalar=DEQ,
                                                     in1=sg[:, f % 2, :], op0=ALU.mult, op1=ALU.mult).then_inc(hid_done, 1)
                        if f > 0:
                            dve.wait_ge(hid_hi_done, NF0 * b + f)
                            dve.tensor_tensor(ho_lo[:, f - 1, :], hid[:, (f - 1) % 2, :],
                                              ho_hi[:, f - 1, :].bitcast(F32), ALU.subtract).then_inc(hid_lo_done, 1)
                            dve.wait_ge(hid_lo_done, NF0 * b + f)
                        if f > 2 and not first:
                            stats(b - 1, f - 3)
                    take_stacks(n)
                    for i in range(NT):
                        rope(n + 1, i, FOUR[i])
                    pair(b, 0, first=True)
                    with dve.Fori(1, NP0 - 2) as hp:
                        pair(b, hp)
                    pair(b, NP0 - 2, slot=None if last else "turn_x")
                    pair(b, NP0 - 1, slot=None if last else "next_row", turn=False)
                    n = b * NP0 + NP0 - 1
                    take_p(n)
                    take_o(n, NP0 - 1)
                    for i in range(NT):
                        dve.wait_ge(wo_done, NT * b + i + 1)
                        if i > 1:
                            dve.wait_ge(mul_done, NT * b + i - 1)
                            dve.wait_ge(x1_ready, NT * b + i - 1)
                        dve.tensor_tensor(so[:, i % 2, :], w[:, FOUR[i], 0:C], c.bo[:], ALU.add).then_inc(so_done, 1)

                norm(0)
                turn_x(0)
                for i in range(NT):
                    rope(0, i, SLOT[i])
                row(0, first=True)
                with dve.Fori(1, B - 1) as b:
                    row(b)
                row(B - 1, last=True)
                for i in range(NT):
                    stats(B - 1, i)
                dve.wait_ge(stats1_done, NT * B + NT)

            @block.gpsimd
            def _(pool):
                def scale(n, h):
                    pool.wait_ge(rinv_done, 2 * n + h + 1)
                    pool.sem_inc(inverse_seen, 1)
                    for i in range(NT):
                        p = pr[:, h, SOFF[i]:SOFF[i] + (i + 1) * P]
                        pool.tensor_scalar(p, p, rinv[:, h, i:i + 1], 1.0, ALU.mult, ALU.mult).then_inc(scaled, 1)

                def rotate(n, i):
                    pool.wait_ge(rope_mult, NT * n + i + 1)
                    if i % 2 == 0 and not (isinstance(n, int) and n == 0):
                        pool.wait_ge(z_hi_done, 4 * n + i - 2)
                        pool.wait_ge(z_lo_done, 4 * n + i - 2)
                    pool.tensor_tensor(qk[:, i, :], ra[:, i % 2, :], rb[:, i % 2, :], ALU.add).then_inc(rope_done, 1)

                def split_z(n, half):
                    two = slice(2 * half, 2 * half + 2)
                    pool.wait_ge(rope_done, NT * n + 2 * half + 3)
                    pool.wait_ge(z_hi_done, 4 * n + 2 * half + 1)
                    pool.tensor_tensor(zq[:, two, :, D0:2 * D0], qk[:, two, 0:2 * D0].rearrange("p t (h d) -> p t h d", h=2),
                                       zq[:, two, :, 0:D0].bitcast(F32), ALU.subtract).then_inc(z_lo_done, 1)
                    pool.wait_ge(z_hi_done, 4 * n + 2 * half + 2)
                    pool.tensor_tensor(zk[:, two, :, D0:2 * D0], qk[:, two, 2 * D0:].rearrange("p t (h d) -> p t h d", h=2),
                                       zk[:, two, :, 0:D0].bitcast(F32), ALU.subtract).then_inc(z_lo_done, 1)

                def pair(b, hp, slot="project", turn=True):
                    n = b * NP0 + hp
                    ahead = n + 2 if slot == "project" else n + 1
                    projects = slot == "project" or slot == "next_row"
                    if turn:
                        split_z(n + 1, 1)
                    scale(n, 0)
                    if projects:
                        rotate(ahead, 0)
                        rotate(ahead, 1)
                    scale(n, 1)
                    if projects:
                        split_z(ahead, 0)
                        rotate(ahead, 2)
                        rotate(ahead, 3)

                def row(b, last=False):
                    n = b * NP0
                    split_z(n, 1)
                    for i in range(NT):
                        rotate(n + 1, i)
                    split_z(n + 1, 0)
                    pair(b, 0)
                    with pool.Fori(1, NP0 - 2) as hp:
                        pair(b, hp)
                    pair(b, NP0 - 2, slot=None if last else "turn_x")
                    pair(b, NP0 - 1, slot=None if last else "next_row", turn=False)
                    for i in range(NT):
                        pool.wait_ge(so_done, NT * b + i + 5)
                        pool.wait_ge(g_done, NT * b + i + 1)
                        pool.tensor_tensor(so[:, i % 2, :], so[:, i % 2, :], gate[:, i, :], ALU.mult).then_inc(mul_done, 1)
                        pool.wait_ge(mul_done, NT * b + i + 1)
                        xi = x[:, bass.ds(b % 2 * NT + i, 1), :].rearrange("p o c -> p (o c)")
                        pool.tensor_tensor(xi, xi, so[:, i % 2, :], ALU.add).then_inc(x1_ready, 1)

                pool.sem_inc(x1_stored, 16)
                pool.sem_inc(stats1_done, NT)
                pool.sem_inc(so_done, 4)
                pool.sem_inc(rope_done, 1)
                pool.sem_inc(z_turned, 1)
                pool.sem_inc(av_done, 1)
                pool.sem_inc(o_lo_done, 1)
                for i in range(NT):
                    rotate(0, i)
                split_z(0, 0)
                with pool.Fori(0, B - 1) as b:
                    row(b)
                row(B - 1, last=True)


def experts(nc, c, io):
    with ExitStack() as ctx:
        t = Mem(nc, ctx)
        r1, r3 = (t.sb(f"raw{n}", [P, NC, FP1]) for n in (1, 3))
        r2 = t.sb("raw2", [P, NF1, C])
        w1h, w1l, w3h, w3l = (t.sb(n, [P, 2, NC, FP1], F32R) for n in ("w1h", "w1l", "w3h", "w3l"))
        w2h, w2l = (t.sb(n, [P, 2, NF1, C], F32R) for n in ("w2h", "w2l"))
        hh, hl = (t.sb(n, [P, NF1, T], F32R) for n in ("hh", "hl"))
        sg_hid = t.sb("sg_hid", [P, 2, 2, T])
        sg, hid = sg_hid[:, 0], sg_hid[:, 1]
        rows = [h[:].bitcast(F32).rearrange("p f t -> p (f t)")[:, r * NT * C:(r + 1) * NT * C] for h in (hh, hl) for r in range(3)]
        rows += [sg_hid[:, r].rearrange("p s t -> p (s t)") for r in range(2)]
        xa = [r.rearrange("p (t c) -> p t c", c=C) for r in rows]
        xn = t.sb("xn1", [P, 2, NT, C])
        aggr = t.sb("aggr1", [P, B * NT, 2])
        dev = t.sb("dev1", [P, B * NT])
        rstd = t.sb("rstd1", [P, B * NT])
        shift = t.sb("shift1", [P, B * NT])
        eps = t.sb("eps1", [P, 1])
        go = t.sb("go", [P, NT, C])
        w = t.ps("wx", [P, 4, 512])
        dn = t.ps("dn", [P, 4, 512])
        x_in = [t.sem(f"x1_in{b}") for b in range(B)]
        eps_set = t.sem("eps_set1")
        aggr_done = t.sem("aggr_done1")
        dev_done = t.sem("dev_done1")
        rstd_done = t.sem("rstd_done1")
        xn_act = t.sem("xn_act1")
        xn_dve = t.sem("xn_dve1")
        xn_turned = t.sem("xn_turned1")
        xt_hi_done = t.sem("xt1_hi_done")
        xt_lo_done = t.sem("xt1_lo_done")
        xt_stored = t.sem("xt1_stored")
        w13_in = t.sem("w13_in")
        w2_in = t.sem("w2_in")
        pad_set = t.sem("pad_set")
        hi13 = t.sem("hi13")
        lo13 = t.sem("lo13")
        hi2 = t.sem("hi2")
        lo2 = t.sem("lo2")
        gate_up_done = t.sem("gate_up_done1")
        silu_done = t.sem("silu_done1")
        hid_done = t.sem("hid_done1")
        hid_hi_done = t.sem("hid_hi_done1")
        hid_lo_done = t.sem("hid_lo_done1")
        down_done = t.sem("down_done1")
        g_done = t.sem("g_done1")
        g_stored = t.sem("g_stored")

        with nc.Block() as block:
            @block.sync
            def _(sp):
                def load(e):
                    one = bass.ds(e, 1)
                    full = (NF1 - 1) * P
                    sp.wait_ge(hi13, 2 * e)
                    sp.wait_ge(lo13, 2 * e)
                    sp.dma_start(r1[:, :, 0:F1], io.w1[one].rearrange("o (c p) f -> p (o c) f", p=P)).then_inc(w13_in, 16)
                    sp.dma_start(r3[:, :, 0:F1], io.w3[one].rearrange("o (c p) f -> p (o c) f", p=P)).then_inc(w13_in, 16)
                    sp.wait_ge(hi2, e)
                    sp.wait_ge(lo2, e)
                    sp.dma_start(r2[:, 0:NF1 - 1, :], io.w2[one, 0:full].rearrange("o (f p) n -> p (o f) n", p=P)).then_inc(w2_in, 16)
                    sp.dma_start(r2[0:FR1, NF1 - 1:NF1, :], io.w2[one, full:F1].rearrange("o p n -> p o n")).then_inc(w2_in, 16)

                def store(e):
                    for i in range(NT):
                        sp.wait_ge(g_done, NT * e + i + 1)
                        dst = io.gate1.rearrange("b (e k) c -> e b k c", e=E1)[bass.ds(e, 1), 2 * i:2 * i + 2]
                        sp.dma_start(dst.rearrange("o b k c -> (o b) k c"), go[:, i, :]).then_inc(g_stored, 16)

                for b in range(B):
                    sp.dma_start(xa[b], io.x1[b].rearrange("(t p) c -> p t c", p=P)).then_inc(x_in[b], 16)
                    if b == 1:
                        sp.wait_ge(pad_set, 3)
                        load(0)
                load(1)
                sp.wait_ge(xt_hi_done, NC * B)
                sp.dma_start(io.xt1_hi, c.xt1_hi[:].bitcast(F32)).then_inc(xt_stored, 16)
                sp.wait_ge(xt_lo_done, NC * B)
                sp.dma_start(io.xt1_lo, c.xt1_lo[:].bitcast(F32)).then_inc(xt_stored, 16)
                with sp.Fori(0, E1 - 2) as e:
                    store(e)
                    load(e + 2)
                store(E1 - 2)
                store(E1 - 1)
                sp.wait_ge(g_stored, 16 * NT * E1)
                sp.wait_ge(xt_stored, 32)

            @block.gpsimd
            def _(pool):
                pool.memset(r2[FR1:P, NF1 - 1, :], 0.0).then_inc(pad_set, 1)
                pool.wait_ge(pad_set, 1)
                pool.memset(r1[:, :, F1:FP1], 0.0).then_inc(pad_set, 1)
                pool.memset(r3[:, :, F1:FP1], 0.0).then_inc(pad_set, 1)
                with pool.Fori(0, E1) as e:
                    for f in range(NF1):
                        pool.wait_ge(hid_hi_done, NF1 * e + f + 1)
                        pool.tensor_tensor(hl[:, f, :], hid[:, f % 2, :], hh[:, f, :].bitcast(F32),
                                           ALU.subtract).then_inc(hid_lo_done, 1)

            @block.scalar
            def _(act):
                def split(e, u, part):
                    if part == 0:
                        act.wait_ge(down_done, NT * (e - 1))
                    if part < 2:
                        act.wait_ge(w13_in, 32 * e + 32)
                        act.copy((w1h, w3h)[part][:, u], (r1, r3)[part][:]).then_inc(hi13, 1)
                    else:
                        act.wait_ge(w2_in, 32 * e + 32)
                        act.copy(w2h[:, u], r2[:]).then_inc(hi2, 1)

                def ffn(e, u, last=False):
                    for f in range(NF1 + 1):
                        if f < NF1:
                            act.wait_ge(gate_up_done, 2 * NF1 * e + 2 * f + 1)
                            if f > 1:
                                act.wait_ge(hid_done, NF1 * e + f - 1)
                            act.activation(sg[:, f % 2, :], w[:, 2 * f % 4, :], ACT.Silu).then_inc(silu_done, 1)
                        if f > 0:
                            act.wait_ge(hid_done, NF1 * e + f)
                            act.copy(hh[:, f - 1, :], hid[:, (f - 1) % 2, :]).then_inc(hid_hi_done, 1)
                        if f in (1, 3, 5) and not last:
                            split(e + 1, 1 - u, f // 2)
                    for i in range(NT):
                        act.wait_ge(down_done, NT * e + i + 1)
                        if i == 0:
                            act.wait_ge(g_stored, 16 * NT * e)
                        act.activation(go[:, i, :], dn[:, i, 0:C], ACT.Silu).then_inc(g_done, 1)

                def turned_hi(b):
                    for k in range(NC):
                        act.wait_ge(xn_turned, NC * b + k + 1)
                        act.copy(c.xt1_hi[:, k, b * T:(b + 1) * T], dn[:, b % 2 * NC + k, :]).then_inc(xt_hi_done, 1)

                act.wait_ge(aggr_done, B * NT)
                act.wait_ge(eps_set, 1)
                act.activation(dev[:], aggr[:, :, 1], ACT.Sqrt, bias=eps[:]).then_inc(dev_done, 1)
                act.wait_ge(pad_set, 3)
                act.wait_ge(w13_in, 32)
                act.copy(w1h[:, 0], r1[:]).then_inc(hi13, 1)
                act.copy(w3h[:, 0], r3[:]).then_inc(hi13, 1)
                act.wait_ge(rstd_done, 2)
                for b in range(B):
                    act.wait_ge(x_in[b], 16)
                    if b > 1:
                        act.wait_ge(xn_turned, NC * (b - 1))
                    for i in range(NT // 2, NT):
                        at = b * NT + i
                        act.activation(xn[:, b % 2, i, :], xa[b][:, i, :], ACT.Identity, bias=shift[:, at:at + 1],
                                       scale=rstd[:, at:at + 1]).then_inc(xn_act, 1)
                    if b > 0:
                        turned_hi(b - 1)
                turned_hi(B - 1)
                act.wait_ge(w2_in, 32)
                act.copy(w2h[:, 0], r2[:]).then_inc(hi2, 1)
                with act.Fori(0, E1 // 2 - 1) as p:
                    ffn(2 * p, 0)
                    ffn(2 * p + 1, 1)
                ffn(E1 - 2, 0)
                ffn(E1 - 1, 1, last=True)

            @block.vector
            def _(dve):
                def split(e, u, part):
                    if part < 2:
                        dve.wait_ge(hi13, 2 * e + part + 1)
                        hi, lo, raw = ((w1h, w1l, r1), (w3h, w3l, r3))[part]
                        dve.tensor_tensor(lo[:, u], raw[:], hi[:, u].bitcast(F32), ALU.subtract).then_inc(lo13, 1)
                    else:
                        dve.wait_ge(hi2, e + 1)
                        dve.tensor_tensor(w2l[:, u], r2[:], w2h[:, u].bitcast(F32), ALU.subtract).then_inc(lo2, 1)

                def ffn(e, u, last=False):
                    for f in range(NF1):
                        dve.wait_ge(silu_done, NF1 * e + f + 1)
                        dve.wait_ge(gate_up_done, 2 * NF1 * e + 2 * f + 2)
                        if f > 1:
                            dve.wait_ge(hid_lo_done, NF1 * e + f - 1)
                        dve.tensor_tensor(hid[:, f % 2, :], w[:, (2 * f + 1) % 4, :], sg[:, f % 2, :],
                                          ALU.mult).then_inc(hid_done, 1)
                        if f in (2, 4, 5) and not last:
                            split(e + 1, 1 - u, {2: 0, 4: 1, 5: 2}[f])

                dve.memset(eps[:], EPS).then_inc(eps_set, 1)
                for i in range(B * NT):
                    dve.bn_aggr(aggr[:, i, :], c.stats1[:, i, :]).then_inc(aggr_done, 1)
                dve.wait_ge(aggr_done, B * NT)
                dve.wait_ge(dev_done, 1)
                dve.reciprocal(rstd[:], dev[:]).then_inc(rstd_done, 1)
                dve.wait_ge(rstd_done, 1)
                dve.scalar_tensor_tensor(out=shift[:], in0=aggr[:, :, 0], scalar=-1.0, in1=rstd[:],
                                         op0=ALU.mult, op1=ALU.mult).then_inc(rstd_done, 1)
                split(0, 0, 0)
                split(0, 0, 1)

                def turned_lo(b):
                    for k in range(NC):
                        dve.wait_ge(xt_hi_done, NC * b + k + 1)
                        at = slice(b * T, (b + 1) * T)
                        dve.tensor_tensor(c.xt1_lo[:, k, at], dn[:, b % 2 * NC + k, :], c.xt1_hi[:, k, at].bitcast(F32),
                                          ALU.subtract).then_inc(xt_lo_done, 1)

                for b in range(B):
                    dve.wait_ge(x_in[b], 16)
                    if b > 1:
                        dve.wait_ge(xn_turned, NC * (b - 1))
                    for i in range(NT // 2):
                        at = b * NT + i
                        dve.tensor_scalar(xn[:, b % 2, i, :], xa[b][:, i, :], aggr[:, at, 0:1], rstd[:, at:at + 1],
                                          ALU.subtract, ALU.mult).then_inc(xn_dve, 1)
                    if b > 0:
                        turned_lo(b - 1)
                turned_lo(B - 1)
                split(0, 0, 2)
                with dve.Fori(0, E1 // 2 - 1) as p:
                    ffn(2 * p, 0)
                    ffn(2 * p + 1, 1)
                ffn(E1 - 2, 0)
                ffn(E1 - 1, 1, last=True)

            @block.tensor
            def _(pe):
                def tokens(xt, k, e):
                    return xt[:, k, :].rearrange("p (b e k) -> p b e k", b=B, e=E1)[:, :, bass.ds(e, 1), :].rearrange("p b o k -> p b (o k)")

                def ffn(e, u):
                    pe.wait_ge(hi13, 2 * e + 2)
                    pe.wait_ge(lo13, 2 * e + 2)
                    for f in range(NF1):
                        cols = slice(f * P, (f + 1) * P)
                        for j, (wh, wl) in enumerate(((w1h, w1l), (w3h, w3l))):
                            if f < 2:
                                pe.wait_ge(silu_done, NF1 * e)
                                pe.wait_ge(hid_done, NF1 * e)
                            elif j == 0:
                                pe.wait_ge(silu_done, NF1 * e + f - 1)
                            else:
                                pe.wait_ge(hid_done, NF1 * e + f - 1)
                            out = w[:, (2 * f + j) % 4, :].rearrange("p (b k) -> p b k", b=B)
                            for k in range(NC):
                                pe.matmul(out, wh[:, u, k, cols], tokens(c.xt1_hi, k, e), start=(k == 0), stop=False)
                                pe.matmul(out, wh[:, u, k, cols], tokens(c.xt1_lo, k, e), start=False, stop=False)
                                mm = pe.matmul(out, wl[:, u, k, cols], tokens(c.xt1_hi, k, e), start=False, stop=(k == NC - 1))
                            mm.then_inc(gate_up_done, 1)
                    pe.wait_ge(hi2, e + 1)
                    pe.wait_ge(lo2, e + 1)
                    pe.wait_ge(g_done, NT * e)
                    for f in range(NF1):
                        pe.wait_ge(hid_hi_done, NF1 * e + f + 1)
                        pe.wait_ge(hid_lo_done, NF1 * e + f + 1)
                        for i in range(NT):
                            a, b = hh[:, f, i * P:(i + 1) * P], hl[:, f, i * P:(i + 1) * P]
                            pe.matmul(dn[:, i, 0:C], a, w2h[:, u, f, :], start=(f == 0), stop=False)
                            pe.matmul(dn[:, i, 0:C], a, w2l[:, u, f, :], start=False, stop=False)
                            mm = pe.matmul(dn[:, i, 0:C], b, w2h[:, u, f, :], start=False, stop=(f == NF1 - 1))
                            if f == NF1 - 1:
                                mm.then_inc(down_done, 1)

                for b in range(B):
                    pe.wait_ge(xn_act, NT // 2 * (b + 1))
                    pe.wait_ge(xn_dve, NT // 2 * (b + 1))
                    if b > 1:
                        pe.wait_ge(xt_lo_done, NC * (b - 1))
                    for k in range(NC):
                        for i in range(NT):
                            mm = pe.transpose(dn[:, b % 2 * NC + k, i * P:(i + 1) * P], xn[:, b % 2, i, k * P:(k + 1) * P], c.ident[:])
                        mm.then_inc(xn_turned, 1)
                pe.wait_ge(xt_hi_done, NC * B)
                pe.wait_ge(xt_lo_done, NC * B)
                with pe.Fori(0, E1 // 2) as p:
                    ffn(2 * p, 0)
                    ffn(2 * p + 1, 1)


def attention1(nc, c, io):
    HG = H1 // NG1
    S3 = 3 * D1
    with ExitStack() as ctx:
        t = Mem(nc, ctx)
        wq_hi, wq_lo = (t.sb(n, [P, NC, 3 * C], F32R) for n in ("wq1_hi", "wq1_lo"))
        wo_hi, wo_lo = (t.sb(n, [P, NC, C], F32R) for n in ("wo1_hi", "wo1_lo"))
        bqkv = t.sb("bqkv1", [P, 3 * C])
        bo = t.sb("bo1_sb", [P, C])
        xs_hi, xs_lo = (t.sb(n, [P, NC, T], F32R) for n in ("xs_hi", "xs_lo"))
        x1 = t.sb("x1_sb", [P, NT, C])
        g1 = t.sb("g1_sb", [P, NT, C])
        qn = t.sb("qn", [P, NT, 3 * C])
        zq = t.sb("zq1", [P, NT, HG, 3, D1], F32R)
        zk = t.sb("zk1", [P, NT, HG, P], F32R)
        qb = t.sb("qb", [P, NG1, 2, T], F32R)
        kb = t.sb("kb", [P, NG1, HG, T], F32R)
        vs = t.sb("vs", [P, NT, H1, 2 * D1])
        pt = t.sb("pt1", [P, 2, HG, NT, T])
        wq_raw = pt[:, 0, 0].rearrange("p t n -> p (t n)")[:, 0:NC * 3 * C].rearrange("p (c n) -> p c n", c=NC)
        wo_raw = pt[:, 0, 1].rearrange("p t n -> p (t n)")[:, 0:NC * C].rearrange("p (c n) -> p c n", c=NC)
        nm = t.sb("nm", [P, 2, NT, HG])
        sn = t.sb("sn", [P, NT, 4, 2 * D1], F32R)
        ou = t.sb("ou", [P, T])
        inv = t.sb("inv", [P, NT, HG, 1])
        on = t.sb("on", [P, NT, C])
        ot_hi, ot_lo = (t.sb(n, [P, NC, T], F32R) for n in ("ot_hi", "ot_lo"))
        so = t.sb("so1", [P, 2, C])
        ps = t.ps("ps", [P, 2, 512])
        pst = t.ps("pst", [P, 2, 512])
        po = t.ps("po1", [P, 512])
        pn = t.ps("pn", [P, 512])
        w = t.ps("w1a", [P, 2, 512])
        wq_in = t.sem("a_wq_in")
        wo_in = t.sem("a_wo_in")
        bias_in = t.sem("a_bias_in")
        w_hi_done = t.sem("a_w_hi_done")
        w_lo_done = t.sem("a_w_lo_done")
        bias_done = t.sem("a_bias_done")
        sn_hi_done = t.sem("a_sn_hi_done")
        xs_in = t.sem("a_xs_in")
        xg_in = t.sem("a_xg_in")
        x_stored = t.sem("a_x_stored")
        x_done = t.sem("a_x_done")
        zs_set = t.sem("a_zs_set")
        vs_set = t.sem("a_vs_set")
        proj_done = t.sem("a_proj_done")
        qn_done = t.sem("a_qn_done")
        z_hi_done = t.sem("a_z_hi_done")
        z_lo_done = t.sem("a_z_lo_done")
        z_turned = t.sem("a_z_turned")
        stack_done = t.sem("a_stack_done")
        s_done = t.sem("a_s_done")
        max_done = t.sem("a_max_done")
        sn_done = t.sem("a_sn_done")
        n_turned = t.sem("a_n_turned")
        n_done = t.sem("a_n_done")
        st_done = t.sem("a_st_done")
        exp_done = t.sem("a_exp_done")
        vs_done = t.sem("a_vs_done")
        av_done = t.sem("a_av_done")
        ou_done = t.sem("a_ou_done")
        o_turned = t.sem("a_o_turned")
        inv_done = t.sem("a_inv_done")
        on_done = t.sem("a_on_done")
        on_turned = t.sem("a_on_turned")
        ot_hi_done = t.sem("a_ot_hi_done")
        ot_lo_done = t.sem("a_ot_lo_done")
        out_done = t.sem("a_out_done")
        so_done = t.sem("a_so_done")
        mul_done = t.sem("a_mul_done")

        with nc.Block() as block:
            @block.sync
            def _(sp):
                def load_xs(b):
                    sp.dma_start(xs_hi[:].bitcast(F32), io.xt1_hi[:, :, bass.ds(b * T, T)]).then_inc(xs_in, 16)
                    sp.dma_start(xs_lo[:].bitcast(F32), io.xt1_lo[:, :, bass.ds(b * T, T)]).then_inc(xs_in, 16)

                def load_xg(b):
                    for dst, src in ((x1, io.x1), (g1, io.gate1)):
                        sp.dma_start(dst[:], src[bass.ds(b, 1)].rearrange("o (t p) c -> p (o t) c", p=P)).then_inc(xg_in, 16)

                def store(b):
                    sp.wait_ge(x_done, NT * b + NT + 2)
                    sp.dma_start(io.out[bass.ds(b, 1)].rearrange("o (t p) c -> p (o t) c", p=P), x1[:]).then_inc(x_stored, 16)
                    sp.wait_ge(x_stored, 16 * b + 16)

                load_xs(0)
                sp.dma_start(bqkv[:], io.bqkv1.partition_broadcast(P)).then_inc(bias_in, 16)
                sp.dma_start(bo[:], io.bo1.partition_broadcast(P)).then_inc(bias_in, 16)
                load_xg(0)
                sp.wait_ge(proj_done, 2 * NT)
                load_xs(1)
                with sp.Fori(0, B - 2) as b:
                    sp.wait_ge(proj_done, 2 * NT * b + 4 * NT)
                    load_xs(b + 2)
                    store(b)
                    load_xg(b + 1)
                store(B - 2)
                load_xg(B - 1)
                store(B - 1)

            @block.gpsimd
            def _(pool):
                pool.memset(zk[:].bitcast(F32), 0.0).then_inc(zs_set, 1)
                pool.memset(sn[:].bitcast(F32), 0.0).then_inc(zs_set, 1)
                pool.memset(vs[:], 0.0).then_inc(vs_set, 1)
                pool.wait_ge(vs_set, 1)
                pool.memset(vs[:, :, :, D1:D1 + 1], 1.0).then_inc(vs_set, 1)
                pool.wait_ge(zs_set, 2)
                for h in range(HG):
                    at = 2 * S3 + h % 2
                    pool.memset(zk[:, :, h, at:at + 3:2].bitcast(F32), 1.0).then_inc(zs_set, 1)

                def split_z(b, g):
                    q = NG1 * b + g
                    src = qn[:, :, g * HG * D1:(g + 1) * HG * D1]
                    pool.wait_ge(z_hi_done, 4 * q + 2)
                    pool.tensor_tensor(zq[:, :, :, 1, :], src.rearrange("p t (h d) -> p t h d", d=D1),
                                       zq[:, :, :, 0, :].bitcast(F32), ALU.subtract).then_inc(z_lo_done, 1)
                    pool.wait_ge(z_hi_done, 4 * q + 4)
                    ks = qn[:, :, C + g * HG * D1:C + (g + 1) * HG * D1]
                    for e in range(2):
                        base = e * S3
                        pool.tensor_tensor(zk[:, :, e::2, base + 2 * D1:base + 3 * D1],
                                           ks.rearrange("p t (h e d) -> p t h e d", e=2, d=D1)[:, :, :, e, :],
                                           zk[:, :, e::2, base:base + D1].bitcast(F32), ALU.subtract).then_inc(z_lo_done, 1)

                def finish(b):
                    for i in range(NT):
                        pool.wait_ge(so_done, NT * b + i + 1)
                        if i == 0:
                            pool.wait_ge(xg_in, 32 * b + 32)
                        pool.tensor_tensor(so[:, i % 2, :], so[:, i % 2, :], g1[:, i, :], ALU.mult).then_inc(mul_done, 1)
                        pool.wait_ge(mul_done, NT * b + i + 1)
                        pool.tensor_tensor(x1[:, i, :], x1[:, i, :], so[:, i % 2, :], ALU.add).then_inc(x_done, 1)

                def row(b, first=False, last=False):
                    for g in range(NG1):
                        if not (last and g > 0):
                            split_z(b + (g + 3) // NG1, (g + 3) % NG1)
                        if g == 2 and not first:
                            finish(b - 1)

                pool.sem_inc(x_done, 2)
                for g in range(3):
                    split_z(0, g)
                row(0, first=True)
                with pool.Fori(1, B - 1) as b:
                    row(b)
                row(B - 1, last=True)
                finish(B - 1)

            @block.tensor
            def _(pe):
                def project(b, i):
                    for j, (at, width) in enumerate(((0, 2 * C), (2 * C, C))):
                        if isinstance(b, int) and b == 0:
                            if i > 0:
                                pe.wait_ge(qn_done, 2 * i - 1 + j)
                        elif i == 2:
                            pe.wait_ge(qn_done, 2 * NT * b + 3 + j)
                        else:
                            pe.wait_ge(stack_done, 6 * (NG1 * b - 1) + (1, 3, 0, 5)[i] + j)
                        for k in range(NC):
                            xh, xl = (a[:, k, i * P:(i + 1) * P] for a in (xs_hi, xs_lo))
                            cols = slice(at, at + width)
                            pe.matmul(w[:, j, 0:width], xh, wq_hi[:, k, cols], start=(k == 0), stop=False)
                            pe.matmul(w[:, j, 0:width], xh, wq_lo[:, k, cols], start=False, stop=False)
                            mm = pe.matmul(w[:, j, 0:width], xl, wq_hi[:, k, cols], start=False, stop=(k == NC - 1))
                        mm.then_inc(proj_done, 1)

                def turn_z(q, j, bank_read):
                    if j == 0:
                        pe.wait_ge(z_hi_done, 4 * q + 4)
                        pe.wait_ge(z_lo_done, 3 * q + 3)
                    pe.wait_ge(bank_read[0], bank_read[1])
                    for i in range(NT):
                        if j < 2:
                            src = zq[:, i, 2 * j:2 * j + 2].rearrange("p h s d -> p (h s d)")
                            mm = pe.transpose(w[0:2 * S3, j % 2, i * P:(i + 1) * P], src.bitcast(F32), c.ident[:])
                        else:
                            mm = pe.transpose(w[:, j % 2, i * P:(i + 1) * P], zk[:, i, j - 2, :].bitcast(F32), c.ident[:])
                    mm.then_inc(z_turned, 1)

                def score(q, g, h, i):
                    if h < 2 and i == 0:
                        pe.wait_ge(stack_done, 6 * q + (3 if h == 0 else 6))
                    n = 16 * q + 4 * h + i
                    pe.wait_ge(max_done, n)
                    pe.matmul(ps[:, i % 2, :], qb[0:2 * S3, g, h // 2, i * P:(i + 1) * P], kb[0:2 * S3, g, h, :],
                              start=True, stop=True).then_inc(s_done, 1)

                def score_t(q, g, h, i):
                    if h == 0 and i == 0:
                        pe.wait_ge(n_done, 2 * q + 2)
                    n = 16 * q + 4 * h + i
                    pe.wait_ge(exp_done, n)
                    pe.matmul(pst[:, i % 2, :], kb[:, g, h, i * P:(i + 1) * P], qb[:, g, h // 2, :],
                              start=True, stop=True).then_inc(st_done, 1)

                def weigh(q, g, kt, rows_done):
                    if kt == 0:
                        pe.wait_ge(exp_done, 16 * q + 17)
                        pe.wait_ge(ou_done, q)
                        pe.wait_ge(vs_done, rows_done)
                    for h in range(HG):
                        mm = pe.matmul(po[2 * D1 * h:2 * D1 * (h + 1), :], vs[:, kt, g * HG + h, :], pt[:, g % 2, h, kt, :],
                                       start=(kt == 0), stop=(kt == NT - 1))
                    if kt == NT - 1:
                        mm.then_inc(av_done, 1)

                def turn_n(q):
                    pe.wait_ge(sn_done, q + 1)
                    if not isinstance(q, int) or q > 3:
                        pe.wait_ge(on_done, q - 2)
                    for i in range(NT):
                        mm = pe.transpose(pn[:, i * P:(i + 1) * P], sn[:, i].rearrange("p a b -> p (a b)").bitcast(F32), c.ident[:])
                    mm.then_inc(n_turned, 1)

                def turn_o(q, n_turns):
                    pe.wait_ge(ou_done, q + 1)
                    pe.wait_ge(n_done, 2 * n_turns)
                    for i in range(NT):
                        mm = pe.transpose(pn[:, i * P:(i + 1) * P], ou[:, i * P:(i + 1) * P], c.ident[:])
                    mm.then_inc(o_turned, 1)

                def turn_on(b, k):
                    if k == 0:
                        pe.wait_ge(on_done, NG1 * b + NG1)
                    for i in range(NT):
                        mm = pe.transpose(w[:, k, i * P:(i + 1) * P], on[:, i, k * P:(k + 1) * P], c.ident[:])
                    mm.then_inc(on_turned, 1)

                def out_project(b, i):
                    if i < 2:
                        pe.wait_ge(ot_lo_done, NC * b + NC)
                    else:
                        pe.wait_ge(so_done, NT * b + i - 1)
                    for k in range(NC):
                        oh, ol = (a[:, k, i * P:(i + 1) * P] for a in (ot_hi, ot_lo))
                        pe.matmul(w[:, i % 2, 0:C], oh, wo_hi[:, k, :], start=(k == 0), stop=False)
                        pe.matmul(w[:, i % 2, 0:C], oh, wo_lo[:, k, :], start=False, stop=False)
                        mm = pe.matmul(w[:, i % 2, 0:C], ol, wo_hi[:, k, :], start=False, stop=(k == NC - 1))
                    mm.then_inc(out_done, 1)

                def group(b, g, first=False, last=False):
                    q = NG1 * b + g
                    more1, more2 = (not (last and g + n >= NG1) for n in (1, 2))
                    back1, back2 = (not (first and g < n) for n in (1, 2))
                    projects = g == 1 and not last
                    for h in range(HG):
                        for i in range(NT):
                            if h < HG - 1 and more1:
                                score(q + 1, (g + 1) % NG1, h + 1, i)
                            elif h == HG - 1 and more2:
                                score(q + 2, (g + 2) % NG1, 0, i)
                            score_t(q, g, h, i)
                            if h < HG - 1 and i < 2 and more2:
                                j = 2 * h + i
                                if h > 0 and projects:
                                    bank_read = (qn_done, 2 * NT * (b + 1) + (0, 1, 5)[h] + i)
                                elif h == 0 and g == 2 and not first:
                                    bank_read = (ot_lo_done, NC * b)
                                elif h == 0 and g == 3 and not first:
                                    bank_read = (so_done, NT * b)
                                else:
                                    bank_read = (stack_done, 6 * (q + 2) + j - 1)
                                turn_z(q + 2, j, bank_read)
                            if i == 2 and projects and h < HG - 1:
                                if h == 0:
                                    pe.wait_ge(xs_in, 32 * b + 64)
                                    pe.wait_ge(z_lo_done, 3 * q + 9)
                                project(b + 1, (0, 1, 3)[h])
                            if i == 3 and projects and h == 1:
                                project(b + 1, 2)
                            if h == 1 and i == 2 and back2:
                                turn_o(q - 2, q + 1)
                            if h == HG - 1:
                                if i == 1 and more1:
                                    turn_n(q + 1)
                                if g == 1 and not first and i >= 2:
                                    if last:
                                        pe.wait_ge(stack_done, 6 * (q + 2) + 3 + i)
                                    else:
                                        pe.wait_ge(qn_done, 2 * NT * (b + 1) + 5 + i)
                                    turn_on(b - 1, i - 2)
                                if g == 2 and not first:
                                    if i < 2 and not last:
                                        pe.wait_ge(stack_done, 6 * (q + 2) + 5 + i)
                                    out_project(b - 1, i)
                        if back1:
                            weigh(q - 1, (g + 3) % NG1, h, b + 1 if g else b)

                pe.wait_ge(w_hi_done, 2)
                pe.wait_ge(w_lo_done, 2)
                pe.wait_ge(xs_in, 32)
                for i in range(NT):
                    project(0, i)
                for q in range(2):
                    for j in range(6):
                        turn_z(q, j, (qn_done, 2 * NT) if q == 0 and j < 2 else (stack_done, 6 * q + j - 1))
                for n in range(HG + 1):
                    for i in range(NT):
                        score(n // HG, n // HG, n % HG, i)
                turn_n(0)
                for g in range(NG1):
                    group(0, g, first=True)
                with pe.Fori(1, B - 1) as b:
                    for g in range(NG1):
                        group(b, g)
                for g in range(NG1):
                    group(B - 1, g, last=True)
                q = NG1 * B - 1
                for kt in range(NT):
                    weigh(q, NG1 - 1, kt, B)
                for g in (q - 1, q):
                    pe.wait_ge(on_done, g)
                    turn_o(g, q + 1)
                for k in range(NC):
                    turn_on(B - 1, k)
                for i in range(NT):
                    out_project(B - 1, i)

            @block.vector
            def _(dve):
                def maximum(q, g, h, i):
                    if h == 0 and i == 0 and not (isinstance(q, int) and q < 2):
                        dve.wait_ge(sn_done, q - 1)
                    dve.wait_ge(s_done, 16 * q + 4 * h + i + 1)
                    dve.tensor_reduce(nm[:, g % 2, i, h:h + 1], ps[:, i % 2, :], AXX, ALU.max, negate=True).then_inc(max_done, 1)

                def split_n(q, g):
                    dve.wait_ge(max_done, 16 * q + 17)
                    dve.wait_ge(n_turned, q)
                    v = nm[:, g % 2].rearrange("p t (a b) -> p t a b", a=2)
                    dve.tensor_copy(sn[:, :, 0:2, 0:2], v).then_inc(sn_hi_done, 1)
                    dve.wait_ge(sn_hi_done, q + 1)
                    dve.tensor_tensor(sn[:, :, 0:2, 2:4], v, sn[:, :, 0:2, 0:2].bitcast(F32), ALU.subtract).then_inc(sn_done, 1)

                def take_n(q, g):
                    dve.wait_ge(n_turned, q + 1)
                    for a in range(2):
                        dve.tensor_copy(qb[2 * S3:P, g, a, :], pn[2 * D1 * a:2 * D1 * (a + 1), :]).then_inc(n_done, 1)

                def take_o(q, g):
                    dve.wait_ge(o_turned, q + 1)
                    v = pn[:].rearrange("p (t h d) -> p t h d", t=NT, h=HG)
                    dve.reciprocal(inv[:], v[:, :, :, D1:D1 + 1]).then_inc(inv_done, 1)
                    dve.wait_ge(inv_done, q + 1)
                    dve.tensor_tensor(on[:, :, g * HG * D1:(g + 1) * HG * D1].rearrange("p t (h d) -> p t h d", h=HG),
                                      v[:, :, :, 0:D1], inv[:].to_broadcast([P, NT, HG, D1]), ALU.mult).then_inc(on_done, 1)

                def take_proj(b, i):
                    for j, (at, width) in enumerate(((0, 2 * C), (2 * C, C))):
                        dve.wait_ge(proj_done, 2 * NT * b + 2 * i + j + 1)
                        dve.tensor_tensor(qn[:, i, at:at + width], w[:, j, 0:width], bqkv[:, at:at + width],
                                          ALU.add).then_inc(qn_done, 1)

                def split_ot(b):
                    for k in range(NC):
                        dve.wait_ge(ot_hi_done, NC * b + k + 1)
                        dve.tensor_tensor(ot_lo[:, k, :], w[:, k, :], ot_hi[:, k, :].bitcast(F32), ALU.subtract).then_inc(ot_lo_done, 1)

                def take_out(b, i):
                    dve.wait_ge(out_done, NT * b + i + 1)
                    dve.wait_ge(x_done, NT * b + i + 1)
                    dve.tensor_tensor(so[:, i % 2, :], w[:, i % 2, 0:C], bo[:], ALU.add).then_inc(so_done, 1)

                def group(b, g, first=False, last=False):
                    q = NG1 * b + g
                    more1, more2 = (not (last and g + n >= NG1) for n in (1, 2))
                    back2 = not (first and g < 2)
                    projects = g == 1 and not last
                    for h in range(HG):
                        if h == HG - 1 and more1:
                            split_n(q + 1, g + 1)
                        for i in range(NT):
                            if h < HG - 1 and more1:
                                maximum(q + 1, g + 1, h + 1, i)
                            elif h == HG - 1 and more2:
                                maximum(q + 2, g, 0, i)
                            if i == 2 and projects and h < HG - 1:
                                if h == 0:
                                    dve.wait_ge(vs_done, b + 1)
                                    dve.wait_ge(z_lo_done, 3 * q + 9)
                                take_proj(b + 1, (0, 1, 3)[h])
                            if i == 3 and projects and h == 1:
                                take_proj(b + 1, 2)
                            if h == 1 and i == 3 and back2:
                                take_o(q - 2, (g + 2) % NG1)
                            if h == HG - 1:
                                if i == 1 and more1:
                                    take_n(q + 1, (g + 1) % NG1)
                                if g == 1 and not first and i == 3:
                                    split_ot(b - 1)
                                if g == 2 and not first:
                                    take_out(b - 1, i)

                dve.memset(inv[:], 0.0).then_inc(max_done, 1)
                dve.wait_ge(bias_in, 32)
                dve.tensor_scalar(bqkv[:, 0:C], bqkv[:, 0:C], 0.25, None, ALU.mult).then_inc(bias_done, 1)
                dve.wait_ge(w_hi_done, 1)
                dve.scalar_tensor_tensor(out=wq_lo[:, :, 0:C], in0=wq_raw[:, :, 0:C], scalar=0.25,
                                         in1=wq_hi[:, :, 0:C].bitcast(F32), op0=ALU.mult, op1=ALU.subtract).then_inc(w_lo_done, 1)
                dve.wait_ge(w_hi_done, 2)
                dve.tensor_tensor(wq_lo[:, :, C:], wq_raw[:, :, C:], wq_hi[:, :, C:].bitcast(F32), ALU.subtract).then_inc(w_lo_done, 1)
                dve.wait_ge(w_hi_done, 3)
                dve.tensor_tensor(wo_lo[:], wo_raw, wo_hi[:].bitcast(F32), ALU.subtract).then_inc(w_lo_done, 1)
                dve.wait_ge(bias_done, 1)
                for i in range(NT):
                    take_proj(0, i)
                dve.wait_ge(zs_set, 2)
                for h in range(HG):
                    for i in range(NT):
                        maximum(0, 0, h, i)
                split_n(0, 0)
                for i in range(NT):
                    maximum(1, 1, 0, i)
                take_n(0, 0)
                for g in range(NG1):
                    group(0, g, first=True)
                with dve.Fori(1, B - 1) as b:
                    for g in range(NG1):
                        group(b, g)
                for g in range(NG1):
                    group(B - 1, g, last=True)
                for q in (NG1 * B - 2, NG1 * B - 1):
                    take_o(q, q % NG1)
                split_ot(B - 1)
                for i in range(NT):
                    take_out(B - 1, i)

            @block.scalar
            def _(act):
                def exps(q, g, h, i):
                    act.wait_ge(st_done, 16 * q + 4 * h + i + 1)
                    act.activation(pt[:, g % 2, h, i, :], pst[:, i % 2, :], ACT.Exp).then_inc(exp_done, 1)

                def split_z(b, g):
                    q = NG1 * b + g
                    if g == 0:
                        act.wait_ge(qn_done, 2 * NT * b + 2 * NT)
                    act.wait_ge(z_turned, 6 * q)
                    qs = qn[:, :, g * HG * D1:(g + 1) * HG * D1].rearrange("p t (h d) -> p t h d", d=D1)
                    for j in (0, 2):
                        act.copy(zq[:, :, :, j, :], qs).then_inc(z_hi_done, 1)
                    ks = qn[:, :, C + g * HG * D1:C + (g + 1) * HG * D1].rearrange("p t (h e d) -> p t h e d", e=2, d=D1)
                    for e in range(2):
                        dst = zk[:, :, e::2, e * S3:e * S3 + 2 * D1]
                        for j in range(2):
                            last = act.copy(dst[:, :, :, j * D1:(j + 1) * D1], ks[:, :, :, e, :])
                        last.then_inc(z_hi_done, 1)

                def take_stack(q, g, j):
                    act.wait_ge(z_turned, 6 * q + j + 1)
                    if j < 2:
                        act.copy(qb[0:2 * S3, g, j, :], w[0:2 * S3, j % 2, :]).then_inc(stack_done, 1)
                    else:
                        act.copy(kb[:, g, j - 2, :], w[:, j % 2, :]).then_inc(stack_done, 1)

                def take_o(q):
                    act.wait_ge(av_done, q + 1)
                    act.wait_ge(o_turned, q)
                    act.copy(ou[:], po[:]).then_inc(ou_done, 1)

                def pass_v(b):
                    act.wait_ge(qn_done, 2 * NT * b + 2 * NT)
                    act.wait_ge(av_done, NG1 * b)
                    act.copy(vs[:, :, :, 0:D1], qn[:, :, 2 * C:].rearrange("p t (h d) -> p t h d", d=D1)).then_inc(vs_done, 1)

                def turn_on(b, k):
                    act.wait_ge(on_turned, NC * b + k + 1)
                    act.copy(ot_hi[:, k, :], w[:, k, :]).then_inc(ot_hi_done, 1)

                def group(b, g, first=False, last=False):
                    q = NG1 * b + g
                    more2, more3 = (not (last and g + n >= NG1) for n in (2, 3))
                    back2 = not (first and g < 2)
                    for h in range(HG):
                        if h == 0 and g == 1 and not first:
                            pass_v(b)
                        if h == HG - 1 and more3:
                            split_z(b + (g + 3) // NG1, (g + 3) % NG1)
                        for i in range(NT):
                            exps(q, g, h, i)
                            if h == 0 and i == 0 and back2:
                                take_o(q - 2)
                            if h < HG - 1 and i < 2 and more2:
                                take_stack(q + 2, (g + 2) % NG1, 2 * h + i)
                            if h == HG - 1 and g == 1 and not first and i >= 2:
                                turn_on(b - 1, i - 2)

                act.dma_start(wq_raw, io.wqkv1.rearrange("(c p) n -> p c n", p=P)).then_inc(wq_in, 16)
                act.dma_start(wo_raw, io.wo1.rearrange("(c p) n -> p c n", p=P)).then_inc(wo_in, 16)
                act.wait_ge(wq_in, 16)
                act.mul(wq_hi[:, :, 0:C], wq_raw[:, :, 0:C], 0.25).then_inc(w_hi_done, 1)
                act.copy(wq_hi[:, :, C:], wq_raw[:, :, C:]).then_inc(w_hi_done, 1)
                act.wait_ge(wo_in, 16)
                act.copy(wo_hi[:], wo_raw).then_inc(w_hi_done, 1)
                act.wait_ge(w_lo_done, 3)
                act.wait_ge(zs_set, 2 + HG)
                act.wait_ge(vs_set, 2)
                act.copy(ou[:, 0:1], c.ident[:, 0:1]).then_inc(exp_done, 1)
                for g in range(2):
                    split_z(0, g)
                    for j in range(6):
                        take_stack(g, g, j)
                split_z(0, 2)
                pass_v(0)
                for g in range(NG1):
                    group(0, g, first=True)
                with act.Fori(1, B - 1) as b:
                    for g in range(NG1):
                        group(b, g)
                for g in range(NG1):
                    group(B - 1, g, last=True)
                for q in (NG1 * B - 2, NG1 * B - 1):
                    take_o(q)
                for k in range(NC):
                    turn_on(B - 1, k)


def program(nc, io):
    with ExitStack() as ctx:
        m, c = Mem(nc, ctx), Names()
        c.stats1 = m.sb("stats1", [P, B * NT, 6])
        setup_constants(nc, m, c)
        with ExitStack() as inner:
            m0 = Mem(nc, inner)
            load_layer0(nc, m0, c, io)
            layer0(nc, m0, c, io)
        with ExitStack() as inner:
            m1 = Mem(nc, inner)
            c.xt1_hi, c.xt1_lo = (m1.sb(n, [P, NC, B * T], F32R) for n in ("xt1_hi", "xt1_lo"))
            experts(nc, c, io)
        attention1(nc, c, io)


def kernel(**inputs):
    import concourse.bacc as bacc
    from concourse.bass_utils import run_bass_kernel_spmd

    a = {k: np.asarray(v) for k, v in inputs.items()}
    wq, wk = (a[n].reshape(C, NP0, 2, D0 // 2, 2).transpose(0, 1, 2, 4, 3).reshape(C, NP0, 2 * D0)
              for n in ("L0_attn_Wq", "L0_attn_Wk"))
    wv = a["L0_attn_Wv"].reshape(C, NP0, 2 * D0)
    arrays = {
        "x": a["L0_attn_x"],
        "wqkv0": np.concatenate([wq, wk, wv], 2).reshape(C, NP0 * PC0),
        "wo0": a["L0_attn_Wo"],
        "bo0": a["L0_attn_bo"],
        "wg0": a["L0_ffn_w_gate"].T,
        "wu0": a["L0_ffn_w_up"].T,
        "wd0": a["L0_ffn_w_down"].T,
        "rope": rope_tables(),
        "wqkv1": np.concatenate([a["L1_attn_wq"].T, a["L1_attn_wk"].T, a["L1_attn_wv"].T], 1),
        "bqkv1": np.concatenate([a["L1_attn_bq"], a["L1_attn_bk_"], a["L1_attn_bv"]]),
        "wo1": a["L1_attn_wo"].T,
        "bo1": a["L1_attn_bo"],
        "w1": a["L1_ffn_w1"],
        "w3": a["L1_ffn_w3"],
        "w2": a["L1_ffn_w2"],
    }
    nc = bacc.Bacc("TRN2", target_bir_lowering=False, num_devices=1)
    io = Names()
    arrays = {"in_" + k: np.ascontiguousarray(v) for k, v in arrays.items()}
    aps = {k: nc.dram_tensor(k, v.shape, mybir.dt.from_np(v.dtype), kind="ExternalInput").ap() for k, v in arrays.items()}
    (io.x, io.wqkv0, io.wo0, io.bo0, io.wg0, io.wu0, io.wd0, io.rope, io.wqkv1, io.bqkv1, io.wo1, io.bo1,
     io.w1, io.w3, io.w2) = aps.values()
    io.x1 = nc.dram_tensor("x1_scratch", (B, T, C), F32, kind="Internal").ap()
    io.gate1 = nc.dram_tensor("gate1_scratch", (B, T, C), F32, kind="Internal").ap()
    io.xt1_hi = nc.dram_tensor("xt1_hi_scratch", (P, NC, B * T), F32, kind="Internal").ap()
    io.xt1_lo = nc.dram_tensor("xt1_lo_scratch", (P, NC, B * T), F32, kind="Internal").ap()
    io.out = nc.dram_tensor("out_dram", (B, T, C), F32, kind="ExternalOutput").ap()
    program(nc, io)
    r = run_bass_kernel_spmd(nc, [arrays], core_ids=[0])
    return r.results[0]["out_dram"]
```

```python
from contextlib import ExitStack

import numpy as np

import concourse.bass as bass
from concourse import mybir
from concourse.alu_op_type import AluOpType as ALU

ACT = mybir.ActivationFunctionType
AXX = mybir.AxisListType.X
F32 = mybir.dt.float32
F32R = mybir.dt.float32r
BF16 = mybir.dt.bfloat16
I32 = mybir.dt.int32

P = 128
B, T, C = 8, 512, 256
NT = T // P
NC = C // P
EPS = 1e-5

H0, D0 = 16, 64
NP0 = H0 // 2
PC0 = 6 * D0
F0 = 768
NF0 = F0 // P
DEQ = 1.0 / 127.0

H1, D1 = 16, 16
NG1 = 4
E1, F1 = 8, 704
NF1 = (F1 + P - 1) // P
FP1 = NF1 * P
FR1 = F1 - (NF1 - 1) * P
CE = T // E1

SOFF = [0, 128, 384, 768]
PTOFF = [0, 512, 1024, 896]
NEG = -1.0e30


def rope_tables():
    inv = (np.float32(1.0) / np.float32(10000.0) ** (np.arange(0, D0, 2, dtype=np.float32) / np.float32(D0))).astype(np.float32)
    ang = (np.arange(T, dtype=np.float32)[:, None] * inv[None, :]).astype(np.float32).astype(np.float64)
    t = np.stack([np.cos(ang), np.sin(ang), -np.sin(ang)], 1).astype(np.float32)
    return np.ascontiguousarray(t.reshape(NT, P, 3, D0 // 2).transpose(1, 0, 2, 3))


class Names:
    pass


class Mem:

    def __init__(self, nc, ctx):
        self.nc, self.ctx = nc, ctx

    def sb(self, name, shape, dt=F32):
        return self.ctx.enter_context(self.nc.sbuf_tensor(name, shape, dt))

    def ps(self, name, shape, dt=F32):
        return self.ctx.enter_context(self.nc.psum_tensor(name, shape, dt))

    def sem(self, name):
        return self.ctx.enter_context(self.nc.semaphore(name))


def setup_constants(nc, m, c):
    c.ident = m.sb("ident", [P, P])
    c.identb = m.sb("identb", [P, P], BF16)
    c.maskb = m.sb("maskb", [P, P], BF16)
    set_done = m.sem("set_done")
    with nc.Block() as block:
        @block.gpsimd
        def _(pool):
            pool.memset(c.ident[:], 0.0).then_inc(set_done, 1)
            pool.memset(c.identb[:], 0.0).then_inc(set_done, 1)
            pool.memset(c.maskb[:], 0.0).then_inc(set_done, 1)
            pool.wait_ge(set_done, 3)
            for eye in (c.ident, c.identb):
                pool.affine_select(out=eye[:], in_=eye[:], compare_op=ALU.not_equal, fill=1.0, base=0,
                                   pattern=[[-1, P]], channel_multiplier=1).then_inc(set_done, 1)
            pool.affine_select(out=c.maskb[:], in_=c.maskb[:], compare_op=ALU.is_ge, fill=NEG, base=0,
                               pattern=[[-1, P]], channel_multiplier=1).then_inc(set_done, 1)
            pool.wait_ge(set_done, 6)


def load_layer0(nc, m, c, io):
    c.wq_hi = m.sb("wq_hi", [P, NC, NP0 * PC0], F32R)
    c.wq_lo = m.sb("wq_lo", [P, NC, NP0 * PC0], F32R)
    c.wo_hi = m.sb("wo_hi", [P, NP0, C], F32R)
    c.wo_lo = m.sb("wo_lo", [P, NP0, C], F32R)
    c.wg = m.sb("wg", [P, NC, F0], F32R)
    c.wu = m.sb("wu", [P, NC, F0], F32R)
    c.wd = m.sb("wd", [P, NF0, C], F32R)
    c.mean = m.sb("mean", [P, B * NT])
    c.rstd = m.sb("rstd", [P, B * NT])
    c.rope = m.sb("rope", [P, NT, 3, D0 // 2])
    c.bo = m.sb("bo", [P, C])
    with ExitStack() as ctx:
        t = Mem(nc, ctx)
        xa = t.sb("xa", [P, B * NT, C])
        wq_raw = t.sb("wq_raw", [P, NC, NP0 * PC0])
        wo_raw = t.sb("wo_raw", [P, NP0, C])
        wg_int, wu_int, wd_int = (t.sb(n, [P, NC * F0], I32) for n in ("wg_int", "wu_int", "wd_int"))
        stats = t.sb("stats", [P, B * NT, 6])
        aggr = t.sb("aggr", [P, B * NT, 2])
        dev = t.sb("dev", [P, B * NT])
        eps = t.sb("eps", [P, 1])
        x_in = [t.sem(f"x_in{i}") for i in range(2)]
        wq_in = [t.sem(f"wq_in{i}") for i in range(NC)]
        wg_in = t.sem("wg_in")
        wu_in = t.sem("wu_in")
        wd_in = t.sem("wd_in")
        wo_in = t.sem("wo_in")
        small_in = t.sem("small_in")
        int_cast = t.sem("int_cast")
        stats_done = t.sem("stats_done")
        aggr_done = t.sem("aggr_done")
        eps_set = t.sem("eps_set")
        dev_done = t.sem("dev_done")
        rstd_done = t.sem("rstd_done")
        hi_done = t.sem("hi_done")
        lo_done = t.sem("lo_done")

        def flat(w):
            return w[:].rearrange("p c n -> p (c n)")

        with nc.Block() as block:
            @block.sync
            def _(sp):
                xt = io.x.rearrange("b (t p) c -> p (b t) c", p=P)
                wq = io.wqkv0.rearrange("(c p) n -> p c n", p=P)
                half = B * NT // 2
                for i in range(2):
                    sp.dma_start(wq_raw[:, i, :], wq[:, i, :]).then_inc(wq_in[i], 16)
                    sp.dma_start(xa[:, i * half:(i + 1) * half, :], xt[:, i * half:(i + 1) * half, :]).then_inc(x_in[i], 16)
                sp.dma_start(wo_raw[:], io.wo0.rearrange("(c p) n -> p c n", p=P)).then_inc(wo_in, 16)
                for dst, src, n, done in ((wg_int, io.wg0, NC, wg_in), (wu_int, io.wu0, NC, wu_in), (wd_int, io.wd0, NF0, wd_in)):
                    sp.dma_start(dst[:].rearrange("p (c n) -> p c n", c=n), src.rearrange("(c p) n -> p c n", p=P)).then_inc(done, 16)
                sp.dma_start(c.rope[:], io.rope).then_inc(small_in, 16)
                sp.dma_start(c.bo[:], io.bo0.partition_broadcast(P)).then_inc(small_in, 16)
                sp.wait_ge(small_in, 32)

            @block.scalar
            def _(act):
                for i in range(NC):
                    act.wait_ge(wq_in[i], 16)
                    v = wq_raw[:, i, :].rearrange("p (h n) -> p h n", n=PC0)
                    o = c.wq_hi[:, i, :].rearrange("p (h n) -> p h n", n=PC0)
                    act.mul(o[:, :, 0:2 * D0], v[:, :, 0:2 * D0], 1.0 / 8.0).then_inc(hi_done, 1)
                    act.copy(o[:, :, 2 * D0:], v[:, :, 2 * D0:]).then_inc(hi_done, 1)
                act.wait_ge(wo_in, 16)
                act.copy(c.wo_hi[:], wo_raw[:]).then_inc(hi_done, 1)
                act.wait_ge(wg_in, 16)
                act.copy(flat(c.wg), wg_int[:]).then_inc(int_cast, 1)
                act.wait_ge(wu_in, 16)
                act.copy(flat(c.wu), wu_int[:]).then_inc(int_cast, 1)
                act.wait_ge(aggr_done, B * NT)
                act.wait_ge(eps_set, 1)
                act.activation(dev[:], aggr[:, :, 1], ACT.Sqrt, bias=eps[:]).then_inc(dev_done, 1)
                act.wait_ge(wd_in, 16)
                act.copy(flat(c.wd), wd_int[:]).then_inc(int_cast, 1)
                act.wait_ge(int_cast, 3)

            @block.vector
            def _(dve):
                dve.memset(eps[:], EPS).then_inc(eps_set, 1)
                for half in range(2):
                    i = half
                    dve.wait_ge(hi_done, 2 * i + 2)
                    v = wq_raw[:, i, :].rearrange("p (h n) -> p h n", n=PC0)
                    h = c.wq_hi[:, i, :].bitcast(F32).rearrange("p (h n) -> p h n", n=PC0)
                    o = c.wq_lo[:, i, :].rearrange("p (h n) -> p h n", n=PC0)
                    dve.scalar_tensor_tensor(out=o[:, :, 0:2 * D0], in0=v[:, :, 0:2 * D0], scalar=1.0 / 8.0,
                                             in1=h[:, :, 0:2 * D0], op0=ALU.mult, op1=ALU.subtract).then_inc(lo_done, 1)
                    dve.tensor_tensor(o[:, :, 2 * D0:], v[:, :, 2 * D0:], h[:, :, 2 * D0:], ALU.subtract).then_inc(lo_done, 1)
                    dve.wait_ge(x_in[half], 16)
                    for i in range(B * NT // 2 * half, B * NT // 2 * (half + 1)):
                        dve.bn_stats(stats[:, i, :], xa[:, i, :]).then_inc(stats_done, 1)
                for i in range(B * NT):
                    dve.wait_ge(stats_done, i + 1)
                    dve.bn_aggr(aggr[:, i, :], stats[:, i, :]).then_inc(aggr_done, 1)
                dve.wait_ge(aggr_done, B * NT)
                dve.tensor_copy(c.mean[:], aggr[:, :, 0]).then_inc(rstd_done, 1)
                dve.wait_ge(hi_done, 2 * NC + 1)
                dve.tensor_tensor(c.wo_lo[:], wo_raw[:], c.wo_hi[:].bitcast(F32), ALU.subtract).then_inc(lo_done, 1)
                dve.wait_ge(dev_done, 1)
                dve.reciprocal(c.rstd[:], dev[:]).then_inc(rstd_done, 1)
                dve.wait_ge(rstd_done, 2)
                dve.wait_ge(lo_done, 2 * NC + 1)


def layer0(nc, m, c, io):
    with ExitStack() as ctx:
        t = Mem(nc, ctx)
        x = t.sb("x", [P, 2 * NT, C])
        xn = t.sb("xn", [P, NT, C])
        xt_hi = t.sb("xt_hi", [P, NC, T], F32R)
        xt_lo = t.sb("xt_lo", [P, NC, T], F32R)
        ho_hi = t.sb("ho_hi", [P, NP0, T], F32R)
        ho_lo = t.sb("ho_lo", [P, NP0, T], F32R)
        gate = t.sb("gate", [P, NT, C])
        spare = t.sb("spare", [P, 1])
        ra = t.sb("ra", [P, 2, 4 * D0])
        rb = t.sb("rb", [P, 2, 4 * D0])
        qk = t.sb("qk", [P, NT, 4 * D0])
        qs = t.sb("qs", [P, 2, T], F32R)
        k1 = t.sb("k1", [P, 2, T], F32R)
        k2 = t.sb("k2", [P, 2, T], F32R)
        pr = t.sb("pr", [P, 2, 1280])
        sg, hid = (pr[:, h, 0:2 * T].rearrange("p (s t) -> p s t", s=2) for h in range(2))
        pt = t.sb("pt", [P, 2, 1280])
        v_ring = t.sb("v_ring", [P, 4 * NT, 2 * D0])
        v_cur = t.sb("v_cur", [P, NT, 2 * D0])
        nmax = t.sb("nmax", [P, 2, NT])
        rsum = t.sb("rsum", [P, 2, NT])
        rinv = t.sb("rinv", [P, 2, NT])
        so = t.sb("so", [P, 2, C])
        sc = t.ps("sc", [P, 3, 512])
        po = t.ps("po", [P, 512])
        w = t.ps("w", [P, 4, 512])
        x_loaded = t.sem("x_loaded")
        x1_stored = t.sem("x1_stored")
        x1_ready = t.sem("x1_ready")
        xn_ready = t.sem("xn_ready")
        xn_turned = t.sem("xn_turned")
        xt_hi_done = t.sem("xt_hi_done")
        xt_lo_done = t.sem("xt_lo_done")
        gate_up_done = t.sem("gate_up_done")
        silu_done = t.sem("silu_done")
        hid_done = t.sem("hid_done")
        hid_hi_done = t.sem("hid_hi_done")
        hid_lo_done = t.sem("hid_lo_done")
        down_done = t.sem("down_done")
        g_done = t.sem("g_done")
        gate_done = t.sem("gate_done")
        proj_done = t.sem("proj_done")
        v_done = t.sem("v_done")
        v_cur_done = t.sem("v_cur_done")
        rope_mult = t.sem("rope_mult")
        rope_done = t.sem("rope_done")
        qk_turned = t.sem("qk_turned")
        stack_hi = t.sem("stack_hi")
        stack_lo = t.sem("stack_lo")
        hi_copied = t.sem("hi_copied")
        lo_copied = t.sem("lo_copied")
        s_done = t.sem("s_done")
        max_done = t.sem("max_done")
        exp_done = t.sem("exp_done")
        rinv_done = t.sem("rinv_done")
        inverse_seen = t.sem("inverse_seen")
        scaled = t.sem("scaled")
        p_turned = t.sem("p_turned")
        pt_a_copied = t.sem("pt_a_copied")
        pt_b_copied = t.sem("pt_b_copied")
        av_done = t.sem("av_done")
        o_hi_done = t.sem("o_hi_done")
        o_lo_done = t.sem("o_lo_done")
        wo_done = t.sem("wo_done")
        so_done = t.sem("so_done")
        mul_done = t.sem("mul_done")
        stats1_done = t.sem("stats1_done")

        SLOT = (3, 0, 3, 0)
        FOUR = (3, 0, 1, 2)
        HALF = (slice(0, D0), slice(D0, 2 * D0))

        def score(i):
            return (0, 256 * i) if i < 2 else (i - 1, 0)

        x_dram = io.x.rearrange("b (t p) c -> p b t c", p=P)
        x1_dram = io.x1.rearrange("b (t p) c -> p b t c", p=P)

        with nc.Block() as block:
            @block.sync
            def _(sp):
                sp.dma_start(x[:, 0:NT, :], x_dram[:, 0]).then_inc(x_loaded, 16)
                with sp.Fori(0, B - 1) as b:
                    sp.wait_ge(x_loaded, 16 * b + 16)
                    sp.wait_ge(x1_stored, 16 * b + 16)
                    sp.wait_ge(stats1_done, NT * b + NT)
                    sp.dma_start(x[:, bass.ds((b + 1) % 2 * NT, NT), :], x_dram[:, bass.ds(b + 1, 1)].rearrange("p o t c -> p (o t) c")).then_inc(x_loaded, 16)
                    sp.wait_ge(x1_ready, NT * b + NT)
                    sp.dma_start(x1_dram[:, bass.ds(b, 1)].rearrange("p o t c -> p (o t) c"), x[:, bass.ds(b % 2 * NT, NT), :]).then_inc(x1_stored, 16)
                sp.wait_ge(x1_ready, NT * B)
                sp.wait_ge(x1_stored, 16 * B)
                sp.dma_start(x1_dram[:, B - 1], x[:, (B - 1) % 2 * NT:(B - 1) % 2 * NT + NT, :]).then_inc(x1_stored, 16)
                sp.wait_ge(x1_stored, 16 * B + 16)

            @block.tensor
            def _(pe):
                def turn_x(b, k):
                    for i in range(NT):
                        pe.wait_ge(xn_ready, NT * b + i + 1)
                        mm = pe.transpose(w[:, SLOT[k], i * P:(i + 1) * P], xn[:, i, k * P:(k + 1) * P], c.ident[:])
                    mm.then_inc(xn_turned, 1)

                def gate_up(b):
                    for f in range(NF0):
                        for j, wt in enumerate((c.wg, c.wu)):
                            bank = (3 + 2 * f + j) % 4
                            if f < 2:
                                pe.wait_ge(so_done, NT * b + 2 * f + j + 1)
                                if f == 0:
                                    pe.wait_ge(rope_mult, NT * NP0 * b + 3 + j)
                            elif j == 0:
                                pe.wait_ge(silu_done, NF0 * b + f - 1)
                            else:
                                pe.wait_ge(hid_done, NF0 * b + f - 1)
                            for k in range(NC):
                                for q, xt in enumerate((xt_hi, xt_lo)):
                                    mm = pe.matmul(w[:, bank, :], wt[:, k, f * P:(f + 1) * P], xt[:, k, :],
                                                   start=(k == 0 and q == 0), stop=(k == NC - 1 and q == 1))
                            mm.then_inc(gate_up_done, 1)

                def down(b):
                    for i in range(NT):
                        pe.wait_ge(rope_mult, NT * (NP0 * b + 1) + i + 1)
                        for f in range(NF0):
                            if i == 0:
                                pe.wait_ge(hid_hi_done, NF0 * b + f + 1)
                                pe.wait_ge(hid_lo_done, NF0 * b + f + 1)
                            for q, hh in enumerate((ho_hi, ho_lo)):
                                mm = pe.matmul(w[:, FOUR[i], 0:C], hh[:, f, i * P:(i + 1) * P], c.wd[:, f, :],
                                               start=(f == 0 and q == 0), stop=(f == NF0 - 1 and q == 1))
                        mm.then_inc(down_done, 1)

                def project(hp, i, bank):
                    cols = bass.ds(hp * PC0, PC0)
                    for k in range(NC):
                        xh, xl = (a[:, k, i * P:(i + 1) * P] for a in (xt_hi, xt_lo))
                        pe.matmul(w[:, bank, 0:PC0], xh, c.wq_hi[:, k, cols], start=(k == 0), stop=False)
                        pe.matmul(w[:, bank, 0:PC0], xh, c.wq_lo[:, k, cols], start=False, stop=False)
                        mm = pe.matmul(w[:, bank, 0:PC0], xl, c.wq_hi[:, k, cols], start=False, stop=(k == NC - 1))
                    mm.then_inc(proj_done, 1)

                def turn_qk(n, j, banks):
                    if j == 0:
                        pe.wait_ge(rope_done, NT * n + 5)
                    for i in range(NT):
                        mm = pe.transpose(banks[:, 1 + j, i * P:(i + 1) * P], qk[:, i, j * P:(j + 1) * P], c.ident[:])
                    mm.then_inc(qk_turned, 1)

                def scores(n, h):
                    pe.wait_ge(hi_copied, 2 * n + h + 1)
                    pe.wait_ge(lo_copied, 2 * n + h + 1)
                    for i in range(NT):
                        bank, at = score(i)
                        pe.wait_ge(exp_done, 8 * n + 4 * h + (2, 2, 3, 4)[i])
                        width = max(256, (i + 1) * P)
                        q = qs[:, h, i * P:(i + 1) * P]
                        out = sc[:, bank, at:at + width]
                        pe.matmul(out, q, k1[:, h, 0:width], start=True, stop=False)
                        pe.matmul(out, q, k2[:, h, 0:width], start=False, stop=False)
                        pe.matmul(sc[:, bank, at + i * P:at + (i + 1) * P], c.identb[:], c.maskb[:],
                                  start=False, stop=True).then_inc(s_done, 1)

                def turn_p(n, h, j):
                    if j == 2 - 2 * h:
                        pe.wait_ge(scaled, 8 * n + 4 * h + 4)
                    tile = ([(0, i, i * P) for i in range(4)],
                            [(1, i, (i - 1) * P) for i in range(1, 4)] + [(3, 3, 3 * P)],
                            [(2, i, (i - 2) * P) for i in range(2, 4)])[j]
                    for kt, i, at in tile:
                        mm = pe.transpose(w[:, 1 - h + j, at:at + P],
                                          pr[:, h, SOFF[i] + kt * P:SOFF[i] + (kt + 1) * P], c.ident[:])
                    mm.then_inc(p_turned, 1)

                def weigh(n):
                    pe.wait_ge(pt_a_copied, 3 * n + 3)
                    pe.wait_ge(pt_b_copied, 3 * n + 3)
                    pe.wait_ge(v_cur_done, n + 1)
                    pe.wait_ge(o_lo_done, n + 1)
                    for kt in range(NT):
                        for h in range(2):
                            mm = pe.matmul(po[h * D0:(h + 1) * D0, kt * P:T], v_cur[:, kt, h * D0:(h + 1) * D0],
                                           pt[:, h, PTOFF[kt]:PTOFF[kt] + T - kt * P], start=(kt == 0), stop=(kt == NT - 1))
                    mm.then_inc(av_done, 1)

                def pair(b, hp, slot="project", turn=True, first=False):
                    n = b * NP0 + hp
                    if first:
                        pe.wait_ge(stack_lo, 4 * n + 4)
                    scores(n, 0)
                    if not first:
                        if slot == "next_row":
                            pe.wait_ge(xt_lo_done, NC * (b + 1) + 2)
                        elif slot is None and not turn:
                            pe.wait_ge(pt_b_copied, 3 * n - 5)
                        else:
                            pe.wait_ge(rope_mult, NT * (n + 1) + 4)
                        turn_p(n - 1, 1, 0)
                        for j in (1, 2):
                            pe.wait_ge(pt_a_copied, 3 * n - 2 + j)
                            turn_p(n - 1, 1, j)
                    for i in range(2):
                        if slot is None:
                            continue
                        if first:
                            pe.wait_ge(g_done, NT * b + i + 1)
                        elif i == 0:
                            pe.wait_ge(pt_a_copied, 3 * n - 2)
                        else:
                            pe.wait_ge(pt_b_copied, 3 * n - 2)
                        if slot == "project":
                            project(hp + 2, i, SLOT[i])
                        elif slot == "turn_x":
                            turn_x(b + 1, i)
                        else:
                            project(0, i, SLOT[i])
                    scores(n, 1)
                    if turn:
                        for j in range(2):
                            if first:
                                pe.wait_ge(g_done, NT * b + j + 3)
                            else:
                                pe.wait_ge(pt_b_copied, 3 * n - 1 + j)
                            turn_qk(n + 1, j, w)
                    for i in range(2, NT):
                        if slot == "project":
                            pe.wait_ge(rope_mult, NT * (n + 2) + i - 1)
                            project(hp + 2, i, SLOT[i])
                        elif slot == "next_row":
                            pe.wait_ge(rope_mult, NT * (n + 1) + i - 1)
                            project(0, i, SLOT[i])
                    if not first:
                        weigh(n - 1)
                    for j in (2, 0, 1):
                        if j < 2 and turn:
                            pe.wait_ge(stack_lo, 4 * (n + 1) + 3 + j)
                        elif j < 2:
                            pe.wait_ge(pt_b_copied, 3 * n - 1 + j)
                        elif slot == "project":
                            pe.wait_ge(rope_mult, NT * (n + 2) + 3)
                        elif slot == "next_row":
                            pe.wait_ge(rope_mult, NT * (n + 1) + 3)
                        elif slot == "turn_x":
                            pe.wait_ge(xt_lo_done, NC * (b + 1) + 1)
                        else:
                            pe.wait_ge(pt_a_copied, 3 * n - 2)
                        turn_p(n, 0, j)

                def out_project(i, pairs):
                    for k in pairs:
                        oh, ol = (a[:, k, i * P:(i + 1) * P] for a in (ho_hi, ho_lo))
                        pe.matmul(w[:, FOUR[i], 0:C], oh, c.wo_hi[:, k, :], start=(k == 0), stop=False)
                        pe.matmul(w[:, FOUR[i], 0:C], oh, c.wo_lo[:, k, :], start=False, stop=False)
                        mm = pe.matmul(w[:, FOUR[i], 0:C], ol, c.wo_hi[:, k, :], start=False, stop=(k == NP0 - 1))
                    if NP0 - 1 in pairs:
                        mm.then_inc(wo_done, 1)

                def row(b, last=False):
                    gate_up(b)
                    n = b * NP0
                    pe.wait_ge(exp_done, 8 * n + 4)
                    for j in range(2):
                        turn_qk(n, j, sc)
                    for i in range(NT):
                        pe.wait_ge((silu_done, hid_done)[i % 2], NF0 * b + 5 + i // 2)
                        project(1, i, FOUR[i])
                    down(b)
                    pair(b, 0, first=True)
                    with pe.Fori(1, NP0 - 2) as hp:
                        pair(b, hp)
                    pair(b, NP0 - 2, slot=None if last else "turn_x")
                    if not last:
                        pe.wait_ge(xt_hi_done, NC * (b + 2))
                        pe.wait_ge(xt_lo_done, NC * (b + 2))
                    pair(b, NP0 - 1, slot=None if last else "next_row", turn=False)
                    n = b * NP0 + NP0 - 1
                    if last:
                        pe.wait_ge(pt_b_copied, 3 * n - 2)
                    else:
                        pe.wait_ge(rope_mult, NT * (n + 1) + 4)
                    turn_p(n, 1, 0)
                    for j in (1, 2):
                        pe.wait_ge(pt_a_copied, 3 * n + 1 + j)
                        turn_p(n, 1, j)
                    early = range(NP0 - 1)
                    pe.wait_ge(pt_a_copied, 3 * n + 1)
                    pe.wait_ge(o_lo_done, n + 1)
                    out_project(0, early)
                    weigh(n)
                    out_project(1, early)
                    pe.wait_ge(o_lo_done, n + 2)
                    for i in range(2):
                        out_project(i, range(NP0 - 1, NP0))
                    for i in range(2, NT):
                        out_project(i, range(NP0))

                for k in range(NC):
                    turn_x(0, k)
                pe.wait_ge(xt_hi_done, NC)
                pe.wait_ge(xt_lo_done, NC)
                for i in range(NT):
                    if i > 1:
                        pe.wait_ge(rope_mult, i - 1)
                    project(0, i, SLOT[i])
                with pe.Fori(0, B - 1) as b:
                    row(b)
                row(B - 1, last=True)

            @block.scalar
            def _(act):
                def exps(n, h):
                    for i in range(NT):
                        act.wait_ge(max_done, 8 * n + 4 * h + (2, 2, 3, 4)[i])
                        bank, at = score(i)
                        act.activation(pr[:, h, SOFF[i]:SOFF[i] + (i + 1) * P], sc[:, bank, at:at + (i + 1) * P], ACT.Exp,
                                       bias=nmax[:, h, i:i + 1], accum_out=rsum[:, h, i:i + 1]).then_inc(exp_done, 1)

                def turn_x(b):
                    for k in range(NC):
                        act.wait_ge(xn_turned, NC * b + k + 1)
                        act.copy(xt_hi[:, k, :], w[:, SLOT[k], :]).then_inc(xt_hi_done, 1)

                def take_v(n, hp, i, bank):
                    act.wait_ge(proj_done, NT * n + i + 1)
                    act.copy(v_ring[:, bass.ds(hp % 4 * NT + i, 1), :].rearrange("p o d -> p (o d)"), w[:, bank, 4 * D0:PC0]).then_inc(v_done, 1)

                def take_qk(n, h, banks=w):
                    own, other = HALF[h], HALF[1 - h]
                    act.wait_ge(qk_turned, 2 * n + 2)
                    if h == 1:
                        act.wait_ge(stack_lo, 4 * n + 1)
                    act.copy(qs[own, h, :], banks[own, 1, :]).then_inc(stack_hi, 1)
                    act.wait_ge(qk_turned, 2 * n + 3)
                    if h == 1:
                        act.wait_ge(stack_lo, 4 * n + 2)
                    act.copy(k1[own, h, :], banks[own, 2, :]).then_inc(stack_hi, 1)

                def copy_half(n, h):
                    act.wait_ge(stack_hi, 4 * n + 2 * h + 2)
                    act.copy(k2[HALF[1 - h], h, :], k1[HALF[h], h, :].bitcast(F32)).then_inc(hi_copied, 1)

                def take_o(n, hp):
                    act.wait_ge(av_done, n + 2)
                    act.copy(ho_hi[:, bass.ds(hp, 1), :].rearrange("p o t -> p (o t)"), po[:, :]).then_inc(o_hi_done, 1)

                def pass_v(n, hp):
                    act.wait_ge(av_done, n + 1)
                    act.wait_ge(v_done, NT * n + NT)
                    act.copy(v_cur[:], v_ring[:, bass.ds(hp % 4 * NT, NT), :]).then_inc(v_cur_done, 1)

                def take_p(n):
                    for turn, (bank, at, width) in enumerate(((3, 1024, 256), (1, 0, 512), (2, 512, 512))):
                        act.wait_ge(p_turned, 6 * n + turn + 1)
                        act.copy(pt[:, 0, at:at + width], w[:, bank, 0:width]).then_inc(pt_a_copied, 1)

                def pair(b, hp, slot="project", turn=True, first=False):
                    n = b * NP0 + hp
                    ahead = (n + 2, hp + 2) if slot == "project" else (n + 1, 0)
                    exps(n, 0)
                    if slot == "turn_x":
                        turn_x(b + 1)
                    elif slot:
                        for i in range(2):
                            take_v(*ahead, i, SLOT[i])
                    if not first:
                        pass_v(n - 1, hp - 1)
                    if turn:
                        take_qk(n + 1, 0)
                    if slot == "project" or slot == "next_row":
                        take_v(*ahead, 2, SLOT[2])
                    exps(n, 1)
                    if turn:
                        take_qk(n + 1, 1)
                    if slot == "project" or slot == "next_row":
                        take_v(*ahead, 3, SLOT[3])
                    if turn:
                        copy_half(n + 1, 0)
                    if turn:
                        copy_half(n + 1, 1)
                    if not first:
                        take_o(n - 1, hp - 1)
                    take_p(n)

                def row(b, last=False):
                    n = b * NP0
                    for f in range(NF0 + 1):
                        if f < NF0:
                            act.wait_ge(gate_up_done, 2 * NF0 * b + 2 * f + 1)
                            if f > 1:
                                act.wait_ge(hid_done, NF0 * b + f - 1)
                            act.activation(sg[:, f % 2, :], w[:, (3 + 2 * f) % 4, :], ACT.Silu, scale=DEQ).then_inc(silu_done, 1)
                        if f > 0:
                            act.wait_ge(hid_done, NF0 * b + f)
                            act.copy(ho_hi[:, f - 1, :], hid[:, (f - 1) % 2, :]).then_inc(hid_hi_done, 1)
                    take_qk(n, 0, sc)
                    for i in range(2):
                        take_v(n + 1, 1, i, FOUR[i])
                    take_qk(n, 1, sc)
                    for i in range(2, NT):
                        take_v(n + 1, 1, i, FOUR[i])
                    copy_half(n, 0)
                    copy_half(n, 1)
                    act.activation(spare[:], c.ident[:, 0:1], ACT.Exp)
                    for i in range(NT):
                        act.wait_ge(down_done, NT * b + i + 1)
                        act.copy(gate[:, i, :], w[:, FOUR[i], 0:C]).then_inc(g_done, 1)
                    pair(b, 0, first=True)
                    with act.Fori(1, NP0 - 2) as hp:
                        pair(b, hp)
                    pair(b, NP0 - 2, slot=None if last else "turn_x")
                    pair(b, NP0 - 1, slot=None if last else "next_row", turn=False)
                    pass_v(b * NP0 + NP0 - 1, NP0 - 1)
                    take_o(b * NP0 + NP0 - 1, NP0 - 1)
                    act.wait_ge(g_done, NT * b + NT)
                    act.activation(gate[:], gate[:], ACT.Silu, scale=DEQ).then_inc(gate_done, 1)

                act.copy(nmax[:, 0, 0:1], c.ident[:, 0:1]).then_inc(exp_done, 4)
                turn_x(0)
                for i in range(NT):
                    take_v(0, 0, i, SLOT[i])
                with act.Fori(0, B - 1) as b:
                    row(b)
                row(B - 1, last=True)

            @block.vector
            def _(dve):
                def norm(b):
                    dve.wait_ge(x_loaded, 16 * b + 16)
                    for i in range(NT):
                        dve.tensor_scalar(xn[:, i, :], x[:, bass.ds(b % 2 * NT + i, 1), :].rearrange("p o c -> p (o c)"),
                                          c.mean[:, bass.ds(b * NT + i, 1)], c.rstd[:, bass.ds(b * NT + i, 1)],
                                          ALU.subtract, ALU.mult).then_inc(xn_ready, 1)

                def turn_x(b):
                    for k in range(NC):
                        dve.wait_ge(xt_hi_done, NC * b + k + 1)
                        dve.tensor_tensor(xt_lo[:, k, :], w[:, SLOT[k], :], xt_hi[:, k, :].bitcast(F32), ALU.subtract).then_inc(xt_lo_done, 1)

                def maxima(n, h):
                    for i in range(NT):
                        bank, at = score(i)
                        dve.wait_ge(s_done, 8 * n + 4 * h + (2, 2, 3, 4)[i])
                        dve.tensor_reduce(nmax[:, h, i:i + 1], sc[:, bank, at:at + (i + 1) * P], AXX, ALU.max,
                                          negate=True).then_inc(max_done, 1)

                def take_p(n):
                    for j, (at, width) in enumerate(((0, 512), (512, 512), (1024, 256))):
                        dve.wait_ge(p_turned, 6 * n + 3 + j + 1)
                        dve.tensor_copy(pt[:, 1, at:at + width], w[:, j, 0:width]).then_inc(pt_b_copied, 1)

                def invert(n, h):
                    dve.wait_ge(exp_done, 8 * n + 4 * h + 8)
                    dve.reciprocal(rinv[:, h, :], rsum[:, h, :]).then_inc(rinv_done, 1)

                def rope(n, i, bank):
                    dve.wait_ge(v_done, NT * n + i + 1)
                    dve.wait_ge(rope_done, NT * n + i)
                    src = w[:, bank, 0:4 * D0].rearrange("p (s e d) -> p s e d", s=4, e=2)
                    a = ra[:, i % 2, :].rearrange("p (s d) -> p s d", d=D0 // 2)
                    r = rb[:, i % 2, :].rearrange("p (s e d) -> p s e d", s=4, e=2)
                    dve.tensor_tensor(a, w[:, bank, 0:4 * D0].rearrange("p (s d) -> p s d", d=D0 // 2),
                                      c.rope[:, i, 0, :].unsqueeze(1).to_broadcast([P, 8, D0 // 2]), ALU.mult)
                    dve.tensor_tensor(r[:, :, 0, :], src[:, :, 1, :],
                                      c.rope[:, i, 2, :].unsqueeze(1).to_broadcast([P, 4, D0 // 2]), ALU.mult)
                    dve.tensor_tensor(r[:, :, 1, :], src[:, :, 0, :],
                                      c.rope[:, i, 1, :].unsqueeze(1).to_broadcast([P, 4, D0 // 2]), ALU.mult).then_inc(rope_mult, 1)

                def take_qk(n, h, banks=w):
                    own, other = HALF[h], HALF[1 - h]
                    dve.wait_ge(stack_hi, 4 * n + 2 * h + 1)
                    dve.tensor_tensor(qs[other, h, :], banks[own, 1, :], qs[own, h, :].bitcast(F32), ALU.subtract).then_inc(stack_lo, 1)
                    dve.wait_ge(stack_hi, 4 * n + 2 * h + 2)
                    dve.tensor_tensor(k2[own, h, :], banks[own, 2, :], k1[own, h, :].bitcast(F32), ALU.subtract).then_inc(stack_lo, 1)

                def copy_half(n, h):
                    dve.wait_ge(stack_lo, 4 * n + 2 * h + 2)
                    dve.tensor_copy(k1[HALF[1 - h], h, :], k2[HALF[h], h, :].bitcast(F32)).then_inc(lo_copied, 1)

                def take_o(n, hp):
                    dve.wait_ge(o_hi_done, n + 1)
                    at = bass.ds(hp, 1)
                    dve.tensor_tensor(ho_lo[:, at, :].rearrange("p o t -> p (o t)"), po[:, :],
                                      ho_hi[:, at, :].bitcast(F32).rearrange("p o t -> p (o t)"), ALU.subtract).then_inc(o_lo_done, 1)

                def pair(b, hp, slot="project", turn=True, first=False):
                    n = b * NP0 + hp
                    ahead = n + 2 if slot == "project" else n + 1
                    maxima(n, 0)
                    if not first:
                        take_p(n - 1)
                    invert(n, 0)
                    if slot == "turn_x":
                        turn_x(b + 1)
                    elif slot:
                        for i in range(2):
                            rope(ahead, i, SLOT[i])
                    maxima(n, 1)
                    if turn:
                        take_qk(n + 1, 0)
                    if slot == "project" or slot == "next_row":
                        rope(ahead, 2, SLOT[2])
                    invert(n, 1)
                    if turn:
                        take_qk(n + 1, 1)
                        copy_half(n + 1, 0)
                        copy_half(n + 1, 1)
                    if slot == "project" or slot == "next_row":
                        rope(ahead, 3, SLOT[3])
                    if not first:
                        take_o(n - 1, hp - 1)

                def stats(b, i):
                    dve.wait_ge(x1_ready, NT * b + NT)
                    dve.bn_stats(c.stats1[:, bass.ds(b * NT + i, 1), :].rearrange("p o s -> p (o s)"), x[:, bass.ds(b % 2 * NT + i, 1), :].rearrange("p o c -> p (o c)")).then_inc(stats1_done, 1)

                def row(b, first=False, last=False):
                    n = b * NP0
                    for f in range(NF0 + 1):
                        if f < NF0:
                            dve.wait_ge(silu_done, NF0 * b + f + 1)
                            dve.wait_ge(gate_up_done, 2 * NF0 * b + 2 * f + 2)
                            dve.scalar_tensor_tensor(out=hid[:, f % 2, :], in0=w[:, (4 + 2 * f) % 4, :], scalar=DEQ,
                                                     in1=sg[:, f % 2, :], op0=ALU.mult, op1=ALU.mult).then_inc(hid_done, 1)
                        if f > 0:
                            dve.wait_ge(hid_hi_done, NF0 * b + f)
                            dve.tensor_tensor(ho_lo[:, f - 1, :], hid[:, (f - 1) % 2, :],
                                              ho_hi[:, f - 1, :].bitcast(F32), ALU.subtract).then_inc(hid_lo_done, 1)
                            dve.wait_ge(hid_lo_done, NF0 * b + f)
                        if f > 2 and not first:
                            stats(b - 1, f - 3)
                    take_qk(n, 0, sc)
                    for i in range(2):
                        rope(n + 1, i, FOUR[i])
                    take_qk(n, 1, sc)
                    for i in range(2, NT):
                        rope(n + 1, i, FOUR[i])
                    copy_half(n, 0)
                    copy_half(n, 1)
                    pair(b, 0, first=True)
                    if not last:
                        norm(b + 1)
                    with dve.Fori(1, NP0 - 2) as hp:
                        pair(b, hp)
                    pair(b, NP0 - 2, slot=None if last else "turn_x")
                    pair(b, NP0 - 1, slot=None if last else "next_row", turn=False)
                    n = b * NP0 + NP0 - 1
                    take_p(n)
                    take_o(n, NP0 - 1)
                    for i in range(NT):
                        dve.wait_ge(wo_done, NT * b + i + 1)
                        if i > 1:
                            dve.wait_ge(mul_done, NT * b + i - 1)
                            dve.wait_ge(x1_ready, NT * b + i - 1)
                        dve.tensor_tensor(so[:, i % 2, :], w[:, FOUR[i], 0:C], c.bo[:], ALU.add).then_inc(so_done, 1)

                norm(0)
                turn_x(0)
                for i in range(NT):
                    rope(0, i, SLOT[i])
                row(0, first=True)
                with dve.Fori(1, B - 1) as b:
                    row(b)
                row(B - 1, last=True)
                for i in range(NT):
                    stats(B - 1, i)
                dve.wait_ge(stats1_done, NT * B + NT)

            @block.gpsimd
            def _(pool):
                def scale(n, h):
                    pool.wait_ge(rinv_done, 2 * n + h + 1)
                    pool.sem_inc(inverse_seen, 1)
                    for i in range(NT):
                        p = pr[:, h, SOFF[i]:SOFF[i] + (i + 1) * P]
                        pool.tensor_scalar(p, p, rinv[:, h, i:i + 1], 1.0, ALU.mult, ALU.mult).then_inc(scaled, 1)

                def rotate(n, i):
                    pool.wait_ge(rope_mult, NT * n + i + 1)
                    if i % 2 == 0:
                        pool.wait_ge(qk_turned, 2 * n + 1)
                    pool.tensor_tensor(qk[:, i, :], ra[:, i % 2, :], rb[:, i % 2, :], ALU.add).then_inc(rope_done, 1)

                def pair(b, hp, slot="project"):
                    n = b * NP0 + hp
                    ahead = n + 2 if slot == "project" else n + 1
                    projects = slot == "project" or slot == "next_row"
                    scale(n, 0)
                    if projects:
                        rotate(ahead, 0)
                        rotate(ahead, 1)
                    scale(n, 1)
                    if projects:
                        rotate(ahead, 2)
                        rotate(ahead, 3)

                def row(b, last=False):
                    n = b * NP0
                    for i in range(NT):
                        rotate(n + 1, i)
                    pair(b, 0)
                    with pool.Fori(1, NP0 - 2) as hp:
                        pair(b, hp)
                    pair(b, NP0 - 2, slot=None if last else "turn_x")
                    pair(b, NP0 - 1, slot=None if last else "next_row")
                    for i in range(NT):
                        pool.wait_ge(so_done, NT * b + i + 5)
                        pool.wait_ge(gate_done, b + 1)
                        pool.tensor_tensor(so[:, i % 2, :], so[:, i % 2, :], gate[:, i, :], ALU.mult).then_inc(mul_done, 1)
                        pool.wait_ge(mul_done, NT * b + i + 1)
                        xi = x[:, bass.ds(b % 2 * NT + i, 1), :].rearrange("p o c -> p (o c)")
                        pool.tensor_tensor(xi, xi, so[:, i % 2, :], ALU.add).then_inc(x1_ready, 1)

                pool.sem_inc(x1_stored, 16)
                pool.sem_inc(stats1_done, NT)
                pool.sem_inc(so_done, 4)
                pool.sem_inc(rope_done, 1)
                pool.sem_inc(qk_turned, 1)
                pool.sem_inc(av_done, 1)
                pool.sem_inc(o_lo_done, 1)
                for i in range(NT):
                    rotate(0, i)
                with pool.Fori(0, B - 1) as b:
                    row(b)
                row(B - 1, last=True)


def experts(nc, c, io):
    with ExitStack() as ctx:
        t = Mem(nc, ctx)
        r1, r3 = (t.sb(f"raw{n}", [P, NC, FP1]) for n in (1, 3))
        r2 = t.sb("raw2", [P, NF1, C])
        w1h, w1l, w3h, w3l = (t.sb(n, [P, 2, NC, FP1], F32R) for n in ("w1h", "w1l", "w3h", "w3l"))
        w2h, w2l = (t.sb(n, [P, 2, NF1, C], F32R) for n in ("w2h", "w2l"))
        hh, hl = (t.sb(n, [P, NF1, T], F32R) for n in ("hh", "hl"))
        sg_hid = t.sb("sg_hid", [P, 2, 2, T])
        sg, hid = sg_hid[:, 0], sg_hid[:, 1]
        SPLIT = 3
        rows = [h[:].bitcast(F32).rearrange("p f t -> p (f t)")[:, r * NT * C:(r + 1) * NT * C] for h in (hh, hl) for r in range(3)]
        rows += [sg_hid[:, r].rearrange("p s t -> p (s t)") for r in range(2)]
        xa = [r.rearrange("p (t c) -> p t c", c=C) for r in rows]
        xn = t.sb("xn1", [P, 2, NT, C])
        aggr = t.sb("aggr1", [P, B * NT, 2])
        dev = t.sb("dev1", [P, B * NT])
        rstd = t.sb("rstd1", [P, B * NT])
        shift = t.sb("shift1", [P, B * NT])
        eps = t.sb("eps1", [P, 1])
        go = t.sb("go", [P, NT, C])
        w = t.ps("wx", [P, 4, 512])
        dn = t.ps("dn", [P, 4, 512])
        x_in = [t.sem(f"x1_in{b}") for b in range(B)]
        eps_set = t.sem("eps_set1")
        aggr_done = t.sem("aggr_done1")
        dev_done = t.sem("dev_done1")
        rstd_done = t.sem("rstd_done1")
        xn_act = t.sem("xn_act1")
        xn_dve = t.sem("xn_dve1")
        xn_turned = t.sem("xn_turned1")
        xt_hi_done = t.sem("xt1_hi_done")
        xt_lo_done = t.sem("xt1_lo_done")
        xt_stored = t.sem("xt1_stored")
        w13_in = t.sem("w13_in")
        w2_in = t.sem("w2_in")
        pad_set = t.sem("pad_set")
        hi13 = t.sem("hi13")
        lo13 = t.sem("lo13")
        hi2 = t.sem("hi2")
        lo2 = t.sem("lo2")
        gate_up_done = t.sem("gate_up_done1")
        silu_done = t.sem("silu_done1")
        hid_done = t.sem("hid_done1")
        hid_hi_done = t.sem("hid_hi_done1")
        hid_lo_done = t.sem("hid_lo_done1")
        down_done = t.sem("down_done1")
        g_done = t.sem("g_done1")
        g_stored = t.sem("g_stored")

        with nc.Block() as block:
            @block.sync
            def _(sp):
                full = (NF1 - 1) * P

                def load13(e):
                    one = bass.ds(e, 1)
                    if not (isinstance(e, int) and e == 0):
                        sp.wait_ge(hi13, 2 * e)
                        sp.wait_ge(lo13, 2 * e)
                    sp.dma_start(r1[:, :, 0:F1], io.w1[one].rearrange("o (c p) f -> p (o c) f", p=P)).then_inc(w13_in, 16)
                    sp.dma_start(r3[:, :, 0:F1], io.w3[one].rearrange("o (c p) f -> p (o c) f", p=P)).then_inc(w13_in, 16)

                def load2(e):
                    one = bass.ds(e, 1)
                    if not (isinstance(e, int) and e == 0):
                        sp.wait_ge(hi2, e)
                        sp.wait_ge(lo2, e)
                    sp.dma_start(r2[:, 0:NF1 - 1, :], io.w2[one, 0:full].rearrange("o (f p) n -> p (o f) n", p=P)).then_inc(w2_in, 16)
                    sp.dma_start(r2[0:FR1, NF1 - 1:NF1, :], io.w2[one, full:F1].rearrange("o p n -> p o n")).then_inc(w2_in, 16)

                def load(e):
                    load13(e)
                    load2(e)

                def store(e):
                    for i in range(NT):
                        sp.wait_ge(g_done, NT * e + i + 1)
                        dst = io.gate1.rearrange("b (e k) c -> e b k c", e=E1)[bass.ds(e, 1), 2 * i:2 * i + 2]
                        sp.dma_start(dst.rearrange("o b k c -> (o b) k c"), go[:, i, :]).then_inc(g_stored, 16)

                for b in range(B):
                    sp.dma_start(xa[b], io.x1[b].rearrange("(t p) c -> p t c", p=P)).then_inc(x_in[b], 16)
                    if b == B // 2 - 1:
                        sp.wait_ge(pad_set, 3)
                        load13(0)
                load2(0)
                load(1)
                sp.wait_ge(xt_hi_done, NC * B)
                sp.dma_start(io.xt1_hi, c.xt1_hi[:].bitcast(F32)).then_inc(xt_stored, 16)
                sp.wait_ge(xt_lo_done, NC * B)
                sp.dma_start(io.xt1_lo, c.xt1_lo[:].bitcast(F32)).then_inc(xt_stored, 16)
                with sp.Fori(0, E1 - 2) as e:
                    store(e)
                    load(e + 2)
                store(E1 - 2)
                store(E1 - 1)
                sp.wait_ge(g_stored, 16 * NT * E1)
                sp.wait_ge(xt_stored, 32)

            @block.gpsimd
            def _(pool):
                pool.memset(r2[FR1:P, NF1 - 1, :], 0.0).then_inc(pad_set, 1)
                pool.wait_ge(pad_set, 1)
                pool.memset(r1[:, :, F1:FP1], 0.0).then_inc(pad_set, 1)
                pool.memset(r3[:, :, F1:FP1], 0.0).then_inc(pad_set, 1)
                with pool.Fori(0, E1) as e:
                    for f in range(NF1):
                        pool.wait_ge(hid_hi_done, NF1 * e + f + 1)
                        pool.tensor_tensor(hl[:, f, :], hid[:, f % 2, :], hh[:, f, :].bitcast(F32),
                                           ALU.subtract).then_inc(hid_lo_done, 1)

            @block.scalar
            def _(act):
                def split(e, u, part):
                    if part == 0:
                        act.wait_ge(down_done, NT * (e - 1))
                    if part < 2:
                        act.wait_ge(w13_in, 32 * e + 32)
                        act.copy((w1h, w3h)[part][:, u], (r1, r3)[part][:]).then_inc(hi13, 1)
                    else:
                        act.wait_ge(w2_in, 32 * e + 32)
                        act.copy(w2h[:, u], r2[:]).then_inc(hi2, 1)

                def ffn(e, u, last=False):
                    for f in range(NF1 + 1):
                        if f < NF1:
                            act.wait_ge(gate_up_done, 2 * NF1 * e + 2 * f + 1)
                            if f > 1:
                                act.wait_ge(hid_done, NF1 * e + f - 1)
                            act.activation(sg[:, f % 2, :], w[:, 2 * f % 4, :], ACT.Silu).then_inc(silu_done, 1)
                        if f > 0:
                            act.wait_ge(hid_done, NF1 * e + f)
                            act.copy(hh[:, f - 1, :], hid[:, (f - 1) % 2, :]).then_inc(hid_hi_done, 1)
                        if f in (1, 3, 5) and not last:
                            split(e + 1, 1 - u, f // 2)
                    for i in range(NT):
                        act.wait_ge(down_done, NT * e + i + 1)
                        if i == 0:
                            act.wait_ge(g_stored, 16 * NT * e)
                        act.activation(go[:, i, :], dn[:, i, 0:C], ACT.Silu).then_inc(g_done, 1)

                def turned_hi(b):
                    for k in range(NC):
                        act.wait_ge(xn_turned, NC * b + k + 1)
                        act.copy(c.xt1_hi[:, k, b * T:(b + 1) * T], dn[:, b % 2 * NC + k, :]).then_inc(xt_hi_done, 1)

                act.wait_ge(aggr_done, B * NT)
                act.wait_ge(eps_set, 1)
                act.activation(dev[:], aggr[:, :, 1], ACT.Sqrt, bias=eps[:]).then_inc(dev_done, 1)
                act.wait_ge(rstd_done, 2)
                for b in range(B):
                    act.wait_ge(x_in[b], 16)
                    if b > 1:
                        act.wait_ge(xn_turned, NC * (b - 1))
                    for i in range(NT // 2, NT):
                        at = b * NT + i
                        act.activation(xn[:, b % 2, i, :], xa[b][:, i, :], ACT.Identity, bias=shift[:, at:at + 1],
                                       scale=rstd[:, at:at + 1]).then_inc(xn_act, 1)
                    if b > 0:
                        turned_hi(b - 1)
                    if b == SPLIT:
                        act.wait_ge(pad_set, 3)
                        act.wait_ge(w13_in, 32)
                        act.copy(w1h[:, 0], r1[:]).then_inc(hi13, 1)
                        act.copy(w3h[:, 0], r3[:]).then_inc(hi13, 1)
                turned_hi(B - 1)
                act.wait_ge(w2_in, 32)
                act.copy(w2h[:, 0], r2[:]).then_inc(hi2, 1)
                with act.Fori(0, E1 // 2 - 1) as p:
                    ffn(2 * p, 0)
                    ffn(2 * p + 1, 1)
                ffn(E1 - 2, 0)
                ffn(E1 - 1, 1, last=True)

            @block.vector
            def _(dve):
                def split(e, u, part):
                    if part < 2:
                        dve.wait_ge(hi13, 2 * e + part + 1)
                        hi, lo, raw = ((w1h, w1l, r1), (w3h, w3l, r3))[part]
                        dve.tensor_tensor(lo[:, u], raw[:], hi[:, u].bitcast(F32), ALU.subtract).then_inc(lo13, 1)
                    else:
                        dve.wait_ge(hi2, e + 1)
                        dve.tensor_tensor(w2l[:, u], r2[:], w2h[:, u].bitcast(F32), ALU.subtract).then_inc(lo2, 1)

                def ffn(e, u, last=False):
                    for f in range(NF1):
                        dve.wait_ge(silu_done, NF1 * e + f + 1)
                        dve.wait_ge(gate_up_done, 2 * NF1 * e + 2 * f + 2)
                        if f > 1:
                            dve.wait_ge(hid_lo_done, NF1 * e + f - 1)
                        dve.tensor_tensor(hid[:, f % 2, :], w[:, (2 * f + 1) % 4, :], sg[:, f % 2, :],
                                          ALU.mult).then_inc(hid_done, 1)
                        if f in (2, 4, 5) and not last:
                            split(e + 1, 1 - u, {2: 0, 4: 1, 5: 2}[f])

                dve.memset(eps[:], EPS).then_inc(eps_set, 1)
                for i in range(B * NT):
                    dve.bn_aggr(aggr[:, i, :], c.stats1[:, i, :]).then_inc(aggr_done, 1)
                dve.wait_ge(aggr_done, B * NT)
                dve.wait_ge(dev_done, 1)
                dve.reciprocal(rstd[:], dev[:]).then_inc(rstd_done, 1)
                dve.wait_ge(rstd_done, 1)
                dve.scalar_tensor_tensor(out=shift[:], in0=aggr[:, :, 0], scalar=-1.0, in1=rstd[:],
                                         op0=ALU.mult, op1=ALU.mult).then_inc(rstd_done, 1)

                def turned_lo(b):
                    for k in range(NC):
                        dve.wait_ge(xt_hi_done, NC * b + k + 1)
                        at = slice(b * T, (b + 1) * T)
                        dve.tensor_tensor(c.xt1_lo[:, k, at], dn[:, b % 2 * NC + k, :], c.xt1_hi[:, k, at].bitcast(F32),
                                          ALU.subtract).then_inc(xt_lo_done, 1)

                for b in range(B):
                    dve.wait_ge(x_in[b], 16)
                    if b > 1:
                        dve.wait_ge(xn_turned, NC * (b - 1))
                    for i in range(NT // 2):
                        at = b * NT + i
                        dve.tensor_scalar(xn[:, b % 2, i, :], xa[b][:, i, :], aggr[:, at, 0:1], rstd[:, at:at + 1],
                                          ALU.subtract, ALU.mult).then_inc(xn_dve, 1)
                    if b > 0:
                        turned_lo(b - 1)
                    if b == SPLIT:
                        split(0, 0, 0)
                        split(0, 0, 1)
                turned_lo(B - 1)
                split(0, 0, 2)
                with dve.Fori(0, E1 // 2 - 1) as p:
                    ffn(2 * p, 0)
                    ffn(2 * p + 1, 1)
                ffn(E1 - 2, 0)
                ffn(E1 - 1, 1, last=True)

            @block.tensor
            def _(pe):
                def tokens(xt, k, e):
                    return xt[:, k, :].rearrange("p (b e k) -> p b e k", b=B, e=E1)[:, :, bass.ds(e, 1), :].rearrange("p b o k -> p b (o k)")

                def ffn(e, u):
                    pe.wait_ge(hi13, 2 * e + 2)
                    pe.wait_ge(lo13, 2 * e + 2)
                    for f in range(NF1):
                        cols = slice(f * P, (f + 1) * P)
                        for j, (wh, wl) in enumerate(((w1h, w1l), (w3h, w3l))):
                            if f < 2:
                                pe.wait_ge(silu_done, NF1 * e)
                                pe.wait_ge(hid_done, NF1 * e)
                            elif j == 0:
                                pe.wait_ge(silu_done, NF1 * e + f - 1)
                            else:
                                pe.wait_ge(hid_done, NF1 * e + f - 1)
                            out = w[:, (2 * f + j) % 4, :].rearrange("p (b k) -> p b k", b=B)
                            for k in range(NC):
                                pe.matmul(out, wh[:, u, k, cols], tokens(c.xt1_hi, k, e), start=(k == 0), stop=False)
                                pe.matmul(out, wh[:, u, k, cols], tokens(c.xt1_lo, k, e), start=False, stop=False)
                                mm = pe.matmul(out, wl[:, u, k, cols], tokens(c.xt1_hi, k, e), start=False, stop=(k == NC - 1))
                            mm.then_inc(gate_up_done, 1)
                    pe.wait_ge(hi2, e + 1)
                    pe.wait_ge(lo2, e + 1)
                    pe.wait_ge(g_done, NT * e)
                    for f in range(NF1):
                        pe.wait_ge(hid_hi_done, NF1 * e + f + 1)
                        pe.wait_ge(hid_lo_done, NF1 * e + f + 1)
                        for i in range(NT):
                            a, b = hh[:, f, i * P:(i + 1) * P], hl[:, f, i * P:(i + 1) * P]
                            pe.matmul(dn[:, i, 0:C], a, w2h[:, u, f, :], start=(f == 0), stop=False)
                            pe.matmul(dn[:, i, 0:C], a, w2l[:, u, f, :], start=False, stop=False)
                            mm = pe.matmul(dn[:, i, 0:C], b, w2h[:, u, f, :], start=False, stop=(f == NF1 - 1))
                            if f == NF1 - 1:
                                mm.then_inc(down_done, 1)

                for b in range(B):
                    pe.wait_ge(xn_act, NT // 2 * (b + 1))
                    pe.wait_ge(xn_dve, NT // 2 * (b + 1))
                    if b > 1:
                        pe.wait_ge(xt_lo_done, NC * (b - 1))
                    for k in range(NC):
                        for i in range(NT):
                            mm = pe.transpose(dn[:, b % 2 * NC + k, i * P:(i + 1) * P], xn[:, b % 2, i, k * P:(k + 1) * P], c.ident[:])
                        mm.then_inc(xn_turned, 1)
                pe.wait_ge(xt_hi_done, NC * B)
                pe.wait_ge(xt_lo_done, NC * B)
                with pe.Fori(0, E1 // 2) as p:
                    ffn(2 * p, 0)
                    ffn(2 * p + 1, 1)


def attention1(nc, c, io):
    HG = H1 // NG1
    S3 = 3 * D1
    with ExitStack() as ctx:
        t = Mem(nc, ctx)
        wq_hi, wq_lo = (t.sb(n, [P, NC, 3 * C], F32R) for n in ("wq1_hi", "wq1_lo"))
        wo_hi, wo_lo = (t.sb(n, [P, NC, C], F32R) for n in ("wo1_hi", "wo1_lo"))
        bqkv = t.sb("bqkv1", [P, 3 * C])
        bo = t.sb("bo1_sb", [P, C])
        xs_hi, xs_lo = (t.sb(n, [P, NC, T], F32R) for n in ("xs_hi", "xs_lo"))
        x1 = t.sb("x1_sb", [P, NT, C])
        g1 = t.sb("g1_sb", [P, NT, C])
        qn = t.sb("qn", [P, NT, 3 * C])
        zq = t.sb("zq1", [P, NT, HG, 3, D1], F32R)
        zk = t.sb("zk1", [P, NT, HG, 3, D1], F32R)
        own = t.sb("own", [P, 2])
        sel = t.sb("sel", [P, 2, T])
        qb = t.sb("qb", [P, NG1, 2, T], F32R)
        kb = t.sb("kb", [P, NG1, HG, T], F32R)
        vs = t.sb("vs", [P, NT, H1, 2 * D1])
        pt = t.sb("pt1", [P, 2, HG, NT, T])
        wq_raw = pt[:, 0, 0].rearrange("p t n -> p (t n)")[:, 0:NC * 3 * C].rearrange("p (c n) -> p c n", c=NC)
        wo_raw = pt[:, 0, 1].rearrange("p t n -> p (t n)")[:, 0:NC * C].rearrange("p (c n) -> p c n", c=NC)
        nm = t.sb("nm", [P, 2, NT, HG])
        sn = t.sb("sn", [P, NT, 4, 2 * D1], F32R)
        ou = t.sb("ou", [P, T])
        inv = t.sb("inv", [P, NT, HG, 1])
        on = t.sb("on", [P, NT, C])
        ot_hi, ot_lo = (t.sb(n, [P, NC, T], F32R) for n in ("ot_hi", "ot_lo"))
        so = t.sb("so1", [P, 2, C])
        ps = t.ps("ps", [P, 2, 512])
        pst = t.ps("pst", [P, 2, 512])
        po = t.ps("po1", [P, 512])
        pn = t.ps("pn", [P, 512])
        w = t.ps("w1a", [P, 2, 512])
        wq_in = t.sem("a_wq_in")
        wo_in = t.sem("a_wo_in")
        bias_in = t.sem("a_bias_in")
        w_hi_done = t.sem("a_w_hi_done")
        w_lo_done = t.sem("a_w_lo_done")
        bias_done = t.sem("a_bias_done")
        sn_hi_done = t.sem("a_sn_hi_done")
        xs_in = t.sem("a_xs_in")
        xg_in = t.sem("a_xg_in")
        x_stored = t.sem("a_x_stored")
        x_done = t.sem("a_x_done")
        zs_set = t.sem("a_zs_set")
        own_set = t.sem("a_own_set")
        sel_set = t.sem("a_sel_set")
        sel_copied = t.sem("a_sel_copied")
        vs_set = t.sem("a_vs_set")
        proj_done = t.sem("a_proj_done")
        qn_done = t.sem("a_qn_done")
        z_hi_done = t.sem("a_z_hi_done")
        z_lo_done = t.sem("a_z_lo_done")
        z_turned = t.sem("a_z_turned")
        stack_done = t.sem("a_stack_done")
        s_done = t.sem("a_s_done")
        max_done = t.sem("a_max_done")
        sn_done = t.sem("a_sn_done")
        n_turned = t.sem("a_n_turned")
        n_done = t.sem("a_n_done")
        st_done = t.sem("a_st_done")
        exp_done = t.sem("a_exp_done")
        vs_done = t.sem("a_vs_done")
        av_done = t.sem("a_av_done")
        ou_done = t.sem("a_ou_done")
        o_turned = t.sem("a_o_turned")
        inv_done = t.sem("a_inv_done")
        on_done = t.sem("a_on_done")
        on_turned = t.sem("a_on_turned")
        ot_hi_done = t.sem("a_ot_hi_done")
        ot_lo_done = t.sem("a_ot_lo_done")
        out_done = t.sem("a_out_done")
        so_done = t.sem("a_so_done")
        mul_done = t.sem("a_mul_done")

        TURNS = ((0, 0), (0, 1), (0, 3), (1, 1))
        STACKS = ((0, 0), (0, 1), (0, 3), (1, 0), (1, 1), (1, 2))
        PROJECTIONS = ((1, 3), (2, 0), (2, 2), (2, 3))

        with nc.Block() as block:
            @block.sync
            def _(sp):
                def load_xs(b):
                    sp.dma_start(xs_hi[:].bitcast(F32), io.xt1_hi[:, :, bass.ds(b * T, T)]).then_inc(xs_in, 16)
                    sp.dma_start(xs_lo[:].bitcast(F32), io.xt1_lo[:, :, bass.ds(b * T, T)]).then_inc(xs_in, 16)

                def load_xg(b):
                    for dst, src in ((x1, io.x1), (g1, io.gate1)):
                        sp.dma_start(dst[:], src[bass.ds(b, 1)].rearrange("o (t p) c -> p (o t) c", p=P)).then_inc(xg_in, 16)

                def store(b):
                    sp.wait_ge(x_done, NT * b + NT + 2)
                    sp.dma_start(io.out[bass.ds(b, 1)].rearrange("o (t p) c -> p (o t) c", p=P), x1[:]).then_inc(x_stored, 16)
                    sp.wait_ge(x_stored, 16 * b + 16)

                load_xs(0)
                sp.dma_start(bqkv[:], io.bqkv1.partition_broadcast(P)).then_inc(bias_in, 16)
                sp.dma_start(bo[:], io.bo1.partition_broadcast(P)).then_inc(bias_in, 16)
                load_xg(0)
                sp.wait_ge(proj_done, 2 * NT)
                load_xs(1)
                with sp.Fori(0, B - 2) as b:
                    sp.wait_ge(proj_done, 2 * NT * b + 4 * NT)
                    load_xs(b + 2)
                    store(b)
                    load_xg(b + 1)
                store(B - 2)
                load_xg(B - 1)
                store(B - 1)

            @block.gpsimd
            def _(pool):
                pool.memset(sel[2 * S3:P], 0.0).then_inc(sel_set, 1)
                pool.wait_ge(sel_set, 1)
                for row in (0, 2):
                    for e in range(2):
                        pool.affine_select(out=sel[2 * S3:P, e, :], in_=sel[2 * S3:P, e, :], compare_op=ALU.not_equal, fill=1.0,
                                           base=-(row + e), pattern=[[0, T]], channel_multiplier=1).then_inc(sel_set, 1)
                    pool.wait_ge(sel_set, 3 + row)
                pool.memset(own[:], 1.0).then_inc(own_set, 1)
                pool.wait_ge(own_set, 1)
                for e, (base, sign) in enumerate(((S3 - 1, -1), (-S3, 1))):
                    pool.affine_select(out=own[:, e:e + 1], in_=own[:, e:e + 1], compare_op=ALU.is_ge, fill=0.0,
                                       base=base, pattern=[[0, 1]], channel_multiplier=sign).then_inc(own_set, 1)
                pool.memset(sn[:].bitcast(F32), 0.0).then_inc(zs_set, 1)
                pool.memset(vs[:], 0.0).then_inc(vs_set, 1)
                pool.wait_ge(vs_set, 1)
                pool.memset(vs[:, :, :, D1:D1 + 1], 1.0).then_inc(vs_set, 1)

                def split_z(b, g):
                    q = NG1 * b + g
                    src = qn[:, :, g * HG * D1:(g + 1) * HG * D1]
                    pool.wait_ge(z_hi_done, 4 * q + 2)
                    pool.tensor_tensor(zq[:, :, :, 1, :], src.rearrange("p t (h d) -> p t h d", d=D1),
                                       zq[:, :, :, 0, :].bitcast(F32), ALU.subtract).then_inc(z_lo_done, 1)
                    pool.wait_ge(z_hi_done, 4 * q + 4)
                    ks = qn[:, :, C + g * HG * D1:C + (g + 1) * HG * D1]
                    pool.tensor_tensor(zk[:, :, :, 2, :], ks.rearrange("p t (h d) -> p t h d", d=D1),
                                       zk[:, :, :, 0, :].bitcast(F32), ALU.subtract).then_inc(z_lo_done, 1)

                def finish(b):
                    for i in range(NT):
                        pool.wait_ge(so_done, NT * b + i + 1)
                        if i == 0:
                            pool.wait_ge(xg_in, 32 * b + 32)
                        pool.tensor_tensor(so[:, i % 2, :], so[:, i % 2, :], g1[:, i, :], ALU.mult).then_inc(mul_done, 1)
                        pool.wait_ge(mul_done, NT * b + i + 1)
                        pool.tensor_tensor(x1[:, i, :], x1[:, i, :], so[:, i % 2, :], ALU.add).then_inc(x_done, 1)

                def row(b, first=False, last=False):
                    for g in range(NG1):
                        if not (last and g > 0):
                            split_z(b + (g + 3) // NG1, (g + 3) % NG1)
                        if g == 2 and not first:
                            finish(b - 1)

                pool.sem_inc(x_done, 2)
                for g in range(3):
                    split_z(0, g)
                row(0, first=True)
                with pool.Fori(1, B - 1) as b:
                    row(b)
                row(B - 1, last=True)
                finish(B - 1)

            @block.tensor
            def _(pe):
                def project(b, i):
                    for j, (at, width) in enumerate(((0, 2 * C), (2 * C, C))):
                        if isinstance(b, int) and b == 0:
                            if i > 0:
                                pe.wait_ge(qn_done, 2 * i - 1 + j)
                        elif i > 0:
                            pe.wait_ge(qn_done, 2 * NT * b + 2 * i - 1 + j)
                        else:
                            pe.wait_ge(stack_done, 6 * (NG1 * b - 1) + 4 + 2 * j)
                        for k in range(NC):
                            xh, xl = (a[:, k, i * P:(i + 1) * P] for a in (xs_hi, xs_lo))
                            cols = slice(at, at + width)
                            pe.matmul(w[:, j, 0:width], xh, wq_hi[:, k, cols], start=(k == 0), stop=False)
                            pe.matmul(w[:, j, 0:width], xh, wq_lo[:, k, cols], start=False, stop=False)
                            mm = pe.matmul(w[:, j, 0:width], xl, wq_hi[:, k, cols], start=False, stop=(k == NC - 1))
                        mm.then_inc(proj_done, 1)

                def turn_z(q, j, bank_read):
                    if j == 0:
                        pe.wait_ge(z_hi_done, 4 * q + 4)
                        pe.wait_ge(z_lo_done, 2 * q + 2)
                    pe.wait_ge(bank_read[0], bank_read[1])
                    for i in range(NT):
                        src = (zq, zk)[j // 2][:, i, j % 2 * 2:j % 2 * 2 + 2].rearrange("p h s d -> p (h s d)")
                        mm = pe.transpose(w[0:2 * S3, j % 2, i * P:(i + 1) * P], src.bitcast(F32), c.ident[:])
                    mm.then_inc(z_turned, 1)

                def score(q, g, h, i):
                    if h < 2 and i == 0:
                        pe.wait_ge(stack_done, 6 * q + (3 if h == 0 else 6))
                    n = 16 * q + 4 * h + i
                    pe.wait_ge(max_done, n)
                    pe.matmul(ps[:, i % 2, :], qb[0:2 * S3, g, h // 2, i * P:(i + 1) * P], kb[0:2 * S3, g, h, :],
                              start=True, stop=True).then_inc(s_done, 1)

                def score_t(q, g, h, i):
                    if h == 0 and i == 0:
                        pe.wait_ge(n_done, 2 * q + 2)
                    n = 16 * q + 4 * h + i
                    pe.wait_ge(exp_done, n)
                    pe.matmul(pst[:, i % 2, :], kb[:, g, h, i * P:(i + 1) * P], qb[:, g, h // 2, :],
                              start=True, stop=True).then_inc(st_done, 1)

                def weigh(q, g, kt, rows_done):
                    if kt == 0:
                        pe.wait_ge(exp_done, 16 * q + 17)
                        pe.wait_ge(ou_done, q)
                        pe.wait_ge(vs_done, rows_done)
                    for h in range(HG):
                        mm = pe.matmul(po[2 * D1 * h:2 * D1 * (h + 1), :], vs[:, kt, g * HG + h, :], pt[:, g % 2, h, kt, :],
                                       start=(kt == 0), stop=(kt == NT - 1))
                    if kt == NT - 1:
                        mm.then_inc(av_done, 1)

                def turn_n(q):
                    pe.wait_ge(sn_done, q + 1)
                    if not isinstance(q, int) or q > 3:
                        pe.wait_ge(on_done, q - 2)
                    for i in range(NT):
                        mm = pe.transpose(pn[:, i * P:(i + 1) * P], sn[:, i].rearrange("p a b -> p (a b)").bitcast(F32), c.ident[:])
                    mm.then_inc(n_turned, 1)

                def turn_o(q, n_turns):
                    pe.wait_ge(ou_done, q + 1)
                    pe.wait_ge(n_done, 2 * n_turns)
                    for i in range(NT):
                        mm = pe.transpose(pn[:, i * P:(i + 1) * P], ou[:, i * P:(i + 1) * P], c.ident[:])
                    mm.then_inc(o_turned, 1)

                def turn_on(b, k):
                    if k == 0:
                        pe.wait_ge(on_done, NG1 * b + NG1)
                    for i in range(NT):
                        mm = pe.transpose(w[:, k, i * P:(i + 1) * P], on[:, i, k * P:(k + 1) * P], c.ident[:])
                    mm.then_inc(on_turned, 1)

                def out_project(b, i):
                    if i < 2:
                        pe.wait_ge(ot_lo_done, NC * b + NC)
                    else:
                        pe.wait_ge(so_done, NT * b + i - 1)
                    for k in range(NC):
                        oh, ol = (a[:, k, i * P:(i + 1) * P] for a in (ot_hi, ot_lo))
                        pe.matmul(w[:, i % 2, 0:C], oh, wo_hi[:, k, :], start=(k == 0), stop=False)
                        pe.matmul(w[:, i % 2, 0:C], oh, wo_lo[:, k, :], start=False, stop=False)
                        mm = pe.matmul(w[:, i % 2, 0:C], ol, wo_hi[:, k, :], start=False, stop=(k == NC - 1))
                    mm.then_inc(out_done, 1)

                def group(b, g, first=False, last=False):
                    q = NG1 * b + g
                    more1, more2 = (not (last and g + n >= NG1) for n in (1, 2))
                    back1, back2 = (not (first and g < n) for n in (1, 2))
                    projects = g == 1 and not last
                    for h in range(HG):
                        for i in range(NT):
                            if h < HG - 1 and more1:
                                score(q + 1, (g + 1) % NG1, h + 1, i)
                            elif h == HG - 1 and more2:
                                score(q + 2, (g + 2) % NG1, 0, i)
                            score_t(q, g, h, i)
                            if (h, i) in TURNS and more2:
                                j = TURNS.index((h, i))
                                if j < 2 and g == 2 and not first:
                                    bank_read = (ot_lo_done, NC * b)
                                elif j < 2 and g == 3 and not first:
                                    bank_read = (so_done, NT * b)
                                else:
                                    bank_read = (stack_done, 6 * (q + 2) + (-2, 0, 1, 2)[j])
                                turn_z(q + 2, j, bank_read)
                            if (h, i) in PROJECTIONS and projects:
                                if (h, i) == PROJECTIONS[0]:
                                    pe.wait_ge(xs_in, 32 * b + 64)
                                    pe.wait_ge(z_lo_done, 2 * q + 6)
                                project(b + 1, PROJECTIONS.index((h, i)))
                            if h == 1 and i == 2 and back2:
                                turn_o(q - 2, q + 1)
                            if h == HG - 1:
                                if i == 1 and more1:
                                    turn_n(q + 1)
                                if g == 1 and not first and i >= 2:
                                    if last:
                                        pe.wait_ge(stack_done, 6 * (q + 2) + 3 + i)
                                    else:
                                        pe.wait_ge(qn_done, 2 * NT * (b + 1) + 5 + i)
                                    turn_on(b - 1, i - 2)
                                if g == 2 and not first:
                                    if i < 2 and not last:
                                        pe.wait_ge(stack_done, 6 * (q + 2) + 5 + i)
                                    out_project(b - 1, i)
                        if back1:
                            weigh(q - 1, (g + 3) % NG1, h, b + 1 if g else b)

                pe.wait_ge(w_hi_done, 2)
                pe.wait_ge(w_lo_done, 2)
                pe.wait_ge(xs_in, 32)
                for i in range(NT):
                    project(0, i)
                for j in range(4):
                    turn_z(0, j, (qn_done, 2 * NT) if j < 2 else (stack_done, j - 1))
                for n in range(HG + 1):
                    for i in range(NT):
                        score(n // HG, n // HG, n % HG, i)
                        if n < 2 and i % 2:
                            j = 2 * n + i // 2
                            turn_z(1, j, (stack_done, 6 + (-2, 0, 1, 2)[j]))
                pe.wait_ge(sel_copied, NG1)
                turn_n(0)
                for g in range(NG1):
                    group(0, g, first=True)
                with pe.Fori(1, B - 1) as b:
                    for g in range(NG1):
                        group(b, g)
                for g in range(NG1):
                    group(B - 1, g, last=True)
                q = NG1 * B - 1
                for kt in range(NT):
                    weigh(q, NG1 - 1, kt, B)
                for g in (q - 1, q):
                    pe.wait_ge(on_done, g)
                    turn_o(g, q + 1)
                for k in range(NC):
                    turn_on(B - 1, k)
                for i in range(NT):
                    out_project(B - 1, i)

            @block.vector
            def _(dve):
                def maximum(q, g, h, i):
                    if h == 0 and i == 0 and not (isinstance(q, int) and q < 2):
                        dve.wait_ge(sn_done, q - 1)
                    dve.wait_ge(s_done, 16 * q + 4 * h + i + 1)
                    dve.tensor_reduce(nm[:, g % 2, i, h:h + 1], ps[:, i % 2, :], AXX, ALU.max, negate=True).then_inc(max_done, 1)

                def split_n(q, g):
                    dve.wait_ge(max_done, 16 * q + 17)
                    dve.wait_ge(n_turned, q)
                    v = nm[:, g % 2].rearrange("p t (a b) -> p t a b", a=2)
                    dve.tensor_copy(sn[:, :, 0:2, 0:2], v).then_inc(sn_hi_done, 1)
                    dve.wait_ge(sn_hi_done, q + 1)
                    dve.tensor_tensor(sn[:, :, 0:2, 2:4], v, sn[:, :, 0:2, 0:2].bitcast(F32), ALU.subtract).then_inc(sn_done, 1)

                def take_n(q, g):
                    dve.wait_ge(n_turned, q + 1)
                    for a in range(2):
                        dve.tensor_copy(qb[2 * S3:P, g, a, :], pn[2 * D1 * a:2 * D1 * (a + 1), :]).then_inc(n_done, 1)

                def take_o(q, g):
                    dve.wait_ge(o_turned, q + 1)
                    v = pn[:].rearrange("p (t h d) -> p t h d", t=NT, h=HG)
                    dve.reciprocal(inv[:], v[:, :, :, D1:D1 + 1]).then_inc(inv_done, 1)
                    dve.wait_ge(inv_done, q + 1)
                    dve.tensor_tensor(on[:, :, g * HG * D1:(g + 1) * HG * D1].rearrange("p t (h d) -> p t h d", h=HG),
                                      v[:, :, :, 0:D1], inv[:].to_broadcast([P, NT, HG, D1]), ALU.mult).then_inc(on_done, 1)

                def take_proj(b, i):
                    for j, (at, width) in enumerate(((0, 2 * C), (2 * C, C))):
                        dve.wait_ge(proj_done, 2 * NT * b + 2 * i + j + 1)
                        dve.tensor_tensor(qn[:, i, at:at + width], w[:, j, 0:width], bqkv[:, at:at + width],
                                          ALU.add).then_inc(qn_done, 1)

                def split_ot(b):
                    for k in range(NC):
                        dve.wait_ge(ot_hi_done, NC * b + k + 1)
                        dve.tensor_tensor(ot_lo[:, k, :], w[:, k, :], ot_hi[:, k, :].bitcast(F32), ALU.subtract).then_inc(ot_lo_done, 1)

                def take_out(b, i):
                    dve.wait_ge(out_done, NT * b + i + 1)
                    dve.wait_ge(x_done, NT * b + i + 1)
                    dve.tensor_tensor(so[:, i % 2, :], w[:, i % 2, 0:C], bo[:], ALU.add).then_inc(so_done, 1)

                def group(b, g, first=False, last=False):
                    q = NG1 * b + g
                    more1, more2 = (not (last and g + n >= NG1) for n in (1, 2))
                    back2 = not (first and g < 2)
                    projects = g == 1 and not last
                    for h in range(HG):
                        if h == HG - 1 and more1:
                            split_n(q + 1, g + 1)
                        for i in range(NT):
                            if h < HG - 1 and more1:
                                maximum(q + 1, g + 1, h + 1, i)
                            elif h == HG - 1 and more2:
                                maximum(q + 2, g, 0, i)
                            if (h, i) in PROJECTIONS and projects:
                                if (h, i) == PROJECTIONS[0]:
                                    dve.wait_ge(vs_done, b + 1)
                                    dve.wait_ge(z_lo_done, 2 * q + 6)
                                take_proj(b + 1, PROJECTIONS.index((h, i)))
                            if h == 1 and i == 3 and back2:
                                take_o(q - 2, (g + 2) % NG1)
                            if h == HG - 1:
                                if i == 1 and more1:
                                    take_n(q + 1, (g + 1) % NG1)
                                if g == 1 and not first and i == 3:
                                    split_ot(b - 1)
                                if g == 2 and not first:
                                    take_out(b - 1, i)

                dve.memset(inv[:], 0.0).then_inc(max_done, 1)
                dve.wait_ge(sel_set, 5)
                for g in range(NG1):
                    dve.tensor_copy(kb[2 * S3:P, g].rearrange("p (a e) t -> p a e t", e=2),
                                    sel[2 * S3:P].unsqueeze(1).to_broadcast([P - 2 * S3, 2, 2, T])).then_inc(sel_copied, 1)
                dve.wait_ge(bias_in, 32)
                dve.tensor_scalar(bqkv[:, 0:C], bqkv[:, 0:C], 0.25, None, ALU.mult).then_inc(bias_done, 1)
                dve.wait_ge(w_hi_done, 1)
                dve.scalar_tensor_tensor(out=wq_lo[:, :, 0:C], in0=wq_raw[:, :, 0:C], scalar=0.25,
                                         in1=wq_hi[:, :, 0:C].bitcast(F32), op0=ALU.mult, op1=ALU.subtract).then_inc(w_lo_done, 1)
                dve.wait_ge(w_hi_done, 2)
                dve.tensor_tensor(wq_lo[:, :, C:], wq_raw[:, :, C:], wq_hi[:, :, C:].bitcast(F32), ALU.subtract).then_inc(w_lo_done, 1)
                dve.wait_ge(w_hi_done, 3)
                dve.tensor_tensor(wo_lo[:], wo_raw, wo_hi[:].bitcast(F32), ALU.subtract).then_inc(w_lo_done, 1)
                dve.wait_ge(bias_done, 1)
                for i in range(NT):
                    take_proj(0, i)
                dve.wait_ge(zs_set, 1)
                for h in range(HG):
                    for i in range(NT):
                        maximum(0, 0, h, i)
                split_n(0, 0)
                for i in range(NT):
                    maximum(1, 1, 0, i)
                take_n(0, 0)
                for g in range(NG1):
                    group(0, g, first=True)
                with dve.Fori(1, B - 1) as b:
                    for g in range(NG1):
                        group(b, g)
                for g in range(NG1):
                    group(B - 1, g, last=True)
                for q in (NG1 * B - 2, NG1 * B - 1):
                    take_o(q, q % NG1)
                split_ot(B - 1)
                for i in range(NT):
                    take_out(B - 1, i)

            @block.scalar
            def _(act):
                def exps(q, g, h, i):
                    act.wait_ge(st_done, 16 * q + 4 * h + i + 1)
                    act.activation(pt[:, g % 2, h, i, :], pst[:, i % 2, :], ACT.Exp).then_inc(exp_done, 1)

                def split_z(b, g):
                    q = NG1 * b + g
                    if g == 0:
                        act.wait_ge(qn_done, 2 * NT * b + 2 * NT)
                    act.wait_ge(z_turned, 4 * q)
                    qs = qn[:, :, g * HG * D1:(g + 1) * HG * D1].rearrange("p t (h d) -> p t h d", d=D1)
                    for j in (0, 2):
                        act.copy(zq[:, :, :, j, :], qs).then_inc(z_hi_done, 1)
                    ks = qn[:, :, C + g * HG * D1:C + (g + 1) * HG * D1].rearrange("p t (h d) -> p t h d", d=D1)
                    for j in (0, 1):
                        act.copy(zk[:, :, :, j, :], ks).then_inc(z_hi_done, 1)

                def take_stack(q, g, j):
                    rows = slice(0, 2 * S3)
                    if j < 2:
                        act.wait_ge(z_turned, 4 * q + j + 1)
                        act.copy(qb[rows, g, j, :], w[rows, j, :]).then_inc(stack_done, 1)
                    else:
                        h = j - 2
                        act.wait_ge(z_turned, 4 * q + 3 + h // 2)
                        act.mul(kb[rows, g, h, :], w[rows, h // 2, :], own[rows, h % 2:h % 2 + 1]).then_inc(stack_done, 1)

                def take_o(q):
                    act.wait_ge(av_done, q + 1)
                    act.wait_ge(o_turned, q)
                    act.copy(ou[:], po[:]).then_inc(ou_done, 1)

                def pass_v(b):
                    act.wait_ge(qn_done, 2 * NT * b + 2 * NT)
                    act.wait_ge(av_done, NG1 * b)
                    act.copy(vs[:, :, :, 0:D1], qn[:, :, 2 * C:].rearrange("p t (h d) -> p t h d", d=D1)).then_inc(vs_done, 1)

                def turn_on(b, k):
                    act.wait_ge(on_turned, NC * b + k + 1)
                    act.copy(ot_hi[:, k, :], w[:, k, :]).then_inc(ot_hi_done, 1)

                def group(b, g, first=False, last=False):
                    q = NG1 * b + g
                    more2, more3 = (not (last and g + n >= NG1) for n in (2, 3))
                    back2 = not (first and g < 2)
                    for h in range(HG):
                        if h == 0 and g == 1 and not first:
                            pass_v(b)
                        if h == HG - 1 and more3:
                            split_z(b + (g + 3) // NG1, (g + 3) % NG1)
                        for i in range(NT):
                            exps(q, g, h, i)
                            if h == 0 and i == 0 and back2:
                                take_o(q - 2)
                            if (h, i) in STACKS and more2:
                                take_stack(q + 2, (g + 2) % NG1, STACKS.index((h, i)))
                            if h == HG - 1 and g == 1 and not first and i >= 2:
                                turn_on(b - 1, i - 2)

                act.dma_start(wq_raw, io.wqkv1.rearrange("(c p) n -> p c n", p=P)).then_inc(wq_in, 16)
                act.dma_start(wo_raw, io.wo1.rearrange("(c p) n -> p c n", p=P)).then_inc(wo_in, 16)
                act.wait_ge(wq_in, 16)
                act.mul(wq_hi[:, :, 0:C], wq_raw[:, :, 0:C], 0.25).then_inc(w_hi_done, 1)
                act.copy(wq_hi[:, :, C:], wq_raw[:, :, C:]).then_inc(w_hi_done, 1)
                act.wait_ge(wo_in, 16)
                act.copy(wo_hi[:], wo_raw).then_inc(w_hi_done, 1)
                act.wait_ge(w_lo_done, 3)
                act.wait_ge(own_set, 3)
                act.wait_ge(vs_set, 2)
                act.copy(ou[:, 0:1], c.ident[:, 0:1]).then_inc(exp_done, 1)
                for g in range(2):
                    split_z(0, g)
                    for j in range(6):
                        take_stack(g, g, j)
                split_z(0, 2)
                pass_v(0)
                for g in range(NG1):
                    group(0, g, first=True)
                with act.Fori(1, B - 1) as b:
                    for g in range(NG1):
                        group(b, g)
                for g in range(NG1):
                    group(B - 1, g, last=True)
                for q in (NG1 * B - 2, NG1 * B - 1):
                    take_o(q)
                for k in range(NC):
                    turn_on(B - 1, k)


def program(nc, io):
    with ExitStack() as ctx:
        m, c = Mem(nc, ctx), Names()
        c.stats1 = m.sb("stats1", [P, B * NT, 6])
        setup_constants(nc, m, c)
        with ExitStack() as inner:
            m0 = Mem(nc, inner)
            load_layer0(nc, m0, c, io)
            layer0(nc, m0, c, io)
        with ExitStack() as inner:
            m1 = Mem(nc, inner)
            c.xt1_hi, c.xt1_lo = (m1.sb(n, [P, NC, B * T], F32R) for n in ("xt1_hi", "xt1_lo"))
            experts(nc, c, io)
        attention1(nc, c, io)


def kernel(**inputs):
    import concourse.bacc as bacc
    from concourse.bass_utils import run_bass_kernel_spmd

    a = {k: np.asarray(v) for k, v in inputs.items()}
    wq, wk = (a[n].reshape(C, NP0, 2, D0 // 2, 2).transpose(0, 1, 2, 4, 3).reshape(C, NP0, 2 * D0)
              for n in ("L0_attn_Wq", "L0_attn_Wk"))
    wv = a["L0_attn_Wv"].reshape(C, NP0, 2 * D0)
    arrays = {
        "x": a["L0_attn_x"],
        "wqkv0": np.concatenate([wq, wk, wv], 2).reshape(C, NP0 * PC0),
        "wo0": a["L0_attn_Wo"],
        "bo0": a["L0_attn_bo"],
        "wg0": a["L0_ffn_w_gate"].T,
        "wu0": a["L0_ffn_w_up"].T,
        "wd0": a["L0_ffn_w_down"].T,
        "rope": rope_tables(),
        "wqkv1": np.concatenate([a["L1_attn_wq"].T, a["L1_attn_wk"].T, a["L1_attn_wv"].T], 1),
        "bqkv1": np.concatenate([a["L1_attn_bq"], a["L1_attn_bk_"], a["L1_attn_bv"]]),
        "wo1": a["L1_attn_wo"].T,
        "bo1": a["L1_attn_bo"],
        "w1": a["L1_ffn_w1"],
        "w3": a["L1_ffn_w3"],
        "w2": a["L1_ffn_w2"],
    }
    nc = bacc.Bacc("TRN2", target_bir_lowering=False, num_devices=1)
    io = Names()
    arrays = {"in_" + k: np.ascontiguousarray(v) for k, v in arrays.items()}
    aps = {k: nc.dram_tensor(k, v.shape, mybir.dt.from_np(v.dtype), kind="ExternalInput").ap() for k, v in arrays.items()}
    (io.x, io.wqkv0, io.wo0, io.bo0, io.wg0, io.wu0, io.wd0, io.rope, io.wqkv1, io.bqkv1, io.wo1, io.bo1,
     io.w1, io.w3, io.w2) = aps.values()
    io.x1 = nc.dram_tensor("x1_scratch", (B, T, C), F32, kind="Internal").ap()
    io.gate1 = nc.dram_tensor("gate1_scratch", (B, T, C), F32, kind="Internal").ap()
    io.xt1_hi = nc.dram_tensor("xt1_hi_scratch", (P, NC, B * T), F32, kind="Internal").ap()
    io.xt1_lo = nc.dram_tensor("xt1_lo_scratch", (P, NC, B * T), F32, kind="Internal").ap()
    io.out = nc.dram_tensor("out_dram", (B, T, C), F32, kind="ExternalOutput").ap()
    program(nc, io)
    r = run_bass_kernel_spmd(nc, [arrays], core_ids=[0])
    return r.results[0]["out_dram"]
```
